# Optimizing a Trainium2 kernel written in Bass

```python
import numpy as np
import jax
import jax.numpy as jnp

def _softmax(x, axis=-1):
    return jax.nn.softmax(x, axis=axis)

def _gelu(x):
    return jax.nn.gelu(x, approximate=True)

def _silu(x):
    return jax.nn.silu(x)

def _sigmoid(x):
    return jax.nn.sigmoid(x)

def _layernorm(x, axis=-1, eps=1e-05):
    m = jnp.mean(x, axis=axis, keepdims=True)
    v = jnp.var(x, axis=axis, keepdims=True)
    return (x - m) / jnp.sqrt(v + eps)

def _scatter_add(tgt, idx, src, axis=0):
    return tgt.at[idx].add(src)

def _segment_sum(src, seg, n):
    return jax.ops.segment_sum(src, seg, n)
kernel_name = 'mk_decoder_postln_d2_seqx_r4_6bc367'

def setup_inputs(seed: int=0):
    np.random.seed(seed)
    _w = jnp.asarray

    def _rec_inputs():
        import jax
        import jax.numpy as jnp
        _rk = jax.random.key(seed)
        x = -1.528e-05 + 0.9999 * jax.random.normal(jax.random.fold_in(_rk, 1), (4, 512, 256), jnp.float32)
        _lenS = 512 - jax.random.randint(jax.random.fold_in(_rk, 7), (4,), 0, max(1, 512 // 4) + 1, jnp.int32)
        _lenS2 = 1024 - jax.random.randint(jax.random.fold_in(_rk, 8), (4,), 0, max(1, 1024 // 4) + 1, jnp.int32)
        _ctx_1024P = jax.random.normal(jax.random.fold_in(_rk, 11), (4, 16, 256), jnp.float32)
        _ctx_1024c = jax.random.dirichlet(jax.random.fold_in(_rk, 511), 0.3 * jnp.ones((16,), jnp.float32), (4, 1024))
        _ctx_1024t = jnp.einsum('bsk,bkd->bsd', _ctx_1024c, _ctx_1024P)
        _ctx_1024t = _ctx_1024t * jax.lax.rsqrt(jnp.mean(jnp.square(_ctx_1024t)) + 1e-12) * 0.953939
        ctx_1024 = 0.000121155 + 1.00018 * (_ctx_1024t + 0.3 * jax.random.normal(jax.random.fold_in(_rk, 611), (4, 1024, 256), jnp.float32))
        return (x, ctx_1024)
    x, ctx_1024 = _rec_inputs()

    def _L0_attn_setup():
        import jax, jax.numpy as jnp
        import numpy as np
        DIM = 256
        HEADS = 16
        DIM_HEAD = 64
        SOFTCLAMP = 50.0

        def _rmsnorm(x, w):
            eps = jnp.finfo(x.dtype).eps
            var = jnp.mean(jnp.square(x), axis=-1, keepdims=True)
            return x * jax.lax.rsqrt(var + eps) * w

        def _head_rmsnorm(x, gamma):
            norm = jnp.linalg.norm(x, axis=-1, keepdims=True)
            normed = x / jnp.maximum(norm, 1e-12)
            scale = (gamma + 1.0) * DIM_HEAD ** 0.5
            return normed * scale[None, :, None, :]
        key = jax.random.key(seed)
        ks = jax.random.split(key, 7)
        b, n = (4, 512)
        di = HEADS * DIM_HEAD
        s = 0.02
        return {'tokens': jax.random.normal(ks[0], (b, n, DIM), dtype=jnp.float32), 'norm_w': jnp.ones((DIM,), dtype=jnp.float32), 'Wq': jax.random.normal(ks[1], (DIM, di), dtype=jnp.float32) * s, 'Wkv': jax.random.normal(ks[2], (DIM, 2 * di), dtype=jnp.float32) * s, 'Wo': jax.random.normal(ks[3], (di, DIM), dtype=jnp.float32) * s, 'q_gamma': jnp.zeros((HEADS, DIM_HEAD), dtype=jnp.float32), 'k_gamma': jnp.zeros((HEADS, DIM_HEAD), dtype=jnp.float32)}
    _L0_attn_all = _L0_attn_setup()
    _L0_attn_in = {k: v for k, v in _L0_attn_all.items() if k in ('norm_w', 'Wq', 'Wkv', 'Wo', 'q_gamma', 'k_gamma')}
    del _L0_attn_all

    def _L0_xattn_setup():
        import jax, jax.numpy as jnp
        import numpy as np
        N_BATCH = 8
        SEQ_S = 1024
        SEQ_L = 1024
        D = 256
        key = jax.random.key(seed)
        ks = jax.random.split(key, 9)
        scale = 0.02
        return {'x1': jax.random.normal(ks[0], (SEQ_S, D), dtype=jnp.float32), 'x2': jax.random.normal(ks[1], (N_BATCH, SEQ_L, D), dtype=jnp.float32), 'x3': jax.random.normal(ks[2], (N_BATCH, SEQ_S, D), dtype=jnp.float32), 'W1': jax.random.normal(ks[3], (D, D), dtype=jnp.float32) * scale, 'b1': jax.random.normal(ks[4], (D,), dtype=jnp.float32) * scale, 'W2': jax.random.normal(ks[5], (D, D), dtype=jnp.float32) * scale, 'b2': jax.random.normal(ks[6], (D,), dtype=jnp.float32) * scale, 'W3': jax.random.normal(ks[7], (D, D), dtype=jnp.float32) * scale, 'b3': jax.random.normal(ks[8], (D,), dtype=jnp.float32) * scale}
    _L0_xattn_all = _L0_xattn_setup()
    _L0_xattn_in = {k: v for k, v in _L0_xattn_all.items() if k in ('x1', 'W1', 'b1', 'W2', 'b2', 'W3', 'b3')}
    del _L0_xattn_all

    def _L0_ffn_setup():
        import jax, jax.numpy as jnp
        import numpy as np
        D_MODEL = 256
        D_FF = 1024
        N_EXPERTS = 8
        TOP_K = 2
        LN_EPS = 1e-06

        def _moe(x, router_w, w1, b1, w2, b2, gamma, beta):
            B, S, D = x.shape
            x_flat = x.reshape(-1, D)
            N = x_flat.shape[0]
            logits = x_flat @ router_w
            gate_vals, gate_idx = jax.lax.top_k(logits, TOP_K)
            gate_w = jax.nn.softmax(gate_vals, axis=-1)
            gates = jnp.zeros_like(logits).at[jnp.arange(N)[:, None], gate_idx].set(gate_w)
            h = jax.nn.gelu(jnp.einsum('nd,edf->enf', x_flat, w1) + b1[:, None, :], approximate=False)
            out = jnp.einsum('enf,efd->end', h, w2) + b2[:, None, :]
            res = x_flat[None, :, :] + out
            mu = jnp.mean(res, axis=-1, keepdims=True)
            var = jnp.mean(jnp.square(res - mu), axis=-1, keepdims=True)
            normed = (res - mu) * jax.lax.rsqrt(var + LN_EPS)
            expert_out = normed * gamma[:, None, :] + beta[:, None, :]
            y = jnp.einsum('end,ne->nd', expert_out, gates)
            return y.reshape(B, S, D)
        key = jax.random.key(seed)
        ks = jax.random.split(key, 8)
        x = jax.random.normal(ks[0], (2, 512, D_MODEL), dtype=jnp.float32)
        router_w = jax.random.normal(ks[1], (D_MODEL, N_EXPERTS), dtype=jnp.float32) * 0.02
        w1 = jax.random.normal(ks[2], (N_EXPERTS, D_MODEL, D_FF), dtype=jnp.float32) * 0.02
        b1 = jnp.zeros((N_EXPERTS, D_FF), dtype=jnp.float32)
        w2 = jax.random.normal(ks[3], (N_EXPERTS, D_FF, D_MODEL), dtype=jnp.float32) * 0.02
        b2 = jnp.zeros((N_EXPERTS, D_MODEL), dtype=jnp.float32)
        gamma = jnp.ones((N_EXPERTS, D_MODEL), dtype=jnp.float32)
        beta = jnp.zeros((N_EXPERTS, D_MODEL), dtype=jnp.float32)
        return {'x': x, 'router_w': router_w, 'w1': w1, 'b1': b1, 'w2': w2, 'b2': b2, 'gamma': gamma, 'beta': beta}
    _L0_ffn_all = _L0_ffn_setup()
    _L0_ffn_in = {k: v for k, v in _L0_ffn_all.items() if k in ('router_w', 'w1', 'b1', 'w2', 'b2', 'gamma', 'beta')}
    del _L0_ffn_all

    def _L1_attn_setup():
        import jax, jax.numpy as jnp
        import numpy as np
        N_HEADS = 16
        SEG = 64
        D_MODEL = 256
        NOISE_EPS = 1e-05

        def _forward(hidden_states, Wq, Wk, Wv, Wc, terrace_mix, index_decays, mega_decays):
            b, L, d = hidden_states.shape
            H, seg = (N_HEADS, SEG)
            Dh = d // H
            r = L // seg
            q = (hidden_states @ Wq.T).reshape(b, L, H, Dh)
            k = (hidden_states @ Wk.T).reshape(b, L, H, Dh)
            v = (hidden_states @ Wv.T).reshape(b, L, H, Dh)
            scores = jnp.einsum('bnhd,bmhd->bhnm', q, k) / jnp.sqrt(jnp.float32(Dh))
            idx = jnp.arange(L)
            causal = idx[:, None] >= idx[None, :]
            dblk = (idx // seg)[:, None] - (idx // seg)[None, :]
            neg = jnp.float32(-jnp.inf)
            scores = jnp.where(causal, scores, neg)
            terrace_allowed = causal & ((dblk == 0) | (dblk == 1))
            scores_t = jnp.where(terrace_allowed, scores, neg)
            att_t = jax.nn.softmax(scores_t, axis=-1)
            out_t = jnp.einsum('bhnm,bmhd->bhnd', att_t, v).reshape(b, H, r, seg, Dh)
            att = jax.nn.softmax(scores, axis=-1)
            awc = att.reshape(b, H, r, seg, L) * jnp.exp(index_decays)[None, :, None, :, None]
            pcs = awc.sum(axis=-2)
            mega = jnp.clip(jnp.exp(mega_decays * seg), 0.0, 2.0)
            s_seq = jnp.moveaxis(pcs, 2, 0)

            def step(carry, s):
                return (carry * mega[None, :, None] + s, carry)
            _, outs = jax.lax.scan(step, jnp.zeros_like(s_seq[0]), s_seq)
            w = jnp.moveaxis(outs, 0, 2)
            w = w / (w.sum(axis=-1, keepdims=True) + NOISE_EPS)
            kv = jnp.einsum('bhrs,bshd,bshe->brhde', w, k, v)
            qc = q.reshape(b, r, seg, H, Dh)
            out_lin = jnp.einsum('brlhd,brhde->bhrle', qc, kv)
            tw = jax.nn.sigmoid(terrace_mix)[None, None, None, :, None]
            y = tw * out_t + (1.0 - tw) * out_lin
            y = y.reshape(b, H, L, Dh).transpose(0, 2, 1, 3).reshape(b, L, d)
            return y @ Wc.T
        key = jax.random.key(seed)
        ks = jax.random.split(key, 8)
        b, L, d = (1, 512, D_MODEL)
        sc = 0.02
        hidden_states = jax.random.normal(ks[0], (b, L, d), jnp.float32)
        Wq = sc * jax.random.normal(ks[1], (d, d), jnp.float32)
        Wk = sc * jax.random.normal(ks[2], (d, d), jnp.float32)
        Wv = sc * jax.random.normal(ks[3], (d, d), jnp.float32)
        Wc = sc * jax.random.normal(ks[4], (d, d), jnp.float32)
        terrace_mix = 0.5 * jnp.ones((SEG,), jnp.float32)
        index_decays = -0.1 * jnp.ones((N_HEADS, SEG), jnp.float32) + 0.01 * jax.random.normal(ks[5], (N_HEADS, SEG), jnp.float32)
        mega_decays = -0.1 * jnp.ones((N_HEADS,), jnp.float32) + 0.01 * jax.random.normal(ks[6], (N_HEADS,), jnp.float32)
        return dict(hidden_states=hidden_states, Wq=Wq, Wk=Wk, Wv=Wv, Wc=Wc, terrace_mix=terrace_mix, index_decays=index_decays, mega_decays=mega_decays)
    _L1_attn_all = _L1_attn_setup()
    _L1_attn_in = {k: v for k, v in _L1_attn_all.items() if k in ('Wq', 'Wk', 'Wv', 'Wc', 'terrace_mix', 'index_decays', 'mega_decays')}
    del _L1_attn_all

    def _L1_xattn_setup():
        import jax, jax.numpy as jnp
        import numpy as np
        DIM = 256
        NUM_HEADS = 16
        DIM_HEAD = 64
        INNER = NUM_HEADS * DIM_HEAD
        SCALE = DIM_HEAD ** (-0.5)

        def _layernorm(x, gamma, beta, eps=1e-05):
            mu = jnp.mean(x, axis=-1, keepdims=True)
            var = jnp.mean(jnp.square(x - mu), axis=-1, keepdims=True)
            return (x - mu) * jax.lax.rsqrt(var + eps) * gamma + beta
        key = jax.random.key(seed)
        ks = jax.random.split(key, 8)
        B, SQ, SK = (2, 512, 1024)
        x = jax.random.normal(ks[0], (B, SQ, DIM), dtype=jnp.float32)
        context = jax.random.normal(ks[1], (B, SK, DIM), dtype=jnp.float32)
        ln_gamma = jnp.ones((DIM,), jnp.float32)
        ln_beta = jnp.zeros((DIM,), jnp.float32)
        w_q = jax.random.normal(ks[2], (DIM, INNER), dtype=jnp.float32) / np.sqrt(DIM)
        w_kv = jax.random.normal(ks[3], (DIM, 2 * INNER), dtype=jnp.float32) / np.sqrt(DIM)
        w_out = jax.random.normal(ks[4], (INNER, DIM), dtype=jnp.float32) / np.sqrt(INNER)
        b_out = jnp.zeros((DIM,), jnp.float32)
        gate = jnp.array([0.5], jnp.float32)
        return {'x': x, 'context': context, 'ln_gamma': ln_gamma, 'ln_beta': ln_beta, 'w_q': w_q, 'w_kv': w_kv, 'w_out': w_out, 'b_out': b_out, 'gate': gate}
    _L1_xattn_all = _L1_xattn_setup()
    _L1_xattn_in = {k: v for k, v in _L1_xattn_all.items() if k in ('ln_gamma', 'ln_beta', 'w_q', 'w_kv', 'w_out', 'b_out', 'gate')}
    del _L1_xattn_all

    def _L1_ffn_setup():
        import jax, jax.numpy as jnp
        import numpy as np
        key = jax.random.key(seed)
        ks = jax.random.split(key, 6)
        B, L, D, E = (4, 512, 256, 4)
        H = 4 * D
        x = jax.random.normal(ks[0], (B, L, D), dtype=jnp.float32)
        rW1 = jax.random.normal(ks[1], (D, 2 * D), dtype=jnp.float32) * (2.0 / D) ** 0.5
        rb1 = jnp.zeros((2 * D,), dtype=jnp.float32)
        rW2 = jax.random.normal(ks[2], (2 * D, E), dtype=jnp.float32) * (2.0 / (2 * D)) ** 0.5
        rb2 = jnp.zeros((E,), dtype=jnp.float32)
        We1 = jax.random.normal(ks[3], (E, D, H), dtype=jnp.float32) * (2.0 / D) ** 0.5
        be1 = jnp.zeros((E, H), dtype=jnp.float32)
        We2 = jax.random.normal(ks[4], (E, H, D), dtype=jnp.float32) * (2.0 / H) ** 0.5
        be2 = jnp.zeros((E, D), dtype=jnp.float32)
        return {'x': x, 'rW1': rW1, 'rb1': rb1, 'rW2': rW2, 'rb2': rb2, 'We1': We1, 'be1': be1, 'We2': We2, 'be2': be2}
    _L1_ffn_all = _L1_ffn_setup()
    _L1_ffn_in = {k: v for k, v in _L1_ffn_all.items() if k in ('rW1', 'rb1', 'rW2', 'rb2', 'We1', 'be1', 'We2', 'be2')}
    del _L1_ffn_all
    return {'x': x, 'ctx_1024': ctx_1024, 'L0_attn_norm_w': _L0_attn_in['norm_w'], 'L0_attn_Wq': _L0_attn_in['Wq'], 'L0_attn_Wkv': _L0_attn_in['Wkv'], 'L0_attn_Wo': _L0_attn_in['Wo'], 'L0_attn_q_gamma': _L0_attn_in['q_gamma'], 'L0_attn_k_gamma': _L0_attn_in['k_gamma'], 'L0_xattn_x1': _L0_xattn_in['x1'], 'L0_xattn_W1': _L0_xattn_in['W1'], 'L0_xattn_b1': _L0_xattn_in['b1'], 'L0_xattn_W2': _L0_xattn_in['W2'], 'L0_xattn_b2': _L0_xattn_in['b2'], 'L0_xattn_W3': _L0_xattn_in['W3'], 'L0_xattn_b3': _L0_xattn_in['b3'], 'L0_ffn_router_w': _L0_ffn_in['router_w'], 'L0_ffn_w1': _L0_ffn_in['w1'], 'L0_ffn_b1': _L0_ffn_in['b1'], 'L0_ffn_w2': _L0_ffn_in['w2'], 'L0_ffn_b2': _L0_ffn_in['b2'], 'L0_ffn_gamma': _L0_ffn_in['gamma'], 'L0_ffn_beta': _L0_ffn_in['beta'], 'L1_attn_Wq': _L1_attn_in['Wq'], 'L1_attn_Wk': _L1_attn_in['Wk'], 'L1_attn_Wv': _L1_attn_in['Wv'], 'L1_attn_Wc': _L1_attn_in['Wc'], 'L1_attn_terrace_mix': _L1_attn_in['terrace_mix'], 'L1_attn_index_decays': _L1_attn_in['index_decays'], 'L1_attn_mega_decays': _L1_attn_in['mega_decays'], 'L1_xattn_ln_gamma': _L1_xattn_in['ln_gamma'], 'L1_xattn_ln_beta': _L1_xattn_in['ln_beta'], 'L1_xattn_w_q': _L1_xattn_in['w_q'], 'L1_xattn_w_kv': _L1_xattn_in['w_kv'], 'L1_xattn_w_out': _L1_xattn_in['w_out'], 'L1_xattn_b_out': _L1_xattn_in['b_out'], 'L1_xattn_gate': _L1_xattn_in['gate'], 'L1_ffn_rW1': _L1_ffn_in['rW1'], 'L1_ffn_rb1': _L1_ffn_in['rb1'], 'L1_ffn_rW2': _L1_ffn_in['rW2'], 'L1_ffn_rb2': _L1_ffn_in['rb2'], 'L1_ffn_We1': _L1_ffn_in['We1'], 'L1_ffn_be1': _L1_ffn_in['be1'], 'L1_ffn_We2': _L1_ffn_in['We2'], 'L1_ffn_be2': _L1_ffn_in['be2']}

def reference(x, ctx_1024, L0_attn_norm_w, L0_attn_Wq, L0_attn_Wkv, L0_attn_Wo, L0_attn_q_gamma, L0_attn_k_gamma, L0_xattn_x1, L0_xattn_W1, L0_xattn_b1, L0_xattn_W2, L0_xattn_b2, L0_xattn_W3, L0_xattn_b3, L0_ffn_router_w, L0_ffn_w1, L0_ffn_b1, L0_ffn_w2, L0_ffn_b2, L0_ffn_gamma, L0_ffn_beta, L1_attn_Wq, L1_attn_Wk, L1_attn_Wv, L1_attn_Wc, L1_attn_terrace_mix, L1_attn_index_decays, L1_attn_mega_decays, L1_xattn_ln_gamma, L1_xattn_ln_beta, L1_xattn_w_q, L1_xattn_w_kv, L1_xattn_w_out, L1_xattn_b_out, L1_xattn_gate, L1_ffn_rW1, L1_ffn_rb1, L1_ffn_rW2, L1_ffn_rb2, L1_ffn_We1, L1_ffn_be1, L1_ffn_We2, L1_ffn_be2):
    import jax
    import jax.numpy as jnp

    def _L0_attn_ref(tokens, norm_w, Wq, Wkv, Wo, q_gamma, k_gamma):
        import jax, jax.numpy as jnp
        import numpy as np
        DIM = 256
        HEADS = 16
        DIM_HEAD = 64
        SOFTCLAMP = 50.0

        def _rmsnorm(x, w):
            eps = jnp.finfo(x.dtype).eps
            var = jnp.mean(jnp.square(x), axis=-1, keepdims=True)
            return x * jax.lax.rsqrt(var + eps) * w

        def _head_rmsnorm(x, gamma):
            norm = jnp.linalg.norm(x, axis=-1, keepdims=True)
            normed = x / jnp.maximum(norm, 1e-12)
            scale = (gamma + 1.0) * DIM_HEAD ** 0.5
            return normed * scale[None, :, None, :]
        b, n, _ = tokens.shape
        x = _rmsnorm(tokens, norm_w)
        q = x @ Wq
        kv = x @ Wkv
        k, v = jnp.split(kv, 2, axis=-1)
        split = lambda t: t.reshape(b, n, HEADS, DIM_HEAD).transpose(0, 2, 1, 3)
        q, k, v = (split(q), split(k), split(v))
        q = _head_rmsnorm(q, q_gamma)
        k = _head_rmsnorm(k, k_gamma)
        sim = jnp.einsum('bhid,bhjd->bhij', q, k)
        sim = jnp.tanh(sim / SOFTCLAMP) * SOFTCLAMP
        sim = sim * DIM_HEAD ** (-0.5)
        attn = jax.nn.softmax(sim, axis=-1)
        out = jnp.einsum('bhij,bhjd->bhid', attn, v)
        out = out.transpose(0, 2, 1, 3).reshape(b, n, HEADS * DIM_HEAD)
        return out @ Wo

    def _L0_xattn_ref(x1, x2, x3, W1, b1, W2, b2, W3, b3):
        import jax, jax.numpy as jnp
        import numpy as np
        N_BATCH = 8
        SEQ_S = 1024
        SEQ_L = 1024
        D = 256
        v1 = x1 @ W1.T + b1
        scores = jnp.einsum('nld,sd->nls', x2, v1) * N_BATCH ** (-0.5)
        attn = jax.nn.softmax(scores, axis=-1)
        v5 = jnp.einsum('nls,nsd->nld', attn, x3)
        v6 = v5 @ W2.T + b2
        v7 = v6 @ W3.T + b3
        return v7

    def _L0_ffn_ref(x, router_w, w1, b1, w2, b2, gamma, beta):
        import jax, jax.numpy as jnp
        import numpy as np
        D_MODEL = 256
        D_FF = 1024
        N_EXPERTS = 8
        TOP_K = 2
        LN_EPS = 1e-06

        def _moe(x, router_w, w1, b1, w2, b2, gamma, beta):
            B, S, D = x.shape
            x_flat = x.reshape(-1, D)
            N = x_flat.shape[0]
            logits = x_flat @ router_w
            gate_vals, gate_idx = jax.lax.top_k(logits, TOP_K)
            gate_w = jax.nn.softmax(gate_vals, axis=-1)
            gates = jnp.zeros_like(logits).at[jnp.arange(N)[:, None], gate_idx].set(gate_w)
            h = jax.nn.gelu(jnp.einsum('nd,edf->enf', x_flat, w1) + b1[:, None, :], approximate=False)
            out = jnp.einsum('enf,efd->end', h, w2) + b2[:, None, :]
            res = x_flat[None, :, :] + out
            mu = jnp.mean(res, axis=-1, keepdims=True)
            var = jnp.mean(jnp.square(res - mu), axis=-1, keepdims=True)
            normed = (res - mu) * jax.lax.rsqrt(var + LN_EPS)
            expert_out = normed * gamma[:, None, :] + beta[:, None, :]
            y = jnp.einsum('end,ne->nd', expert_out, gates)
            return y.reshape(B, S, D)
        return _moe(x, router_w, w1, b1, w2, b2, gamma, beta)

    def _L1_attn_ref(hidden_states, Wq, Wk, Wv, Wc, terrace_mix, index_decays, mega_decays):
        import jax, jax.numpy as jnp
        import numpy as np
        N_HEADS = 16
        SEG = 64
        D_MODEL = 256
        NOISE_EPS = 1e-05

        def _forward(hidden_states, Wq, Wk, Wv, Wc, terrace_mix, index_decays, mega_decays):
            b, L, d = hidden_states.shape
            H, seg = (N_HEADS, SEG)
            Dh = d // H
            r = L // seg
            q = (hidden_states @ Wq.T).reshape(b, L, H, Dh)
            k = (hidden_states @ Wk.T).reshape(b, L, H, Dh)
            v = (hidden_states @ Wv.T).reshape(b, L, H, Dh)
            scores = jnp.einsum('bnhd,bmhd->bhnm', q, k) / jnp.sqrt(jnp.float32(Dh))
            idx = jnp.arange(L)
            causal = idx[:, None] >= idx[None, :]
            dblk = (idx // seg)[:, None] - (idx // seg)[None, :]
            neg = jnp.float32(-jnp.inf)
            scores = jnp.where(causal, scores, neg)
            terrace_allowed = causal & ((dblk == 0) | (dblk == 1))
            scores_t = jnp.where(terrace_allowed, scores, neg)
            att_t = jax.nn.softmax(scores_t, axis=-1)
            out_t = jnp.einsum('bhnm,bmhd->bhnd', att_t, v).reshape(b, H, r, seg, Dh)
            att = jax.nn.softmax(scores, axis=-1)
            awc = att.reshape(b, H, r, seg, L) * jnp.exp(index_decays)[None, :, None, :, None]
            pcs = awc.sum(axis=-2)
            mega = jnp.clip(jnp.exp(mega_decays * seg), 0.0, 2.0)
            s_seq = jnp.moveaxis(pcs, 2, 0)

            def step(carry, s):
                return (carry * mega[None, :, None] + s, carry)
            _, outs = jax.lax.scan(step, jnp.zeros_like(s_seq[0]), s_seq)
            w = jnp.moveaxis(outs, 0, 2)
            w = w / (w.sum(axis=-1, keepdims=True) + NOISE_EPS)
            kv = jnp.einsum('bhrs,bshd,bshe->brhde', w, k, v)
            qc = q.reshape(b, r, seg, H, Dh)
            out_lin = jnp.einsum('brlhd,brhde->bhrle', qc, kv)
            tw = jax.nn.sigmoid(terrace_mix)[None, None, None, :, None]
            y = tw * out_t + (1.0 - tw) * out_lin
            y = y.reshape(b, H, L, Dh).transpose(0, 2, 1, 3).reshape(b, L, d)
            return y @ Wc.T
        return _forward(hidden_states, Wq, Wk, Wv, Wc, terrace_mix, index_decays, mega_decays)

    def _L1_xattn_ref(x, context, ln_gamma, ln_beta, w_q, w_kv, w_out, b_out, gate):
        import jax, jax.numpy as jnp
        import numpy as np
        DIM = 256
        NUM_HEADS = 16
        DIM_HEAD = 64
        INNER = NUM_HEADS * DIM_HEAD
        SCALE = DIM_HEAD ** (-0.5)

        def _layernorm(x, gamma, beta, eps=1e-05):
            mu = jnp.mean(x, axis=-1, keepdims=True)
            var = jnp.mean(jnp.square(x - mu), axis=-1, keepdims=True)
            return (x - mu) * jax.lax.rsqrt(var + eps) * gamma + beta
        B, SQ, _ = x.shape
        SK = context.shape[1]
        xn = _layernorm(x, ln_gamma, ln_beta)
        q = (xn @ w_q).reshape(B, SQ, NUM_HEADS, DIM_HEAD)
        kv = context @ w_kv
        k, v = jnp.split(kv, 2, axis=-1)
        k = k.reshape(B, SK, NUM_HEADS, DIM_HEAD)
        v = v.reshape(B, SK, NUM_HEADS, DIM_HEAD)
        scores = jnp.einsum('bqhd,bkhd->bhqk', q * SCALE, k)
        attn = jax.nn.softmax(scores, axis=-1)
        out = jnp.einsum('bhqk,bkhd->bqhd', attn, v).reshape(B, SQ, INNER)
        out = out @ w_out + b_out
        return out * jnp.tanh(gate[0])

    def _L1_ffn_ref(x, rW1, rb1, rW2, rb2, We1, be1, We2, be2):
        import jax, jax.numpy as jnp
        import numpy as np
        E = We1.shape[0]
        top_k = min(2, E)
        rh = jax.nn.gelu(x @ rW1 + rb1, approximate=False)
        router_logits = rh @ rW2 + rb2
        router_probs = jax.nn.softmax(router_logits, axis=-1)
        expert_weights, expert_indices = jax.lax.top_k(router_probs, top_k)
        one_hot = jax.nn.one_hot(expert_indices, E, dtype=x.dtype)
        token_mask = one_hot.sum(axis=2)
        combine_w = (one_hot * expert_weights[..., None]).sum(axis=2)
        out = jnp.zeros_like(x)
        for e in range(E):
            xi = x * token_mask[..., e:e + 1]
            h = jax.nn.gelu(xi @ We1[e] + be1[e], approximate=False)
            yo = h @ We2[e] + be2[e]
            out = out + yo * combine_w[..., e:e + 1]
        return out
    x = _layernorm(x + _L0_attn_ref(x, L0_attn_norm_w, L0_attn_Wq, L0_attn_Wkv, L0_attn_Wo, L0_attn_q_gamma, L0_attn_k_gamma), axis=-1)
    x = _layernorm(x + _L0_xattn_ref(L0_xattn_x1, x, ctx_1024, L0_xattn_W1, L0_xattn_b1, L0_xattn_W2, L0_xattn_b2, L0_xattn_W3, L0_xattn_b3), axis=-1)
    x = _layernorm(x + _L0_ffn_ref(x, L0_ffn_router_w, L0_ffn_w1, L0_ffn_b1, L0_ffn_w2, L0_ffn_b2, L0_ffn_gamma, L0_ffn_beta), axis=-1)
    x = _layernorm(x + _L1_attn_ref(x, L1_attn_Wq, L1_attn_Wk, L1_attn_Wv, L1_attn_Wc, L1_attn_terrace_mix, L1_attn_index_decays, L1_attn_mega_decays), axis=-1)
    x = _layernorm(x + _L1_xattn_ref(x, ctx_1024, L1_xattn_ln_gamma, L1_xattn_ln_beta, L1_xattn_w_q, L1_xattn_w_kv, L1_xattn_w_out, L1_xattn_b_out, L1_xattn_gate), axis=-1)
    x = _layernorm(x + _L1_ffn_ref(x, L1_ffn_rW1, L1_ffn_rb1, L1_ffn_rW2, L1_ffn_rb2, L1_ffn_We1, L1_ffn_be1, L1_ffn_We2, L1_ffn_be2), axis=-1)
    return x

_drawn_inputs = setup_inputs


def setup_inputs(seed=0):
    import zlib

    import numpy as np

    out = dict(_drawn_inputs(seed))
    spreads = {'L0_attn_norm_w': (1.0, 0.6),
     'L0_attn_q_gamma': (0.0, 0.706),
     'L0_attn_k_gamma': (0.0, 0.736),
     'L0_ffn_b1': (0.0, 0.302),
     'L0_ffn_b2': (0.0, 0.1),
     'L0_ffn_gamma': (1.0, 0.2),
     'L0_ffn_beta': (0.0, 0.1),
     'L1_attn_terrace_mix': (0.5, 0.6),
     'L1_xattn_ln_gamma': (1.0, 0.2),
     'L1_xattn_ln_beta': (0.0, 0.276),
     'L1_xattn_b_out': (0.0, 0.1),
     'L1_ffn_rb1': (0.0, 0.1),
     'L1_ffn_rb2': (0.0, 0.1),
     'L1_ffn_be1': (0.0, 0.1),
     'L1_ffn_be2': (0.0, 0.1)}
    factors = {'L0_xattn_b1': 64.0,
     'L0_xattn_b2': 2.68,
     'L1_attn_Wq': 7.739,
     'L1_attn_Wk': 8.0,
     'L1_attn_index_decays': 23.131,
     'L1_attn_mega_decays': 8.0}
    for name, (base, spread) in spreads.items():
        noise = np.random.default_rng([zlib.crc32(name.encode()), seed]).standard_normal(out[name].shape)
        drawn = base * np.exp(spread * noise) if base else spread * noise
        out[name] = jnp.asarray(drawn.astype(out[name].dtype))
    for name, factor in factors.items():
        out[name] = (out[name] * factor).astype(out[name].dtype)
    return out
```

```python
from contextlib import ExitStack

import concourse.bass as bass
from concourse import mybir

F32 = mybir.dt.float32
F32R = mybir.dt.float32r
BF16 = mybir.dt.bfloat16
ALU = mybir.AluOpType
ACT = mybir.ActivationFunctionType
AX = mybir.AxisListType

P = 128
B = 4
L = 512
D = 256
TC = L // P
KC = D // P
SC = 1024
LN_EPS = 1e-5
SLOTS = 23 * 256


ds = bass.ds


class Shared:

    def after_wait(self, engine):
        engine.sem_inc(self.passed[engine.engine], 1)


def setup(nc, g, ctx, x):
    g.X = ctx.enter_context(nc.sbuf_tensor("X", [P, B * TC, D], F32))
    g.ident = ctx.enter_context(nc.sbuf_tensor("ident", [P, P], F32))
    g.ones = ctx.enter_context(nc.sbuf_tensor("ones", [P, 64], F32))
    g.neg_half = ctx.enter_context(nc.sbuf_tensor("neg_half", [P, 16], F32))
    g.bank = ctx.enter_context(nc.psum_tensor("bank", [P, 8, 512], F32))
    g.zeros = ctx.enter_context(nc.sbuf_tensor("zeros", [P, D], F32))
    g.x_slots = nc.dram_tensor("x_slots", [SLOTS, D], F32).ap()
    g.y_slots = nc.dram_tensor("y_slots", [SLOTS, D], F32).ap()
    g.slots_zeroed = nc.alloc_semaphore("slots_zeroed")
    g.passed = {e.engine: nc.alloc_semaphore(f"passed_{n}")
                for n, e in (("dve", nc.vector), ("pool", nc.gpsimd), ("act", nc.scalar), ("pe", nc.tensor))}
    with ExitStack() as c:
        x_loaded = nc.alloc_semaphore("x_loaded")
        zeroed = nc.alloc_semaphore("ident_zeroed")
        made = nc.alloc_semaphore("constants_made")
        block = c.enter_context(nc.Block())

        @block.sync
        def _(sp):
            sp.dma_start(g.X[:, :, :], x.rearrange("b (t p) d -> p (b t) d", p=P)).then_inc(x_loaded, 16)
            sp.wait_ge(made, 4)
            sp.dma_start(g.x_slots.rearrange("(t p) d -> p t d", p=P),
                         g.zeros[:, None, :].to_broadcast([P, SLOTS // P, D])).then_inc(g.slots_zeroed, 16)
            sp.wait_ge(x_loaded, 16)

        @block.gpsimd
        def _(pool):
            pool.memset(g.ident[:, :], 0.0).then_inc(zeroed, 1)
            pool.memset(g.ones[:, :], 1.0).then_inc(made, 1)
            pool.memset(g.neg_half[:, :], -0.5).then_inc(made, 1)
            pool.memset(g.zeros[:, :], 0.0).then_inc(made, 1)
            pool.wait_ge(zeroed, 1)
            pool.affine_select(out=g.ident[:, :], in_=g.ident[:, :], compare_op=ALU.not_equal, fill=1.0,
                               base=0, pattern=[[-1, P]], channel_multiplier=1).then_inc(made, 1)
            pool.wait_ge(made, 4)


def finish(nc, g, out):
    with ExitStack() as c:
        stored = nc.alloc_semaphore("stored")
        block = c.enter_context(nc.Block())

        @block.sync
        def _(sp):
            sp.dma_start(out.rearrange("b (t p) d -> p (b t) d", p=P), g.X[:, :, :]).then_inc(stored, 16)
            sp.wait_ge(stored, 16)



class Norm:

    def __init__(self, nc, c, name):
        self.t = c.enter_context(nc.sbuf_tensor(f"{name}_sum", [P, TC, D], F32))
        self.st = c.enter_context(nc.sbuf_tensor(f"{name}_stats", [P, TC, 6], F32))
        self.mv = c.enter_context(nc.sbuf_tensor(f"{name}_mean_var", [P, TC, 2], F32))
        self.ve = c.enter_context(nc.sbuf_tensor(f"{name}_var_eps", [P, TC], F32))
        self.rs = c.enter_context(nc.sbuf_tensor(f"{name}_rstd", [P, TC], F32))
        self.sum_ready = nc.alloc_semaphore(f"{name}_sum_ready")
        self.stats_ready = nc.alloc_semaphore(f"{name}_stats_ready")
        self.mv_ready = nc.alloc_semaphore(f"{name}_mv_ready")
        self.ve_ready = nc.alloc_semaphore(f"{name}_ve_ready")
        self.rs_ready = nc.alloc_semaphore(f"{name}_rs_ready")
        self.banks_free = nc.alloc_semaphore(f"{name}_banks_free")
        self.x_ready = nc.alloc_semaphore(f"{name}_x_ready")

    def stats(self, g, dve, b):
        for t in range(TC):
            dve.wait_ge(self.sum_ready, b * TC + t + 1)
            dve.bn_stats(self.st[:, t, :], self.t[:, t, :]).then_inc(self.stats_ready, 1)
        for t in range(TC):
            dve.wait_ge(self.stats_ready, b * TC + t + 1)
            g.after_wait(dve)
            dve.bn_aggr(self.mv[:, t, :], self.st[:, t, :]).then_inc(self.mv_ready, 1)

    def rstd(self, g, pool, b, eps=LN_EPS):
        pool.wait_ge(self.mv_ready, b * TC + TC)
        g.after_wait(pool)
        pool.tensor_scalar(self.ve[:, :], self.mv[:, :, 1], eps, 0.0, ALU.add, ALU.add).then_inc(self.ve_ready, 1)
        pool.wait_ge(self.ve_ready, b + 1)
        pool.tensor_tensor(self.rs[:, :], self.ve[:, :], g.neg_half[:, 0:TC], ALU.pow).then_inc(self.rs_ready, 1)

    def apply(self, dve, out, b):
        dve.wait_ge(self.rs_ready, b + 1)
        for t in range(TC):
            dve.tensor_scalar(out(t), self.t[:, t, :], self.mv[:, t, 0:1], self.rs[:, t:t + 1],
                              ALU.subtract, ALU.mult).then_inc(self.x_ready, 1)



def l0_attention(nc, g, norm_w, wq, wkv, wo, q_gamma_t, k_gamma_t):
    H, DH, CLAMP = 16, 64, 50.0
    NP = H // 2
    RMS_EPS = 1.1920929e-07
    X, ident, bank = g.X, g.ident, g.bank
    with ExitStack() as c:
        def sb(name, shape, dt=F32):
            return c.enter_context(nc.sbuf_tensor("a0_" + name, shape, dt))

        def sem(name):
            return nc.alloc_semaphore("a0_" + name)

        w_qkv = sb("w_qkv", [P, KC, 3, H * DH])
        w_o = sb("w_o", [P, NP, D])
        nw = sb("norm_w", [P, KC])
        gam = sb("gammas", [P, 2, H])
        gam1 = sb("gammas_plus_1", [P, 2, H])
        gq = sb("gamma_product", [P, H])
        sq_junk = sb("sq_junk", [P, D])
        ssq = sb("ssq", [P, TC])
        ms = sb("mean_square", [P, TC])
        rs = sb("rms_scale", [P, TC])
        xs = sb("xs", [P, TC, D])
        xT = sb("xT", [P, KC, L])
        raw = sb("raw", [P, 3, TC, 3 * P])
        sq = sb("sq", [P, TC, 4, DH])
        ss = sb("ss", [P, TC, 4])
        sf = sb("sf", [P, TC, 4])
        rn = sb("rn", [P, TC, 4])
        nd = sb("nd", [P, TC, 4, 2, DH])
        KT = sb("KT", [P, 2, 2, L], F32R)
        QH = sb("QH", [P, 2, 2, L], F32R)
        QL = sb("QL", [P, 2, 2, L], F32R)
        E = sb("E", [P, 4, TC, L])
        es1 = sb("es1", [P, 2, L])
        es = sb("es", [P, 4, L])
        rec = sb("rec", [P, L])
        oT = sb("oT", [P, NP, L])
        ln = Norm(nc, c, "a0_ln")

        w_loaded, gam_loaded = sem("w_loaded"), sem("gam_loaded")
        gam_ready = sem("gam_ready")
        ssq_ready, ms_ready, rs_ready, xs_ready = sem("ssq_ready"), sem("ms_ready"), sem("rs_ready"), sem("xs_ready")
        xtp_ready, xT_ready = sem("xtp_ready"), sem("xT_ready")
        proj_ready, raw_ready = sem("proj_ready"), sem("raw_ready")
        sq_ready, ss_ready, sf_ready, rn_ready, nd_ready = sem("sq_ready"), sem("ss_ready"), sem("sf_ready"), sem("rn_ready"), sem("nd_ready")
        tr_ready, hi_ready, lo_ready = sem("tr_ready"), sem("hi_ready"), sem("lo_ready")
        s_ready, tanh_ready = sem("s_ready"), sem("tanh_ready")
        e_ready, es1_ready, es_ready = sem("e_ready"), sem("es1_ready"), sem("es_ready")
        o_ready, den_ready = sem("o_ready"), sem("den_ready")
        rec_ready, oT_ready = sem("rec_ready"), sem("oT_ready")
        wo_ready = sem("wo_ready")

        block = c.enter_context(nc.Block())

        @block.sync
        def _(sp):
            for kc in range(KC):
                rows = slice(kc * P, kc * P + P)
                sp.dma_start(w_qkv[:, kc, 0, :], wq[rows, :]).then_inc(w_loaded, 16)
                sp.dma_start(w_qkv[:, kc, 1:3, :], wkv[rows, :].rearrange("p (s n) -> p s n", s=2)).then_inc(w_loaded, 16)
            sp.dma_start(w_o[:, :, :], wo.rearrange("(n p) d -> p n d", p=P)).then_inc(w_loaded, 16)
            sp.wait_ge(w_loaded, 16 * 5)

        @block.gpsimd
        def _(pool):
            with pool.Fori(0, B) as b:
                pool.wait_ge(ssq_ready, b * TC + TC)
                g.after_wait(pool)
                pool.tensor_scalar(ms[:, :], ssq[:, :], 1.0 / D, RMS_EPS, ALU.mult, ALU.add).then_inc(ms_ready, 1)
                pool.wait_ge(ms_ready, b + 1)
                pool.tensor_tensor(rs[:, :], ms[:, :], g.neg_half[:, 0:TC], ALU.pow).then_inc(rs_ready, 1)

                def head_scales(p):
                    pool.wait_ge(ss_ready, b * NP + p + 1)
                    g.after_wait(pool)
                    pool.tensor_scalar(sf[:, :, :], ss[:, :, :], 1e-24, 0.0, ALU.max, ALU.add).then_inc(sf_ready, 1)
                    pool.wait_ge(sf_ready, b * NP + p + 1)
                    pool.tensor_tensor(rn[:, :, :], sf[:, :, :], g.neg_half[:, :].rearrange("p (t h) -> p t h", t=TC),
                                       ALU.pow).then_inc(rn_ready, 1)

                def key_sums(p, h):
                    n = 2 * p + h
                    pool.wait_ge(e_ready, b * H + n + 1)
                    if p >= 2:
                        pool.wait_ge(den_ready, b * NP + p - 1)
                    e = E[:, n % 4, :, :]
                    pool.tensor_tensor(es1[:, :, :], e[:, 0:2, :], e[:, 2:4, :], ALU.add).then_inc(es1_ready, 1)
                    pool.wait_ge(es1_ready, b * H + n + 1)
                    pool.tensor_tensor(es[:, n % 4, :], es1[:, 0, :], es1[:, 1, :], ALU.add).then_inc(es_ready, 1)
                    pool.wait_ge(es_ready, b * H + n + 1)

                head_scales(0)
                for p in range(NP):
                    if p + 1 < NP:
                        head_scales(p + 1)
                    key_sums(p, 0)
                    key_sums(p, 1)
                ln.rstd(g, pool, b)

        @block.scalar
        def _(act):
            act.dma_start(nw[:, :], norm_w).then_inc(gam_loaded, 16)
            for n, src in ((0, q_gamma_t), (1, k_gamma_t)):
                for half in range(2):
                    act.dma_start(gam[64 * half:64 * half + 64, n, :], src).then_inc(gam_loaded, 16)
            act.wait_ge(gam_loaded, 16 * 5)
            act.wait_ge(gam_ready, 2)
            with act.Fori(0, B) as b:
                for t in range(TC):
                    if t:
                        act.wait_ge(ssq_ready, b * TC + t)
                    act.activation(sq_junk[:, :], X[:, b * TC + t, :], ACT.Square,
                                   accum_out=ssq[:, t:t + 1]).then_inc(ssq_ready, 1)
                for kc in range(KC):
                    act.wait_ge(xtp_ready, b * KC + kc + 1)
                    act.activation(xT[:, kc, :], bank[:, 4 + kc, :], ACT.Copy, scale=nw[:, kc:kc + 1]).then_inc(xT_ready, 1)

                def keep_raw(p):
                    for t in range(TC):
                        act.wait_ge(proj_ready, b * TC * NP + TC * p + t + 1)
                        if t == 0 and p >= 3:
                            act.wait_ge(o_ready, b * NP + p - 2)
                            act.wait_ge(nd_ready, b * 4 * NP + 4 * (p - 2))
                        act.activation(raw[:, p % 3, t, :], bank[:, 2 + t % 2, 0:3 * P], ACT.Copy).then_inc(raw_ready, 1)

                def high_parts(p):
                    for j in range(4):
                        n = TC * p + j
                        act.wait_ge(tr_ready, b * TC * NP + n + 1)
                        src = bank[:, 4 + j % 2, :]
                        if j < 2:
                            act.activation(QH[:, p % 2, j, :], src, ACT.Copy, scale=gq[:, 2 * p + j:2 * p + j + 1]).then_inc(hi_ready, 1)
                        else:
                            act.activation(KT[:, p % 2, j - 2, :], src, ACT.Copy).then_inc(hi_ready, 1)

                def exps(p, h):
                    n = 2 * p + h
                    if n >= 4:
                        act.wait_ge(o_ready, b * NP + p - 1)
                        act.wait_ge(es_ready, b * H + n - 3)
                    for k in range(TC):
                        act.wait_ge(s_ready, b * H * TC + n * TC + k + 1)
                        act.activation(E[:, n % 4, k, :], bank[:, k % 2, :], ACT.Tanh, scale=1.0 / CLAMP).then_inc(tanh_ready, 1)
                    act.wait_ge(tanh_ready, b * H * TC + n * TC + TC)
                    act.activation(E[:, n % 4, :, :], E[:, n % 4, :, :], ACT.Exp, scale=CLAMP * DH ** -0.5).then_inc(e_ready, 1)

                keep_raw(0)
                high_parts(0)
                for p in range(NP):
                    if p + 1 < NP:
                        keep_raw(p + 1)
                    exps(p, 0)
                    exps(p, 1)
                    if p + 1 < NP:
                        high_parts(p + 1)

        @block.vector
        def _(dve):
            dve.wait_ge(gam_loaded, 16 * 5)
            dve.tensor_scalar(gam1[:, :, :], gam[:, :, :], 1.0, DH ** 0.5, ALU.add, ALU.mult).then_inc(gam_ready, 1)
            dve.wait_ge(gam_ready, 1)
            dve.tensor_tensor(gq[:, :], gam1[:, 0, :], gam1[:, 1, :], ALU.mult).then_inc(gam_ready, 1)
            dve.wait_ge(gam_ready, 2)
            dve.sem_inc(ln.banks_free, TC)
            with dve.Fori(0, B) as b:
                dve.wait_ge(rs_ready, b + 1)
                for t in range(TC):
                    dve.tensor_scalar(xs[:, t, :], X[:, b * TC + t, :], rs[:, t:t + 1], None, ALU.mult).then_inc(xs_ready, 1)

                def squares(p):
                    dve.wait_ge(raw_ready, b * TC * NP + TC * p + TC)
                    qk = raw[:, p % 3, :, 0:2 * P].rearrange("p t (h d) -> p t h d", d=DH)
                    dve.tensor_tensor(sq[:, :, :, :], qk, qk, ALU.mult).then_inc(sq_ready, 1)
                    dve.wait_ge(sq_ready, b * NP + p + 1)
                    dve.tensor_reduce(ss[:, :, :], sq[:, :, :, :], AX.X, ALU.add).then_inc(ss_ready, 1)

                def head_norms(p):
                    dve.wait_ge(rn_ready, b * NP + p + 1)
                    if p >= 1:
                        dve.wait_ge(tr_ready, b * TC * NP + TC * p)
                    for h in range(4):
                        src = raw[:, p % 3, :, DH * h:DH * h + DH]
                        dve.tensor_tensor(nd[:, :, h, :, :], src[:, :, None, :].to_broadcast([P, TC, 2, DH]),
                                          rn[:, :, h:h + 1, None].to_broadcast([P, TC, 2, DH]), ALU.mult).then_inc(nd_ready, 1)

                def low_parts(p):
                    for j in range(4):
                        dve.wait_ge(hi_ready, b * TC * NP + TC * p + j + 1)
                        src = bank[:, 4 + j % 2, :]
                        if j < 2:
                            dve.scalar_tensor_tensor(out=QL[:, p % 2, j, :], in0=src, scalar=gq[:, 2 * p + j:2 * p + j + 1],
                                                     in1=QH[:, p % 2, j, :].bitcast(F32), op0=ALU.mult,
                                                     op1=ALU.subtract).then_inc(lo_ready, 1)
                        else:
                            dve.tensor_tensor(KT[DH:P, p % 2, j - 2, :], src[DH:P], KT[DH:P, p % 2, j - 2, :].bitcast(F32),
                                              ALU.subtract).then_inc(lo_ready, 1)

                def normalise(p):
                    dve.wait_ge(den_ready, b * NP + p + 1)
                    if p >= 1:
                        dve.wait_ge(oT_ready, b * NP + p)
                    dve.reciprocal(rec[:, :], bank[:, 7, :]).then_inc(rec_ready, 1)
                    dve.wait_ge(rec_ready, b * NP + p + 1)
                    dve.wait_ge(o_ready, b * NP + p + 1)
                    dve.tensor_tensor(oT[:, p, :], bank[:, 6, :], rec[:, :], ALU.mult).then_inc(oT_ready, 1)

                squares(0)
                head_norms(0)
                low_parts(0)
                for p in range(NP):
                    if p >= 2:
                        normalise(p - 2)
                    if p + 1 < NP:
                        squares(p + 1)
                        head_norms(p + 1)
                        low_parts(p + 1)
                normalise(NP - 2)
                normalise(NP - 1)
                for t in range(TC):
                    dve.wait_ge(wo_ready, b * TC + t + 1)
                    dve.tensor_tensor(ln.t[:, t, :], bank[:, 2 + t, 0:D], X[:, b * TC + t, :], ALU.add).then_inc(ln.sum_ready, 1)
                dve.wait_ge(ln.sum_ready, b * TC + TC)
                dve.sem_inc(ln.banks_free, TC)
                ln.stats(g, dve, b)
                ln.apply(dve, lambda t: X[:, b * TC + t, :], b)

        @block.tensor
        def _(pe):
            pe.wait_ge(w_loaded, 16 * 5)
            with pe.Fori(0, B) as b:
                pe.wait_ge(ln.banks_free, b * TC + TC)
                pe.wait_ge(xs_ready, b * TC + TC)
                for kc in range(KC):
                    for t in range(TC):
                        i = pe.transpose(bank[:, 4 + kc, t * P:t * P + P], xs[:, t, kc * P:kc * P + P], ident[:, :])
                    i.then_inc(xtp_ready, 1)
                pe.wait_ge(xT_ready, b * KC + KC)

                def project(p):
                    for t in range(TC):
                        n = TC * p + t
                        if n >= 2:
                            pe.wait_ge(raw_ready, b * TC * NP + n - 1)
                        for kc in range(KC):
                            i = pe.matmul(bank[:, 2 + t % 2, 0:3 * P].rearrange("p (s n) -> p s n", s=3),
                                          xT[:, kc, t * P:t * P + P], w_qkv[:, kc, :, p * P:p * P + P],
                                          start=(kc == 0), stop=(kc == KC - 1))
                        i.then_inc(proj_ready, 1)

                def turn(p):
                    pe.wait_ge(nd_ready, b * 4 * NP + 4 * p + 4)
                    for j in range(4):
                        n = TC * p + j
                        if n >= 2:
                            pe.wait_ge(lo_ready, b * TC * NP + n - 1)
                        for t in range(TC):
                            i = pe.transpose(bank[:, 4 + j % 2, t * P:t * P + P],
                                             nd[:, t, j, :, :].rearrange("p a d -> p (a d)"), ident[:, :])
                        i.then_inc(tr_ready, 1)

                def scores(p, h):
                    if h == 0:
                        pe.wait_ge(lo_ready, b * TC * NP + TC * p + TC)
                    for k in range(TC):
                        n = (2 * p + h) * TC + k
                        if n >= 2:
                            pe.wait_ge(tanh_ready, b * H * TC + n - 1)
                        kt = KT[:, p % 2, h, k * P:k * P + P]
                        pe.matmul(bank[:, k % 2, :], kt, QL[:, p % 2, h, :], start=True, stop=False)
                        pe.matmul(bank[:, k % 2, :], kt, QH[:, p % 2, h, :], start=False, stop=True).then_inc(s_ready, 1)

                def values(p, chunks):
                    for k in chunks:
                        for h in range(2):
                            n = 2 * p + h
                            if k == 0:
                                pe.wait_ge(e_ready, b * H + n + 1)
                            if k == 0 and h == 0 and p >= 1:
                                pe.wait_ge(oT_ready, b * NP + p)
                            i = pe.matmul(bank[DH * h:DH * h + DH, 6, :], raw[:, p % 3, k, 2 * P + DH * h:2 * P + DH * h + DH],
                                          E[:, n % 4, k, :], start=(k == 0), stop=(k == TC - 1))
                    if k == TC - 1:
                        i.then_inc(o_ready, 1)

                def denominators(p):
                    pe.wait_ge(es_ready, b * H + 2 * p + 2)
                    if p >= 1:
                        pe.wait_ge(rec_ready, b * NP + p)
                    for h in range(2):
                        i = pe.matmul(bank[DH * h:DH * h + DH, 7, :], g.ones[:, :], es[:, (2 * p + h) % 4, :],
                                      start=True, stop=True)
                    i.then_inc(den_ready, 1)

                project(0)
                turn(0)
                for p in range(NP):
                    if p + 1 < NP:
                        project(p + 1)
                    scores(p, 0)
                    if p >= 1:
                        values(p - 1, (0, 1))
                    scores(p, 1)
                    if p >= 1:
                        values(p - 1, (2, 3))
                        denominators(p - 1)
                    if p + 1 < NP:
                        turn(p + 1)
                values(NP - 1, range(TC))
                denominators(NP - 1)
                pe.wait_ge(oT_ready, b * NP + NP)
                for t in range(TC):
                    for p in range(NP):
                        i = pe.matmul(bank[:, 2 + t, 0:D], oT[:, p, t * P:t * P + P], w_o[:, p, :],
                                      start=(p == 0), stop=(p == NP - 1))
                    i.then_inc(wo_ready, 1)

def l0_cross_attention(nc, g, ctx_rows, x1_t, w1_t, b1, w2_t, b2, w3_t, b3):
    SCALE = 8 ** -0.5
    NS = SC // P
    X, ident, bank = g.X, g.ident, g.bank
    with ExitStack() as c:
        def sb(name, shape, dt=F32):
            return c.enter_context(nc.sbuf_tensor("c0_" + name, shape, dt))

        def sem(name):
            return nc.alloc_semaphore("c0_" + name)

        ctx = sb("ctx", [P, B * NS, D])
        x1T = sb("x1T", [P, KC, SC])
        w1, w2, w3 = sb("w1", [P, KC, D]), sb("w2", [P, KC, D]), sb("w3", [P, KC, D])
        bias = sb("bias", [P, 2, KC])
        b3row = sb("b3row", [P, D])
        v1T = sb("v1T", [P, KC, SC])
        xT = sb("xT", [P, KC, L])
        xs = sb("xs", [P, TC, D])
        xb = sb("xb", [P, TC, D])
        mx, nm = sb("mx", [P, TC]), sb("nm", [P, TC])
        sums, rsum = sb("sums", [P, TC]), sb("rsum", [P, TC])
        E = sb("E", [P, 2, SC])
        ET = sb("ET", [P, 2, NS, P])
        v5 = sb("v5", [P, 2, D])
        v5T = sb("v5T", [P, KC, L])
        v6T = sb("v6T", [P, KC, L])
        ln = Norm(nc, c, "c0_ln")

        w_loaded, ctx_loaded, small_loaded = sem("w_loaded"), sem("ctx_loaded"), sem("small_loaded")
        v1_ready, v1_kept = sem("v1_ready"), sem("v1_kept")
        xs_ready = sem("xs_ready")
        xtp_ready, xT_ready, xb_ready = sem("xtp_ready"), sem("xT_ready"), sem("xb_ready")
        s_ready, mx_ready, nm_ready, e_ready = sem("s_ready"), sem("mx_ready"), sem("nm_ready"), sem("e_ready")
        et_ready = sem("et_ready")
        et0_kept, et1_kept = sem("et0_kept"), sem("et1_kept")
        av_ready, rsum_ready, v5_ready = sem("av_ready"), sem("rsum_ready"), sem("v5_ready")
        v5t_ready, v5T_ready = sem("v5t_ready"), sem("v5T_ready")
        v6_ready, v6T_ready, v7_ready = sem("v6_ready"), sem("v6T_ready"), sem("v7_ready")

        block = c.enter_context(nc.Block())

        @block.sync
        def _(sp):
            sp.dma_start(w1[:, :, :], w1_t.rearrange("(k p) n -> p k n", p=P)).then_inc(w_loaded, 16)
            sp.dma_start(x1T[:, :, :], x1_t.rearrange("(k p) n -> p k n", p=P)).then_inc(w_loaded, 16)
            sp.dma_start(w2[:, :, :], w2_t.rearrange("(k p) n -> p k n", p=P)).then_inc(w_loaded, 16)
            sp.dma_start(w3[:, :, :], w3_t.rearrange("(k p) n -> p k n", p=P)).then_inc(w_loaded, 16)
            sp.dma_start(ctx[:, :, :], ctx_rows.rearrange("b (k p) d -> p (b k) d", p=P)).then_inc(ctx_loaded, 16)
            sp.wait_ge(w_loaded, 64)
            sp.wait_ge(ctx_loaded, 16)

        @block.gpsimd
        def _(pool):
            pool.wait_ge(small_loaded, 48)
            with pool.Fori(0, B) as b:
                for t in range(TC):
                    pool.tensor_tensor(xb[:, t, :], X[:, b * TC + t, :], b3row[:, :], ALU.add).then_inc(xb_ready, 1)
                ln.rstd(g, pool, b)

        @block.scalar
        def _(act):
            act.dma_start(bias[:, 0, :], b1).then_inc(small_loaded, 16)
            act.dma_start(bias[:, 1, :], b2).then_inc(small_loaded, 16)
            act.dma_start(b3row[:, :], b3.partition_broadcast(P)).then_inc(small_loaded, 16)
            act.wait_ge(small_loaded, 48)
            for n in range(4):
                e, s = n // 2, n % 2
                act.wait_ge(v1_ready, n + 1)
                act.activation(v1T[:, e, s * 512:s * 512 + 512], bank[:, n, :], ACT.Identity,
                               bias=bias[:, 0, e:e + 1]).then_inc(v1_kept, 1)
            with act.Fori(0, B) as b:
                for kc in range(KC):
                    act.wait_ge(xtp_ready, b * KC + kc + 1)
                    act.activation(xT[:, kc, :], bank[:, 6 + kc, :], ACT.Copy).then_inc(xT_ready, 1)

                def exps(t):
                    if t >= 2:
                        act.wait_ge(et_ready, b * 2 * TC + 2 * (t - 1))
                    act.wait_ge(nm_ready, b * TC + t + 1)
                    s = bank[:, 2 * (t % 2):2 * (t % 2) + 2, :].rearrange("p a n -> p (a n)")
                    act.activation(E[:, t % 2, :], s, ACT.Exp, bias=nm[:, t:t + 1], scale=SCALE,
                                   accum_out=sums[:, t:t + 1]).then_inc(e_ready, 1)

                def keep(t):
                    if t >= 2:
                        act.wait_ge(av_ready, b * TC + t - 1)
                    act.wait_ge(et_ready, b * 2 * TC + 2 * t + 1)
                    act.activation(ET[:, t % 2, 0:4, :].rearrange("p k n -> p (k n)"), bank[:, 4, :], ACT.Copy).then_inc(et0_kept, 1)

                def weighted(t):
                    act.wait_ge(av_ready, b * TC + t + 1)
                    act.wait_ge(rsum_ready, b * TC + t + 1)
                    if t >= 2:
                        act.wait_ge(v5t_ready, b * TC + t - 1)
                    act.activation(v5[:, t % 2, :], bank[:, 6, 0:D], ACT.Copy, scale=rsum[:, t:t + 1]).then_inc(v5_ready, 1)

                exps(0)
                exps(1)
                for t in range(TC):
                    keep(t)
                    weighted(t)
                    if t + 2 < TC:
                        exps(t + 2)
                for e in range(KC):
                    act.wait_ge(v6_ready, b * KC + e + 1)
                    act.activation(v6T[:, e, :], bank[:, e, :], ACT.Identity, bias=bias[:, 1, e:e + 1]).then_inc(v6T_ready, 1)

        @block.vector
        def _(dve):
            dve.sem_inc(ln.banks_free, TC)
            with dve.Fori(0, B) as b:
                dve.tensor_copy(xs[:, :, :], X[:, ds(b * TC, TC), :]).then_inc(xs_ready, 1)

                def maxima(t):
                    dve.wait_ge(s_ready, b * TC + t + 1)
                    s = bank[:, 2 * (t % 2):2 * (t % 2) + 2, :]
                    dve.tensor_reduce(mx[:, t:t + 1], s, AX.XY, ALU.max).then_inc(mx_ready, 1)
                    dve.wait_ge(mx_ready, b * TC + t + 1)
                    dve.tensor_scalar(nm[:, t:t + 1], mx[:, t:t + 1], -SCALE, None, ALU.mult).then_inc(nm_ready, 1)

                def keep(t):
                    if t >= 2:
                        dve.wait_ge(av_ready, b * TC + t - 1)
                    dve.wait_ge(et_ready, b * 2 * TC + 2 * t + 2)
                    dve.tensor_copy(ET[:, t % 2, 4:8, :].rearrange("p k n -> p (k n)"), bank[:, 5, :]).then_inc(et1_kept, 1)
                    dve.wait_ge(e_ready, b * TC + t + 1)
                    dve.reciprocal(rsum[:, t:t + 1], sums[:, t:t + 1]).then_inc(rsum_ready, 1)

                def keep_v5T(t):
                    dve.wait_ge(v5t_ready, b * TC + t + 1)
                    dve.tensor_copy(v5T[:, :, t * P:t * P + P], bank[:, 7, 0:2 * P].rearrange("p (k n) -> p k n", k=KC)).then_inc(v5T_ready, 1)

                maxima(0)
                maxima(1)
                for t in range(TC):
                    keep(t)
                    if t + 2 < TC:
                        maxima(t + 2)
                    keep_v5T(t)
                dve.wait_ge(xb_ready, b * TC + TC)
                for t in range(TC):
                    dve.wait_ge(v7_ready, b * TC + t + 1)
                    dve.tensor_tensor(ln.t[:, t, :], bank[:, 2 + t, 0:D], xb[:, t, :], ALU.add).then_inc(ln.sum_ready, 1)
                dve.wait_ge(ln.sum_ready, b * TC + TC)
                dve.sem_inc(ln.banks_free, TC)
                ln.stats(g, dve, b)
                ln.apply(dve, lambda t: X[:, b * TC + t, :], b)

        @block.tensor
        def _(pe):
            pe.wait_ge(w_loaded, 64)
            for n in range(4):
                e, s = n // 2, n % 2
                for kc in range(KC):
                    i = pe.matmul(bank[:, n, :], w1[:, kc, e * P:e * P + P], x1T[:, kc, s * 512:s * 512 + 512],
                                  start=(kc == 0), stop=(kc == KC - 1))
                i.then_inc(v1_ready, 1)
            pe.wait_ge(v1_kept, 4)
            pe.wait_ge(ctx_loaded, 16)
            with pe.Fori(0, B) as b:
                pe.wait_ge(ln.banks_free, b * TC + TC)
                pe.wait_ge(xs_ready, b + 1)
                for kc in range(KC):
                    for t in range(TC):
                        i = pe.transpose(bank[:, 6 + kc, t * P:t * P + P], xs[:, t, kc * P:kc * P + P], ident[:, :])
                    i.then_inc(xtp_ready, 1)
                pe.wait_ge(xT_ready, b * KC + KC)

                def scores(t):
                    if t >= 2:
                        pe.wait_ge(e_ready, b * TC + t - 1)
                    for s in range(2):
                        for kc in range(KC):
                            i = pe.matmul(bank[:, 2 * (t % 2) + s, :], xT[:, kc, t * P:t * P + P],
                                          v1T[:, kc, s * 512:s * 512 + 512], start=(kc == 0), stop=(kc == KC - 1))
                    i.then_inc(s_ready, 1)

                def turn(t):
                    pe.wait_ge(e_ready, b * TC + t + 1)
                    for half in range(2):
                        if t >= 1:
                            pe.wait_ge(et1_kept if half else et0_kept, b * TC + t)
                        for k in range(4):
                            s = (4 * half + k) * P
                            i = pe.transpose(bank[:, 4 + half, k * P:k * P + P], E[:, t % 2, s:s + P], ident[:, :])
                        i.then_inc(et_ready, 1)

                def values(t):
                    pe.wait_ge(et0_kept, b * TC + t + 1)
                    pe.wait_ge(et1_kept, b * TC + t + 1)
                    if t >= 1:
                        pe.wait_ge(v5_ready, b * TC + t)
                    for k in range(NS):
                        i = pe.matmul(bank[:, 6, 0:D], ET[:, t % 2, k, :], ctx[:, b * NS + k, :],
                                      start=(k == 0), stop=(k == NS - 1))
                    i.then_inc(av_ready, 1)

                def turn_v5(t):
                    pe.wait_ge(v5_ready, b * TC + t + 1)
                    if t >= 1:
                        pe.wait_ge(v5T_ready, b * TC + t)
                    for kc in range(KC):
                        i = pe.transpose(bank[:, 7, kc * P:kc * P + P], v5[:, t % 2, kc * P:kc * P + P], ident[:, :])
                    i.then_inc(v5t_ready, 1)

                scores(0)
                scores(1)
                for t in range(TC):
                    turn(t)
                    if t >= 1:
                        turn_v5(t - 1)
                    values(t)
                    if t + 2 < TC:
                        scores(t + 2)
                turn_v5(TC - 1)
                pe.wait_ge(v5T_ready, b * TC + TC)
                for e in range(KC):
                    for kc in range(KC):
                        i = pe.matmul(bank[:, e, :], w2[:, kc, e * P:e * P + P], v5T[:, kc, :],
                                      start=(kc == 0), stop=(kc == KC - 1))
                    i.then_inc(v6_ready, 1)
                pe.wait_ge(v6T_ready, b * KC + KC)
                for t in range(TC):
                    for kc in range(KC):
                        i = pe.matmul(bank[:, 2 + t, 0:D], v6T[:, kc, t * P:t * P + P], w3[:, kc, :],
                                      start=(kc == 0), stop=(kc == KC - 1))
                    i.then_inc(v7_ready, 1)



NT = B * TC
FF = 1024
FC = FF // P
BLOCK = 256
BC = BLOCK // P


def most_blocks(experts):
    return (2 * B * L + experts * (BLOCK - 1)) // BLOCK


class Routing:

    def __init__(self, nc, c, name, experts):
        self.blocks = most_blocks(experts)
        self.weight = c.enter_context(nc.sbuf_tensor(f"{name}_weight", [P, 2, NT, 1], F32))
        self.slot = c.enter_context(nc.sbuf_tensor(f"{name}_slot", [P, 2, NT], mybir.dt.uint32))
        self.block_expert = c.enter_context(nc.sbuf_tensor(f"{name}_block_expert", [P, self.blocks], mybir.dt.int32))


class TopTwo:

    def __init__(self, nc, c, name):
        self.score = c.enter_context(nc.sbuf_tensor(f"{name}_score", [P, NT, 8], F32))
        self.top = c.enter_context(nc.sbuf_tensor(f"{name}_top", [P, NT, 8], F32))
        self.index = c.enter_context(nc.sbuf_tensor(f"{name}_index", [P, NT, 8], mybir.dt.uint32))
        self.index_f = c.enter_context(nc.sbuf_tensor(f"{name}_index_f", [P, NT, 2], F32))
        self.expert = c.enter_context(nc.sbuf_tensor(f"{name}_expert", [P, 8], mybir.dt.int32))
        self.expert_f = c.enter_context(nc.sbuf_tensor(f"{name}_expert_f", [P, 8], F32))
        self.pick = c.enter_context(nc.sbuf_tensor(f"{name}_pick", [P, 2, NT, 8], F32))
        self.numbered = nc.alloc_semaphore(f"{name}_numbered")
        self.top_ready = nc.alloc_semaphore(f"{name}_top_ready")
        self.index_ready = nc.alloc_semaphore(f"{name}_index_ready")
        self.pick_ready = nc.alloc_semaphore(f"{name}_pick_ready")
        self.gated = nc.alloc_semaphore(f"{name}_gated")

    def number_experts(self, pool):
        pool.iota(self.expert[:, :], pattern=[[1, 8]], base=0, channel_multiplier=0).then_inc(self.numbered, 1)

    def find(self, dve):
        for n in range(NT):
            dve.max(self.top[:, n, :], self.score[:, n, :]).then_inc(self.top_ready, 1)
        for n in range(NT):
            dve.wait_ge(self.top_ready, n + 1)
            dve.max_index(self.index[:, n, :], self.top[:, n, :], self.score[:, n, :]).then_inc(self.index_ready, 1)
        dve.wait_ge(self.index_ready, NT)
        dve.tensor_copy(self.index_f[:, :, :], self.index[:, :, 0:2]).then_inc(self.index_ready, 1)
        dve.wait_ge(self.numbered, 1)
        dve.tensor_copy(self.expert_f[:, :], self.expert[:, :]).then_inc(self.index_ready, 1)
        dve.wait_ge(self.index_ready, NT + 2)
        for k in range(2):
            dve.tensor_tensor(self.pick[:, k, :, :], self.expert_f[:, None, :].to_broadcast([P, NT, 8]),
                              self.index_f[:, :, k:k + 1].to_broadcast([P, NT, 8]), ALU.is_equal).then_inc(self.pick_ready, 1)


class Slots:

    def __init__(self, nc, c, name, experts, routing):
        def sb(n, shape, dt=F32):
            return c.enter_context(nc.sbuf_tensor(f"{name}_{n}", shape, dt))

        self.experts, self.routing = experts, routing
        NB = routing.blocks
        self.chosen = sb("chosen", [P, NT, 8])
        self.before = sb("before", [P, P])
        self.all = sb("all", [P, P])
        self.cum = sb("cum", [P, NT + 1, 8])
        self.number = sb("number", [P, NB], mybir.dt.int32)
        self.number_f = sb("number_f", [P, NB])
        self.full = sb("full", [P, 8])
        self.started = sb("started", [P, 8, 8])
        self.blocks = sb("blocks", [P, 8])
        self.end = sb("end", [P, 8])
        self.base = sb("base", [P, 8])
        self.past = sb("past", [P, NB, 8])
        self.expert_of = sb("expert_of", [P, NB])
        self.position = sb("position", [P, NT, 8])
        self.picked = sb("picked", [P, 2, NT, 8])
        self.slot_f = sb("slot_f", [P, 2, NT])
        self.made = nc.alloc_semaphore(f"{name}_made")
        self.chosen_ready = nc.alloc_semaphore(f"{name}_chosen_ready")
        self.counted = nc.alloc_semaphore(f"{name}_counted")
        self.step = nc.alloc_semaphore(f"{name}_step")

    def constants(self, pool):
        pool.memset(self.all[:, :], 1.0).then_inc(self.made, 1)
        pool.memset(self.before[:, :], 1.0).then_inc(self.made, 1)
        pool.iota(self.number[:, :], pattern=[[1, self.routing.blocks]], base=0, channel_multiplier=0).then_inc(self.made, 1)
        pool.wait_ge(self.made, 2)
        pool.affine_select(out=self.before[:, :], in_=self.before[:, :], compare_op=ALU.is_ge, fill=0.0,
                           base=-1, pattern=[[1, P]], channel_multiplier=-1).then_inc(self.made, 1)

    def count(self, g, pe):
        pe.wait_ge(self.made, 4)
        pe.wait_ge(self.chosen_ready, 1)
        for n, ones in ((0, self.before), (1, self.all)):
            i = pe.matmul(g.bank[:, 3, P * n:P * n + P], ones[:, :], self.chosen[:, :, :].rearrange("p n e -> p (n e)"),
                          start=True, stop=True)
        i.then_inc(self.counted, 1)

    def assign(self, g, dve, top):
        NB, steps = self.routing.blocks, [0]

        def step(instruction):
            instruction.then_inc(self.step, 1)
            steps[0] += 1
            dve.wait_ge(self.step, steps[0])

        dve.wait_ge(top.pick_ready, 2)
        dve.tensor_tensor(self.chosen[:, :, :], top.pick[:, 0, :, :], top.pick[:, 1, :, :], ALU.add).then_inc(self.chosen_ready, 1)
        step(dve.memset(self.cum[:, 0, :], 0.0))
        step(dve.tensor_scalar(self.full[:, :], top.expert_f[:, :], float(BLOCK), None, ALU.mult))
        dve.wait_ge(self.made, 4)
        step(dve.tensor_copy(self.number_f[:, :], self.number[:, :]))
        dve.wait_ge(self.counted, 1)
        before = g.bank[:, 3, 0:P].rearrange("p (n e) -> p n e", e=8)
        whole = g.bank[:, 3, P:2 * P].rearrange("p (n e) -> p n e", e=8)
        for n in range(NT):
            step(dve.tensor_tensor(self.cum[:, n + 1, :], self.cum[:, n, :], whole[:, n, :], ALU.add))
        step(dve.tensor_tensor(self.started[:, :, :], self.cum[:, NT, :, None].to_broadcast([P, 8, 8]),
                               self.full[:, None, :].to_broadcast([P, 8, 8]), ALU.is_gt))
        step(dve.tensor_reduce(self.blocks[:, :], self.started[:, :, :], AX.X, ALU.add))
        step(dve.tensor_copy(self.end[:, 0:1], self.blocks[:, 0:1]))
        for e in range(1, 8):
            step(dve.tensor_tensor(self.end[:, e:e + 1], self.end[:, e - 1:e], self.blocks[:, e:e + 1], ALU.add))
        step(dve.tensor_tensor(self.base[:, :], self.end[:, :], self.blocks[:, :], ALU.subtract))
        step(dve.tensor_scalar(self.base[:, :], self.base[:, :], float(BLOCK), None, ALU.mult))
        step(dve.tensor_tensor(self.past[:, :, :], self.number_f[:, :, None].to_broadcast([P, NB, 8]),
                               self.end[:, None, :].to_broadcast([P, NB, 8]), ALU.is_ge))
        step(dve.tensor_reduce(self.expert_of[:, :], self.past[:, :, :], AX.X, ALU.add))
        step(dve.tensor_scalar(self.routing.block_expert[:, :], self.expert_of[:, :], float(self.experts - 1), None, ALU.min))
        step(dve.tensor_tensor(self.position[:, :, :], before, self.cum[:, 0:NT, :], ALU.add))
        step(dve.tensor_tensor(self.position[:, :, :], self.position[:, :, :], self.base[:, None, :].to_broadcast([P, NT, 8]), ALU.add))
        for k in range(2):
            step(dve.tensor_tensor(self.picked[:, k, :, :], top.pick[:, k, :, :], self.position[:, :, :], ALU.mult))
        step(dve.tensor_reduce(self.slot_f[:, :, :], self.picked[:, :, :, :], AX.X, ALU.add))
        step(dve.tensor_copy(self.routing.slot[:, :, :], self.slot_f[:, :, :]))


class TurnX:

    def __init__(self, nc, c, name):
        self.xs = c.enter_context(nc.sbuf_tensor(f"{name}_xs", [P, TC, D], F32))
        self.xTb = c.enter_context(nc.sbuf_tensor(f"{name}_xTb", [P, KC, L], F32))
        self.xs_ready = nc.alloc_semaphore(f"{name}_xs_ready")
        self.turned = nc.alloc_semaphore(f"{name}_turned")
        self.xTb_ready = nc.alloc_semaphore(f"{name}_xTb_ready")

    def copy(self, g, dve, b):
        dve.tensor_copy(self.xs[:, :, :], g.X[:, ds(b * TC, TC), :]).then_inc(self.xs_ready, 1)

    def turn(self, g, pe, b):
        pe.wait_ge(self.xs_ready, b + 1)
        for kc in range(KC):
            for t in range(TC):
                i = pe.transpose(g.bank[:, kc, t * P:t * P + P], self.xs[:, t, kc * P:kc * P + P], g.ident[:, :])
            i.then_inc(self.turned, 1)

    def take(self, g, act, b):
        for kc in range(KC):
            act.wait_ge(self.turned, b * KC + kc + 1)
            act.activation(self.xTb[:, kc, :], g.bank[:, kc, :], ACT.Copy).then_inc(self.xTb_ready, 1)


def l0_router(nc, g, routing, router_w):
    E = 8
    with ExitStack() as c:
        def sb(name, shape, dt=F32):
            return c.enter_context(nc.sbuf_tensor("r0_" + name, shape, dt))

        def sem(name):
            return nc.alloc_semaphore("r0_" + name)

        w = sb("w", [P, KC, E])
        diff, weight = sb("diff", [P, NT, 1]), routing.weight
        den = sb("den", [P, NT, 1])
        turn, top = TurnX(nc, c, "r0"), TopTwo(nc, c, "r0_top")
        slots = Slots(nc, c, "r0_slots", E, routing)
        w_loaded, logits_ready, logits_kept = sem("w_loaded"), sem("logits_ready"), sem("logits_kept")
        diff_ready, exp_ready, weight_ready = sem("diff_ready"), sem("exp_ready"), sem("weight_ready")
        block = c.enter_context(nc.Block())

        @block.sync
        def _(sp):
            sp.dma_start(w[:, :, :], router_w.rearrange("(k p) e -> p k e", p=P)).then_inc(w_loaded, 16)
            sp.wait_ge(w_loaded, 16)

        @block.gpsimd
        def _(pool):
            top.number_experts(pool)
            slots.constants(pool)

        @block.scalar
        def _(act):
            with act.Fori(0, B) as b:
                turn.take(g, act, b)
            act.wait_ge(diff_ready, 1)
            act.activation(weight[:, 1, :, :], diff[:, :, :], ACT.Exp).then_inc(exp_ready, 1)

        @block.tensor
        def _(pe):
            pe.wait_ge(w_loaded, 16)
            with pe.Fori(0, B) as b:
                turn.turn(g, pe, b)
                pe.wait_ge(turn.xTb_ready, b * KC + KC)
                pe.wait_ge(logits_kept, b + 1)
                for t in range(TC):
                    for kc in range(KC):
                        i = pe.matmul(g.bank[:, 2, t * E:t * E + E], turn.xTb[:, kc, t * P:t * P + P], w[:, kc, :],
                                      start=(kc == 0), stop=(kc == KC - 1))
                i.then_inc(logits_ready, 1)
            slots.count(g, pe)

        @block.vector
        def _(dve):
            dve.sem_inc(logits_kept, 1)
            with dve.Fori(0, B) as b:
                turn.copy(g, dve, b)
                dve.wait_ge(logits_ready, b + 1)
                dve.tensor_copy(top.score[:, ds(b * TC, TC), :],
                                g.bank[:, 2, 0:TC * E].rearrange("p (t e) -> p t e", e=E)).then_inc(logits_kept, 1)
            dve.wait_ge(logits_kept, B + 1)
            top.find(dve)
            dve.tensor_tensor(diff[:, :, :], top.top[:, :, 1:2], top.top[:, :, 0:1], ALU.subtract).then_inc(diff_ready, 1)
            dve.wait_ge(exp_ready, 1)
            dve.tensor_scalar(den[:, :, :], weight[:, 1, :, :], 1.0, None, ALU.add).then_inc(weight_ready, 1)
            dve.wait_ge(weight_ready, 1)
            dve.reciprocal(weight[:, 0, :, :], den[:, :, :]).then_inc(weight_ready, 1)
            dve.wait_ge(weight_ready, 2)
            dve.tensor_tensor(weight[:, 1, :, :], weight[:, 1, :, :], weight[:, 0, :, :], ALU.mult).then_inc(weight_ready, 1)
            dve.wait_ge(weight_ready, 3)
            slots.assign(g, dve, top)


def l1_router(nc, g, routing, rw1, rb1, rw2, rb2):
    E, RC = 4, 4
    with ExitStack() as c:
        def sb(name, shape, dt=F32):
            return c.enter_context(nc.sbuf_tensor("r1_" + name, shape, dt))

        def sem(name):
            return nc.alloc_semaphore("r1_" + name)

        w1 = sb("w1", [P, KC, RC * P])
        b1 = sb("b1", [P, RC])
        w2 = sb("w2", [P, RC, E])
        b2row = sb("b2row", [P, E])
        rh = sb("rh", [P, RC, L])
        logits = sb("logits", [P, NT, E])
        mx, sub, ex = sb("mx", [P, NT]), sb("sub", [P, NT, E]), sb("ex", [P, NT, E])
        sums, rsum = sb("sums", [P, NT]), sb("rsum", [P, NT])
        turn, top = TurnX(nc, c, "r1"), TopTwo(nc, c, "r1_top")
        slots = Slots(nc, c, "r1_slots", E, routing)
        w_loaded, h_ready, rh_ready = sem("w_loaded"), sem("h_ready"), sem("rh_ready")
        logits_ready, logits_kept, padded = sem("logits_ready"), sem("logits_kept"), sem("padded")
        step_ready, exp_ready = sem("step_ready"), sem("exp_ready")
        block = c.enter_context(nc.Block())

        @block.sync
        def _(sp):
            sp.dma_start(w1[:, :, :], rw1.rearrange("(k p) n -> p k n", p=P)).then_inc(w_loaded, 16)
            sp.dma_start(w2[:, :, :], rw2.rearrange("(k p) e -> p k e", p=P)).then_inc(w_loaded, 16)
            sp.dma_start(b1[:, :], rb1).then_inc(w_loaded, 16)
            sp.dma_start(b2row[:, :], rb2.partition_broadcast(P)).then_inc(w_loaded, 16)
            sp.wait_ge(w_loaded, 64)

        @block.gpsimd
        def _(pool):
            top.number_experts(pool)
            pool.memset(top.score[:, :, :], -1.0).then_inc(padded, 1)
            slots.constants(pool)

        @block.scalar
        def _(act):
            act.wait_ge(w_loaded, 64)
            with act.Fori(0, B) as b:
                turn.take(g, act, b)
                for r in range(RC):
                    if r == 0:
                        act.wait_ge(logits_kept, b + 1)
                    act.wait_ge(h_ready, b * RC + r + 1)
                    act.activation(rh[:, r, :], g.bank[:, 4 + r, :], ACT.Gelu, bias=b1[:, r:r + 1]).then_inc(rh_ready, 1)
            act.wait_ge(step_ready, 2)
            act.activation(ex[:, :, :], sub[:, :, :], ACT.Exp).then_inc(exp_ready, 1)

        @block.tensor
        def _(pe):
            pe.wait_ge(w_loaded, 64)
            with pe.Fori(0, B) as b:
                turn.turn(g, pe, b)
                pe.wait_ge(turn.xTb_ready, b * KC + KC)
                pe.wait_ge(logits_kept, b + 1)
                for r in range(RC):
                    for kc in range(KC):
                        i = pe.matmul(g.bank[:, 4 + r, :], w1[:, kc, r * P:r * P + P], turn.xTb[:, kc, :],
                                      start=(kc == 0), stop=(kc == KC - 1))
                    i.then_inc(h_ready, 1)
                pe.wait_ge(rh_ready, b * RC + RC)
                for t in range(TC):
                    for r in range(RC):
                        i = pe.matmul(g.bank[:, 2, t * E:t * E + E], rh[:, r, t * P:t * P + P], w2[:, r, :],
                                      start=(r == 0), stop=(r == RC - 1))
                i.then_inc(logits_ready, 1)
            slots.count(g, pe)

        @block.vector
        def _(dve):
            dve.sem_inc(logits_kept, 1)
            dve.wait_ge(w_loaded, 64)
            with dve.Fori(0, B) as b:
                turn.copy(g, dve, b)
                dve.wait_ge(logits_ready, b + 1)
                dve.tensor_tensor(logits[:, ds(b * TC, TC), :], g.bank[:, 2, 0:TC * E].rearrange("p (t e) -> p t e", e=E),
                                  b2row[:, None, :].to_broadcast([P, TC, E]), ALU.add).then_inc(logits_kept, 1)
            dve.wait_ge(logits_kept, B + 1)
            dve.tensor_reduce(mx[:, :], logits[:, :, :], AX.X, ALU.max).then_inc(step_ready, 1)
            dve.wait_ge(step_ready, 1)
            dve.tensor_tensor(sub[:, :, :], logits[:, :, :], mx[:, :, None].to_broadcast([P, NT, E]), ALU.subtract).then_inc(step_ready, 1)
            dve.wait_ge(exp_ready, 1)
            dve.tensor_reduce(sums[:, :], ex[:, :, :], AX.X, ALU.add).then_inc(step_ready, 1)
            dve.wait_ge(step_ready, 3)
            dve.reciprocal(rsum[:, :], sums[:, :]).then_inc(step_ready, 1)
            dve.wait_ge(step_ready, 4)
            dve.wait_ge(padded, 1)
            dve.tensor_tensor(top.score[:, :, 0:E], ex[:, :, :], rsum[:, :, None].to_broadcast([P, NT, E]), ALU.mult).then_inc(step_ready, 1)
            dve.wait_ge(step_ready, 5)
            top.find(dve)
            for k in range(2):
                dve.tensor_copy(routing.weight[:, k, :, :], top.top[:, :, k:k + 1]).then_inc(step_ready, 1)
            dve.wait_ge(step_ready, 7)
            slots.assign(g, dve, top)


def experts(nc, g, name, E, routing, w1, b1, w2, b2, gamma=None, beta=None, eps=None):
    X, bank = g.X, g.bank
    NB = routing.blocks
    normed = gamma is not None
    rows = 3 if normed else 1
    loads = 3 + rows
    row_slots = g.x_slots[0:NB * BLOCK, :].rearrange("(t p) d -> p t d", p=P)
    result_slots = g.y_slots[0:NB * BLOCK, :].rearrange("(t p) d -> p t d", p=P)
    with ExitStack() as c:
        def sb(n, shape, dt=F32):
            return c.enter_context(nc.sbuf_tensor(f"{name}_{n}", shape, dt))

        def sem(n):
            return nc.alloc_semaphore(f"{name}_{n}")

        w1s = sb("w1s", [P, 2, KC, FF])
        w2s = sb("w2s", [P, 2, FC, D])
        b1s = sb("b1s", [P, 2, FC])
        row = sb("row", [P, 2, rows, D])
        xs = sb("xs", [P, 2, BC, D])
        xT = sb("xT", [P, 2, KC, BLOCK])
        hT = sb("hT", [P, FC, BLOCK])
        xb = sb("xb", [P, BC, D])
        r, z = sb("r", [P, BC, D]), sb("z", [P, BC, D])
        o = sb("o", [P, 2, BC, D])
        st, mv = sb("st", [P, BC, 6]), sb("mv", [P, BC, 2])
        ve, rstd = sb("ve", [P, BC]), sb("rstd", [P, BC])
        fetched = sb("fetched", [P, NT, 2, D])
        first = sb("first", [P, TC, D])
        wb = sb("wb", [P, 2, TC])
        ln = Norm(nc, c, name + "_ln")

        sent = sem("sent")
        x_loaded = [sem("x_loaded_even"), sem("x_loaded_odd")]
        loaded = [sem("loaded_even"), sem("loaded_odd")]
        free = [sem("free_even"), sem("free_odd")]
        stored = [sem("stored_even"), sem("stored_odd")]
        turned, xT_ready = sem("turned"), sem("xT_ready")
        h_ready, hT_ready = sem("h_ready"), sem("hT_ready")
        out_ready, out_taken = sem("out_ready"), sem("out_taken")
        xb_ready, st_ready, mv_ready = sem("xb_ready"), sem("st_ready"), sem("mv_ready")
        ve_ready, rstd_ready, z_ready, o_ready = sem("ve_ready"), sem("rstd_ready"), sem("z_ready"), sem("o_ready")
        results_fetched = [sem(f"results_fetched_{b}") for b in range(B)]
        batch_fetched, wb_ready, first_ready = sem("batch_fetched"), sem("wb_ready"), sem("first_ready")
        block = c.enter_context(nc.Block())

        def each_block(engine, body):
            assert NB % 2 == 1
            with engine.Fori(0, NB // 2) as pair:
                body(pair, 0, False)
                body(pair, 1, False)
            body(NB // 2, 0, True)

        def at(pair, u, per_block, extra):
            return pair * (2 * per_block) + (u * per_block + extra)

        @block.sync
        def _(sp):
            sp.wait_ge(sent, 16 * 2 * NT)

            def store(pair, u):
                sp.wait_ge(o_ready, at(pair, u, BC, BC))
                sp.dma_start(result_slots[:, ds(pair * (2 * BC) + u * BC, BC), :], o[:, u, :, :]).then_inc(stored[u], 16)

            def load(pair, u):
                sp.wait_ge(free[u], pair * 2 + 2)
                sp.dma_start(xs[:, u, :, :], row_slots[:, ds(pair * (2 * BC) + u * BC, BC), :]).then_inc(x_loaded[u], 16)
                e = sp.value_load(routing.block_expert[0:1, ds(pair * 2 + u, 1)], min_val=0, max_val=E - 1)
                sp.dma_start(w1s[:, u, :, :], w1[ds(e, 1)].rearrange("o (k p) n -> p (o k) n", p=P)).then_inc(loaded[u], 16)
                sp.dma_start(b1s[:, u, :], b1[:, ds(e, 1), :].rearrange("p o f -> p (o f)")).then_inc(loaded[u], 16)
                sp.dma_start(w2s[:, u, :, :], w2[ds(e, 1)].rearrange("o (k p) n -> p (o k) n", p=P)).then_inc(loaded[u], 16)
                for n, v in enumerate((b2, gamma, beta)[0:rows]):
                    sp.dma_start(row[:, u, n, :], v[ds(e, 1)].rearrange("o d -> (o d)").partition_broadcast(P)).then_inc(loaded[u], 16)

            load(0, 0)
            load(0, 1)
            with sp.Fori(1, NB // 2) as pair:
                for u in range(2):
                    load(pair, u)
                    store(pair - 1, u)
            load(NB // 2, 0)
            for u in range(2):
                store(NB // 2 - 1, u)
            store(NB // 2, 0)
            for u in range(2):
                sp.wait_ge(loaded[u], 16 * loads * (NB // 2 + 1 - u))

        @block.scalar
        def _(act):
            def take_xT(pair, u):
                act.wait_ge(turned, at(pair, u, 1, 1))
                act.activation(xT[:, u, :, :].rearrange("p k n -> p (k n)"), bank[:, 2 + u, :], ACT.Copy).then_inc(xT_ready, 1)

            take_xT(0, 0)

            def body(pair, u, last):
                act.wait_ge(loaded[u], pair * (16 * loads) + 16 * loads)
                for f in range(FC):
                    act.wait_ge(h_ready, at(pair, u, FC, f + 1))
                    act.activation(hT[:, f, :], bank[:, f % 2, 0:BLOCK], ACT.Gelu, bias=b1s[:, u, f:f + 1]).then_inc(hT_ready, 1)
                if not last:
                    take_xT(pair + u, 1 - u)

            each_block(act, body)

        @block.tensor
        def _(pe):
            def turn(pair, u):
                pe.wait_ge(x_loaded[u], pair * 16 + 16)
                for kc in range(KC):
                    for t in range(BC):
                        i = pe.transpose(bank[:, 2 + u, kc * BLOCK + t * P:kc * BLOCK + t * P + P],
                                         xs[:, u, t, kc * P:kc * P + P], g.ident[:, :])
                i.then_inc(turned, 1)

            turn(0, 0)

            def body(pair, u, last):
                pe.wait_ge(loaded[u], pair * (16 * loads) + 16 * loads)
                pe.wait_ge(xT_ready, at(pair, u, 1, 1))
                for f in range(FC):
                    pe.wait_ge(hT_ready, at(pair, u, FC, f + 1))
                    for kc in range(KC):
                        i = pe.matmul(bank[:, f % 2, 0:BLOCK], w1s[:, u, kc, f * P:f * P + P], xT[:, u, kc, :],
                                      start=(kc == 0), stop=(kc == KC - 1))
                    i.then_inc(h_ready, 1)
                if not last:
                    turn(pair + u, 1 - u)
                pe.wait_ge(out_taken, at(pair, u, BC, BC))
                for f in range(FC):
                    pe.wait_ge(hT_ready, at(pair, u, FC, f + 3))
                    for t in range(BC):
                        i = pe.matmul(bank[:, 4 + 2 * u + t, 0:D], hT[:, f, t * P:t * P + P], w2s[:, u, f, :],
                                      start=(f == 0), stop=(f == FC - 1))
                        if f == FC - 1:
                            i.then_inc(out_ready, 1)
                pe.sem_inc(free[u], 1)

            each_block(pe, body)

        @block.gpsimd
        def _(pool):
            pool.wait_ge(g.slots_zeroed, 16)
            for n in range(NT):
                for k in range(2):
                    pool.indirect_dma_start(g.x_slots[0:NB * BLOCK, :], bass.IndirectOffsetOnAxis(ap=routing.slot[:, k, n:n + 1], axis=0),
                                            X[:, n, :], None).then_inc(sent, 16)
            pool.wait_ge(sent, 16 * 2 * NT)

            def body(pair, u, last):
                pool.wait_ge(loaded[u], pair * (16 * loads) + 16 * loads)
                pool.wait_ge(x_loaded[u], pair * 16 + 16)
                pool.wait_ge(out_taken, at(pair, u, BC, 2 * BC))
                for t in range(BC):
                    pool.tensor_tensor(xb[:, t, :], xs[:, u, t, :], row[:, u, 0, :], ALU.add).then_inc(xb_ready, 1)
                pool.wait_ge(mv_ready, at(pair, u, BC, BC))
                g.after_wait(pool)
                pool.tensor_scalar(ve[:, :], mv[:, :, 1], eps, 0.0, ALU.add, ALU.add).then_inc(ve_ready, 1)
                pool.wait_ge(ve_ready, at(pair, u, 1, 1))
                pool.tensor_tensor(rstd[:, :], ve[:, :], g.neg_half[:, 0:BC], ALU.pow).then_inc(rstd_ready, 1)

            if normed:
                each_block(pool, body)
            for u in range(2):
                pool.wait_ge(stored[u], 16 + 16 * (NB // 2 + 1 - u))
            for b in range(B):
                for t in range(TC):
                    for k in range(2):
                        n = b * TC + t
                        pool.indirect_dma_start(fetched[:, n, k, :], None, g.y_slots[0:NB * BLOCK, :],
                                                bass.IndirectOffsetOnAxis(ap=routing.slot[:, k, n:n + 1], axis=0)).then_inc(results_fetched[b], 16)
                if b >= 1:
                    pool.wait_ge(results_fetched[b - 1], 16 * 2 * TC)
                    pool.sem_inc(batch_fetched, 1)
                    ln.rstd(g, pool, b - 1)
            pool.wait_ge(results_fetched[B - 1], 16 * 2 * TC)
            pool.sem_inc(batch_fetched, 1)
            ln.rstd(g, pool, B - 1)

        @block.vector
        def _(dve):
            dve.sem_inc(out_taken, 2 * BC)
            dve.sem_inc(hT_ready, 2)
            for u in range(2):
                dve.sem_inc(free[u], 2)
                dve.sem_inc(stored[u], 16)

            def body(pair, u, last):
                dve.wait_ge(loaded[u], pair * (16 * loads) + 16 * loads)
                if not normed:
                    dve.wait_ge(stored[u], pair * 16 + 16)
                for t in range(BC):
                    dve.wait_ge(out_ready, at(pair, u, BC, t + 1))
                    if normed:
                        dve.wait_ge(xb_ready, at(pair, u, BC, t + 1))
                        dve.tensor_tensor(r[:, t, :], bank[:, 4 + 2 * u + t, 0:D], xb[:, t, :], ALU.add).then_inc(out_taken, 1)
                    else:
                        dve.tensor_tensor(o[:, u, t, :], bank[:, 4 + 2 * u + t, 0:D], row[:, u, 0, :], ALU.add).then_inc(o_ready, 1)
                if not normed:
                    dve.wait_ge(o_ready, at(pair, u, BC, BC))
                    dve.sem_inc(out_taken, BC)
                else:
                    for t in range(BC):
                        dve.wait_ge(out_taken, at(pair, u, BC, 2 * BC + t + 1))
                        dve.bn_stats(st[:, t, :], r[:, t, :]).then_inc(st_ready, 1)
                    for t in range(BC):
                        dve.wait_ge(st_ready, at(pair, u, BC, t + 1))
                        g.after_wait(dve)
                        dve.bn_aggr(mv[:, t, :], st[:, t, :]).then_inc(mv_ready, 1)
                    for t in range(BC):
                        dve.wait_ge(mv_ready, at(pair, u, BC, t + 1))
                        dve.scalar_tensor_tensor(out=z[:, t, :], in0=r[:, t, :], scalar=mv[:, t, 0:1], in1=row[:, u, 1, :],
                                                 op0=ALU.subtract, op1=ALU.mult).then_inc(z_ready, 1)
                    dve.wait_ge(rstd_ready, at(pair, u, 1, 1))
                    dve.wait_ge(stored[u], pair * 16 + 16)
                    for t in range(BC):
                        dve.wait_ge(z_ready, at(pair, u, BC, t + 1))
                        dve.scalar_tensor_tensor(out=o[:, u, t, :], in0=z[:, t, :], scalar=rstd[:, t:t + 1], in1=row[:, u, 2, :],
                                                 op0=ALU.mult, op1=ALU.add).then_inc(o_ready, 1)
                    dve.wait_ge(o_ready, at(pair, u, BC, BC))
                dve.sem_inc(free[u], 1)

            each_block(dve, body)
            with dve.Fori(0, B) as b:
                dve.tensor_copy(wb[:, :, :], routing.weight[:, :, ds(b * TC, TC), 0]).then_inc(wb_ready, 1)
                dve.wait_ge(wb_ready, b + 1)
                dve.wait_ge(batch_fetched, b + 1)
                for t in range(TC):
                    dve.scalar_tensor_tensor(out=first[:, t, :], in0=fetched[:, b * TC + t, 0, :], scalar=wb[:, 0, t:t + 1],
                                             in1=X[:, b * TC + t, :], op0=ALU.mult, op1=ALU.add).then_inc(first_ready, 1)
                for t in range(TC):
                    dve.wait_ge(first_ready, b * TC + t + 1)
                    dve.scalar_tensor_tensor(out=ln.t[:, t, :], in0=fetched[:, b * TC + t, 1, :], scalar=wb[:, 1, t:t + 1],
                                             in1=first[:, t, :], op0=ALU.mult, op1=ALU.add).then_inc(ln.sum_ready, 1)
                ln.stats(g, dve, b)
                ln.apply(dve, lambda t: X[:, b * TC + t, :], b)
                dve.wait_ge(ln.x_ready, b * TC + TC)


def l0_ffn(nc, g, router_w, w1, b1, w2, b2, gamma, beta):
    with ExitStack() as c:
        routing = Routing(nc, c, "m0", 8)
        l0_router(nc, g, routing, router_w)
        experts(nc, g, "e0", 8, routing, w1, b1, w2, b2, gamma, beta, 1e-6)


def l1_ffn(nc, g, rw1, rb1, rw2, rb2, w1, b1, w2, b2):
    with ExitStack() as c:
        routing = Routing(nc, c, "m1", 4)
        l1_router(nc, g, routing, rw1, rb1, rw2, rb2)
        experts(nc, g, "e1", 4, routing, w1, b1, w2, b2)

def l1_attention(nc, g, w_qkv_t, w_c_t, mix2, index_decays_t2, mega_decays):
    H, DH, SEG = 16, 16, 64
    NR = L // SEG
    HQ = H // 4
    NG = HQ * TC
    NOISE_EPS = 1e-5
    MASKED = -1e30
    X, ident, bank = g.X, g.ident, g.bank
    with ExitStack() as c:
        def sb(name, shape, dt=F32):
            return c.enter_context(nc.sbuf_tensor("t1_" + name, shape, dt))

        def sem(name):
            return nc.alloc_semaphore("t1_" + name)

        w_qkv = sb("w_qkv", [P, KC, 3 * D])
        w_c = sb("w_c", [P, KC, D])
        ident_b = sb("ident_b", [P, P], BF16)
        mask = sb("mask", [P, 2 * P], BF16)
        in_half = sb("in_half", [P, 2])
        mix = sb("mix", [P, 4])
        dec, dec_e = sb("dec", [P, H]), sb("dec_e", [P, H])
        mega = sb("mega", [P, H])
        pw = sb("pw", [P, H, NR])
        RC = sb("RC", [P, TC, H, NR])
        xs = sb("xs", [P, TC, D])
        xT = sb("xT", [P, KC, L])
        raw = sb("raw", [P, TC, 3 * D])
        q4 = sb("q4", [P, 2, H, 4, DH], F32R)
        k4 = sb("k4", [P, 2, H, 4, DH], F32R)
        qm = sb("qm", [P, 2, H, 2, DH])
        QT = sb("QT", [P, H // 2, L], F32R)
        KZ = sb("KZ", [P, H // 2, 2, L], F32R)
        QMT = sb("QMT", [P, TC, HQ, P])
        E = sb("E", [P, 2, 4, L])
        Et = sb("Et", [P, 2, 4, 2 * P])
        EtT = sb("EtT", [P, 2, 4, 2, P])
        nmax, nmax_t = sb("nmax", [P, 2, 4]), sb("nmax_t", [P, 2, 4])
        sums, rsum = sb("sums", [P, 2, 4]), sb("rsum", [P, 2, 4])
        sums_t, rsum_t, ct = sb("sums_t", [P, HQ, TC, 4]), sb("rsum_t", [P, TC, 4]), sb("ct", [P, TC, 4])
        R = sb("R", [P, 2, 4, 32])
        wn = sb("wn", [P, HQ, L])
        wsum, wse, rws = sb("wsum", [P, HQ]), sb("wse", [P, HQ]), sb("rws", [P, HQ])
        wm = wn
        wT = sb("wT", [P, HQ, TC, 4, NR])
        A = sb("A", [P, 2, TC, 4, NR, DH])
        BD = sb("BD", [P, TC, HQ, 4, DH])
        y = sb("y", [P, TC, D])
        y2 = sb("y2", [P, 2, D])
        yT = sb("yT", [P, KC, L])
        ln = Norm(nc, c, "t1_ln")

        w_loaded, small_loaded, zeroed = sem("w_loaded"), sem("small_loaded"), sem("zeroed")
        mask_step, mask_ready = sem("mask_step"), sem("mask_ready")
        half_ready, kz_zeroed = sem("half_ready"), sem("kz_zeroed")
        c_exp, c_step, c_ready = sem("c_exp"), sem("c_step"), sem("c_ready")
        xs_ready, xtp_ready, xT_ready = sem("xs_ready"), sem("xtp_ready"), sem("xT_ready")
        proj_ready, raw_ready = sem("proj_ready"), sem("raw_ready")
        hi_ready, lo_ready, qm_ready = sem("hi_ready"), sem("lo_ready"), sem("qm_ready")
        turn_ready = sem("turn_ready")
        kept_act, kept_dve = sem("kept_act"), sem("kept_dve")
        s_ready, st_ready = sem("s_ready"), sem("st_ready")
        nmax_ready, nmax_t_ready = sem("nmax_ready"), sem("nmax_t_ready")
        e_ready, et_ready = sem("e_ready"), sem("et_ready")
        rsum_ready, R_ready = sem("rsum_ready"), sem("R_ready")
        ett_ready, EtT_ready = sem("ett_ready"), sem("EtT_ready")
        wacc_ready, av_ready = sem("wacc_ready"), sem("av_ready")
        rt_ready, ct_ready, yt_ready = sem("rt_ready"), sem("ct_ready"), sem("yt_ready")
        wn_ready, wse_ready, rws_ready, wm_ready = sem("wn_ready"), sem("wse_ready"), sem("rws_ready"), sem("wm_ready")
        wt_ready, wT_ready, A_ready = sem("wt_ready"), sem("wT_ready"), sem("A_ready")
        kv_ready, BD_ready = sem("kv_ready"), sem("BD_ready")
        lin_ready, y_ready = sem("lin_ready"), sem("y_ready")
        yt2_ready, yT_ready, out_ready = sem("yt2_ready"), sem("yT_ready"), sem("out_ready")

        block = c.enter_context(nc.Block())

        def kept(n):
            t, j = divmod(n, 5)
            if j in (2, 3):
                return kept_dve, 4 * TC, 4 * t + 2 * (j - 1)
            return kept_act, 3 * TC, 3 * t + (j + 1 if j < 2 else 3)

        def chunk(n):
            return n % TC

        @block.sync
        def _(sp):
            sp.dma_start(w_qkv[:, :, :], w_qkv_t.rearrange("(k p) n -> p k n", p=P)).then_inc(w_loaded, 16)
            sp.dma_start(w_c[:, :, :], w_c_t.rearrange("(k p) n -> p k n", p=P)).then_inc(w_loaded, 16)
            sp.wait_ge(w_loaded, 32)

        @block.gpsimd
        def _(pool):
            pool.wait_ge(mask_step, 5)
            pool.affine_select(out=mask[:, P:2 * P], in_=mask[:, P:2 * P], compare_op=ALU.is_ge, fill=MASKED,
                               base=0, pattern=[[-1, P]], channel_multiplier=1).then_inc(mask_ready, 1)
            pool.affine_select(out=ident_b[:, :], in_=ident_b[:, :], compare_op=ALU.not_equal, fill=1.0,
                               base=0, pattern=[[-1, P]], channel_multiplier=1).then_inc(mask_ready, 1)
            pool.memset(R[:, :, :, NR:32], 0.0).then_inc(zeroed, 1)
            pool.memset(BD[:, :, :, :, :], 0.0).then_inc(zeroed, 1)
            pool.memset(RC[:, :, :, :], 0.0).then_inc(zeroed, 1)
            pool.wait_ge(half_ready, 4)
            with pool.Fori(0, B) as b:
                for t in range(TC):
                    pool.wait_ge(raw_ready, b * 2 * TC + 2 * t + 1)
                    if t >= 2:
                        pool.wait_ge(turn_ready, b * 5 * TC + 5 * (t - 1))
                    g.after_wait(pool)
                    for half in range(2):
                        pool.tensor_scalar(qm[:, t % 2, :, half, :], raw[:, t, 0:D].rearrange("p (h d) -> p h d", d=DH),
                                           in_half[:, half:half + 1], 1.0, ALU.mult, ALU.mult).then_inc(qm_ready, 1)
                for hq in range(HQ):
                    pool.wait_ge(wT_ready, b * HQ + hq + 1)
                    if hq >= 2:
                        pool.wait_ge(kv_ready, b * HQ + hq - 1)
                    for m in range(TC):
                        k = raw[:, m, D + 64 * hq:D + 64 * hq + 64].rearrange("p (h d) -> p h d", d=DH)
                        pool.tensor_tensor(A[:, hq % 2, m, :, :, :], k[:, :, None, :].to_broadcast([P, 4, NR, DH]),
                                           wT[:, hq, m, :, :, None].to_broadcast([P, 4, NR, DH]), ALU.mult).then_inc(A_ready, 1)
                ln.rstd(g, pool, b)

        @block.scalar
        def _(act):
            for half in range(2):
                rows = slice(64 * half, 64 * half + 64)
                act.dma_start(mix[rows, 0:1], mix2).then_inc(small_loaded, 16)
                act.dma_start(dec[rows, :], index_decays_t2).then_inc(small_loaded, 16)
            act.dma_start(mega[:, :], mega_decays.partition_broadcast(P)).then_inc(small_loaded, 16)
            act.wait_ge(small_loaded, 80)
            act.activation(mix[:, 1:2], mix[:, 0:1], ACT.Exp, scale=-1.0).then_inc(c_exp, 1)
            act.activation(dec_e[:, :], dec[:, :], ACT.Exp).then_inc(c_exp, 1)
            act.activation(pw[:, :, 1], mega[:, :], ACT.Exp, scale=float(SEG)).then_inc(c_exp, 1)
            with act.Fori(0, B) as b:
                for kc in range(KC):
                    act.wait_ge(xtp_ready, b * KC + kc + 1)
                    act.activation(xT[:, kc, :], bank[:, 6 + kc, :], ACT.Copy).then_inc(xT_ready, 1)

                def keep_raw(t):
                    act.wait_ge(proj_ready, b * TC + t + 1)
                    act.activation(raw[:, t, 0:2 * D], bank[:, 2 * (t % 2), :], ACT.Copy).then_inc(raw_ready, 1)
                    act.activation(raw[:, t, 2 * D:3 * D], bank[:, 2 * (t % 2) + 1, 0:D], ACT.Copy).then_inc(raw_ready, 1)

                def keep_turned(t):
                    for j in (0, 1, 4):
                        n = 5 * t + j
                        act.wait_ge(turn_ready, b * 5 * TC + n + 1)
                        src = bank[:, 4 + n % 4, :].rearrange("p (a n) -> p a n", a=4)
                        if j < 2:
                            act.activation(QT[:, 4 * j:4 * j + 4, t * P:t * P + P], src, ACT.Copy).then_inc(kept_act, 1)
                        else:
                            act.activation(QMT[:, t, :, :], src, ACT.Copy).then_inc(kept_act, 1)

                keep_raw(0)
                keep_raw(1)
                for t in range(TC):
                    keep_turned(t)
                    if t + 2 < TC:
                        keep_raw(t + 2)

                for n in range(NG):
                    i, hq = chunk(n), n // TC
                    keys = (i + 1) * P
                    window = min(keys, 2 * P)
                    for pair in range(2):
                        for h in (2 * pair, 2 * pair + 1):
                            u = 4 * n + h
                            if h == 0 and n >= 2:
                                act.wait_ge(wacc_ready, b * NG + n - 1)
                                act.wait_ge(R_ready, b * NG + n - 1)
                            act.wait_ge(nmax_ready, b * 4 * NG + u + 1)
                            act.activation(E[:, n % 2, h, 0:keys], bank[:, u % 2, 0:keys], ACT.Exp,
                                           bias=nmax[:, n % 2, h:h + 1], accum_out=sums[:, n % 2, h:h + 1]).then_inc(e_ready, 1)
                        for h in (2 * pair, 2 * pair + 1):
                            if h == 0 and n >= 2:
                                act.wait_ge(ett_ready, b * 2 * NG + 2 * (n - 1))
                            act.wait_ge(nmax_t_ready, b * 2 * NG + 2 * n + pair + 1)
                            act.activation(Et[:, n % 2, h, 0:window], bank[:, 2 + pair, 256 * (h % 2):256 * (h % 2) + window],
                                           ACT.Exp, bias=nmax_t[:, n % 2, h:h + 1],
                                           accum_out=sums_t[:, hq, i, h:h + 1]).then_inc(et_ready, 1)
                    if n % TC == 1 and hq >= 1:
                        act.wait_ge(wacc_ready, b * NG + TC * hq)
                        act.activation(wn[:, hq - 1, :], bank[:, 7, :], ACT.Copy, accum_out=wsum[:, hq - 1:hq]).then_inc(wn_ready, 1)
                act.wait_ge(wacc_ready, b * NG + NG)
                act.activation(wn[:, HQ - 1, :], bank[:, 7, :], ACT.Copy, accum_out=wsum[:, HQ - 1:HQ]).then_inc(wn_ready, 1)
                for hq in range(HQ):
                    act.wait_ge(wt_ready, b * HQ + hq + 1)
                    src = bank[:, 4 + hq % 2, :].rearrange("p (m h r) -> p m h r", m=TC, h=4)[:, :, :, 0:NR]
                    act.activation(wT[:, hq, :, :, :], src, ACT.Copy).then_inc(wT_ready, 1)
                for t in range(TC):
                    act.wait_ge(yt2_ready, b * TC + t + 1)
                    act.activation(yT[:, :, t * P:t * P + P], bank[:, 6 + t % 2, 0:2 * P].rearrange("p (k n) -> p k n", k=KC),
                                   ACT.Copy).then_inc(yT_ready, 1)

        @block.vector
        def _(dve):
            dve.memset(mask[:, P:2 * P], 0.0).then_inc(mask_step, 1)
            dve.memset(mask[:, 0:SEG], MASKED).then_inc(mask_step, 1)
            dve.memset(mask[0:SEG, SEG:P], 0.0).then_inc(mask_step, 1)
            dve.memset(mask[SEG:P, SEG:P], MASKED).then_inc(mask_step, 1)
            dve.memset(ident_b[:, :], 0.0).then_inc(mask_step, 1)
            for half in range(2):
                rows = slice(64 * half, 64 * half + 64)
                dve.memset(in_half[rows, half:half + 1], 1.0).then_inc(half_ready, 1)
                dve.memset(in_half[rows, 1 - half:2 - half], 0.0).then_inc(half_ready, 1)
                dve.memset(KZ[rows, :, 1 - half, :].bitcast(F32), 0.0).then_inc(kz_zeroed, 1)
            dve.wait_ge(c_exp, 3)
            dve.tensor_scalar(mix[:, 3:4], mix[:, 1:2], 1.0, None, ALU.add).then_inc(c_step, 1)
            dve.tensor_scalar(pw[:, :, 1], pw[:, :, 1], 0.0, 2.0, ALU.max, ALU.min).then_inc(c_step, 1)
            dve.memset(pw[:, :, 0], 1.0).then_inc(c_step, 1)
            dve.wait_ge(c_step, 3)
            dve.reciprocal(mix[:, 2:3], mix[:, 3:4]).then_inc(c_step, 1)
            dve.wait_ge(c_step, 4)
            dve.tensor_scalar(mix[:, 3:4], mix[:, 2:3], -1.0, 1.0, ALU.mult, ALU.add).then_inc(c_step, 1)
            for k in range(2, NR):
                dve.tensor_tensor(pw[:, :, k], pw[:, :, k - 1], pw[:, :, 1], ALU.mult).then_inc(c_step, 1)
                dve.wait_ge(c_step, 4 + k)
            dve.wait_ge(zeroed, 3)
            for r in range(NR - 1):
                i, half = divmod(r, 2)
                rows = slice(64 * half, 64 * half + 64)
                dve.tensor_tensor(RC[rows, i, :, r + 1:NR], pw[rows, :, 0:NR - 1 - r],
                                  dec_e[rows, :, None].to_broadcast([64, H, NR - 1 - r]), ALU.mult).then_inc(c_ready, 1)
            dve.wait_ge(c_ready, NR - 1)
            dve.sem_inc(ln.banks_free, TC)
            with dve.Fori(0, B) as b:
                dve.tensor_copy(xs[:, :, :], X[:, ds(b * TC, TC), :]).then_inc(xs_ready, 1)

                def split(t):
                    dve.wait_ge(raw_ready, b * 2 * TC + 2 * t + 1)
                    if t >= 2:
                        dve.wait_ge(turn_ready, b * 5 * TC + 5 * (t - 1))
                    q = raw[:, t, 0:D].rearrange("p (h d) -> p h d", d=DH)
                    k = raw[:, t, D:2 * D].rearrange("p (h d) -> p h d", d=DH)
                    s = t % 2
                    for j in range(2):
                        dve.tensor_scalar(q4[:, s, :, 2 * j, :], q, 0.25, None, ALU.mult).then_inc(hi_ready, 1)
                        dve.tensor_copy(k4[:, s, :, j, :], k).then_inc(hi_ready, 1)
                    dve.wait_ge(hi_ready, b * 4 * TC + 4 * t + 4)
                    for j in range(2):
                        dve.scalar_tensor_tensor(out=q4[:, s, :, 2 * j + 1, :], in0=q, scalar=0.25,
                                                 in1=q4[:, s, :, 0, :].bitcast(F32), op0=ALU.mult, op1=ALU.subtract).then_inc(lo_ready, 1)
                        dve.tensor_tensor(k4[:, s, :, 2 + j, :], k, k4[:, s, :, 0, :].bitcast(F32), ALU.subtract).then_inc(lo_ready, 1)

                def keep_turned(t):
                    for j in (2, 3):
                        n = 5 * t + j
                        dve.wait_ge(turn_ready, b * 5 * TC + n + 1)
                        for half in range(2):
                            rows = slice(64 * half, 64 * half + 64)
                            src = bank[rows, 4 + n % 4, :].rearrange("p (a n) -> p a n", a=4)
                            dve.tensor_copy(KZ[rows, 4 * (j - 2):4 * (j - 2) + 4, half, t * P:t * P + P], src).then_inc(kept_dve, 1)

                split(0)
                for t in range(TC):
                    if t + 1 < TC:
                        split(t + 1)
                    keep_turned(t)

                def maxima(n):
                    i = chunk(n)
                    keys = (i + 1) * P
                    window = min(keys, 2 * P)
                    for pair in range(2):
                        for h in (2 * pair, 2 * pair + 1):
                            u = 4 * n + h
                            if h == 0 and n >= 2:
                                dve.wait_ge(e_ready, b * 4 * NG + 4 * (n - 1))
                                dve.wait_ge(et_ready, b * 4 * NG + 4 * (n - 1))
                            dve.wait_ge(s_ready, b * 4 * NG + u + 1)
                            dve.tensor_reduce(nmax[:, n % 2, h:h + 1], bank[:, u % 2, 0:keys], AX.X, ALU.max,
                                              negate=True).then_inc(nmax_ready, 1)
                        dve.wait_ge(st_ready, b * 2 * NG + 2 * n + pair + 1)
                        src = bank[:, 2 + pair, :].rearrange("p (h n) -> p h n", h=2)[:, :, 0:window]
                        dve.tensor_reduce(nmax_t[:, n % 2, 2 * pair:2 * pair + 2], src, AX.X, ALU.max,
                                          negate=True).then_inc(nmax_t_ready, 1)

                def scales(n):
                    i, hq = chunk(n), n // TC
                    dve.wait_ge(e_ready, b * 4 * NG + 4 * n + 4)
                    dve.reciprocal(rsum[:, n % 2, :], sums[:, n % 2, :]).then_inc(rsum_ready, 1)
                    dve.wait_ge(rsum_ready, b * NG + n + 1)
                    if n >= 2:
                        dve.wait_ge(wacc_ready, b * NG + n - 1)
                    dve.tensor_tensor(R[:, n % 2, :, 0:NR], RC[:, i, 4 * hq:4 * hq + 4, :],
                                      rsum[:, n % 2, :, None].to_broadcast([P, 4, NR]), ALU.mult).then_inc(R_ready, 1)

                def keep_EtT(n):
                    w = 1 if chunk(n) == 0 else 2
                    for pair in range(2):
                        if n >= 2 and pair == 0:
                            dve.wait_ge(av_ready, b * NG + n - 1)
                        dve.wait_ge(ett_ready, b * 2 * NG + 2 * n + pair + 1)
                        src = bank[:, 4 + pair, :].rearrange("p (h w n) -> p h w n", h=2, w=2)[:, :, 0:w, :]
                        dve.tensor_copy(EtT[:, n % 2, 2 * pair:2 * pair + 2, 0:w, :], src).then_inc(EtT_ready, 1)

                def keep_terrace(hq):
                    dve.wait_ge(et_ready, b * 4 * NG + 16 * (hq + 1))
                    if hq >= 1:
                        dve.wait_ge(yt_ready, b * HQ + hq)
                    dve.reciprocal(rsum_t[:, :, :], sums_t[:, hq, :, :]).then_inc(rt_ready, 1)
                    dve.wait_ge(rt_ready, b * HQ + hq + 1)
                    dve.tensor_scalar(ct[:, :, :], rsum_t[:, :, :], mix[:, 2:3], None, ALU.mult).then_inc(ct_ready, 1)
                    dve.wait_ge(ct_ready, b * HQ + hq + 1)
                    dve.wait_ge(av_ready, b * NG + TC * (hq + 1))
                    src = bank[:, 6, 0:4 * 64].rearrange("p (i h d) -> p i h d", i=TC, h=4)
                    dve.tensor_tensor(y[:, :, 64 * hq:64 * hq + 64].rearrange("p i (h d) -> p i h d", h=4), src,
                                      ct[:, :, :, None].to_broadcast([P, TC, 4, DH]), ALU.mult).then_inc(yt_ready, 1)

                for n in range(NG):
                    maxima(n)
                    if n >= 1:
                        scales(n - 1)
                        keep_EtT(n - 1)
                    if n % TC == 0 and n >= TC:
                        keep_terrace(n // TC - 1)
                scales(NG - 1)
                keep_EtT(NG - 1)
                keep_terrace(HQ - 1)
                dve.wait_ge(wn_ready, b * HQ + HQ)
                dve.tensor_scalar(wse[:, :], wsum[:, :], NOISE_EPS, None, ALU.add).then_inc(wse_ready, 1)
                dve.wait_ge(wse_ready, b + 1)
                dve.reciprocal(rws[:, :], wse[:, :]).then_inc(rws_ready, 1)
                dve.wait_ge(rws_ready, b + 1)
                for hq in range(HQ):
                    dve.tensor_scalar(wm[:, hq, :], wn[:, hq, :], rws[:, hq:hq + 1], None, ALU.mult).then_inc(wm_ready, 1)
                dve.wait_ge(kv_ready, b * HQ + HQ)
                for i in range(TC):
                    for h in range(4):
                        src = bank[32 * i:32 * i + 32, 0, 0:D].rearrange("p (q h d) -> p q h d", q=HQ, h=4)[:, :, h, :]
                        dve.tensor_copy(BD[32 * h:32 * h + 32, i, :, h, :], src).then_inc(BD_ready, 1)
                for t in range(TC):
                    dve.wait_ge(lin_ready, b * TC + t + 1)
                    if t == 0:
                        dve.wait_ge(yt_ready, b * HQ + HQ)
                    if t >= 2:
                        dve.wait_ge(yt2_ready, b * TC + t - 1)
                    dve.scalar_tensor_tensor(out=y2[:, t % 2, :], in0=bank[:, 2 + t % 2, 0:D], scalar=mix[:, 3:4], in1=y[:, t, :],
                                             op0=ALU.mult, op1=ALU.add).then_inc(y_ready, 1)
                for t in range(TC):
                    dve.wait_ge(out_ready, b * TC + t + 1)
                    dve.tensor_tensor(ln.t[:, t, :], bank[:, t, 0:D], xs[:, t, :], ALU.add).then_inc(ln.sum_ready, 1)
                dve.wait_ge(ln.sum_ready, b * TC + TC)
                dve.sem_inc(ln.banks_free, TC)
                ln.stats(g, dve, b)
                ln.apply(dve, lambda t: X[:, b * TC + t, :], b)

        @block.tensor
        def _(pe):
            pe.wait_ge(w_loaded, 32)
            pe.wait_ge(mask_ready, 2)
            pe.wait_ge(zeroed, 3)
            pe.wait_ge(kz_zeroed, 2)
            with pe.Fori(0, B) as b:
                pe.wait_ge(ln.banks_free, b * TC + TC)
                pe.wait_ge(xs_ready, b + 1)
                for kc in range(KC):
                    for t in range(TC):
                        i = pe.transpose(bank[:, 6 + kc, t * P:t * P + P], xs[:, t, kc * P:kc * P + P], ident[:, :])
                    i.then_inc(xtp_ready, 1)
                pe.wait_ge(xT_ready, b * KC + KC)

                def project(t):
                    if t >= 2:
                        pe.wait_ge(raw_ready, b * 2 * TC + 2 * (t - 1))
                    for out, cols in ((bank[:, 2 * (t % 2), :], slice(0, 2 * D)), (bank[:, 2 * (t % 2) + 1, 0:D], slice(2 * D, 3 * D))):
                        for kc in range(KC):
                            i = pe.matmul(out, xT[:, kc, t * P:t * P + P], w_qkv[:, kc, cols], start=(kc == 0), stop=(kc == KC - 1))
                    i.then_inc(proj_ready, 1)

                def turn(t):
                    pe.wait_ge(lo_ready, b * 4 * TC + 4 * t + 4)
                    for j in range(5):
                        n = 5 * t + j
                        if n >= 4:
                            s, per, k = kept(n - 4)
                            pe.wait_ge(s, b * per + k)
                        if j == 4:
                            pe.wait_ge(qm_ready, b * 2 * TC + 2 * t + 2)
                        for a in range(4):
                            if j == 4:
                                src = qm[:, t % 2, 4 * a:4 * a + 4, :, :].rearrange("p h s d -> p (h s d)")
                            else:
                                h = 8 * (j % 2) + 2 * a
                                src = (q4 if j < 2 else k4)[:, t % 2, h:h + 2, :, :].rearrange("p h s d -> p (h s d)").bitcast(F32)
                            i = pe.transpose(bank[:, 4 + n % 4, a * P:a * P + P], src, ident[:, :])
                        i.then_inc(turn_ready, 1)

                project(0)
                project(1)
                for t in range(TC):
                    turn(t)
                    if t + 2 < TC:
                        project(t + 2)
                pe.wait_ge(kept_act, b * 3 * TC + 3 * TC)
                pe.wait_ge(kept_dve, b * 4 * TC + 4 * TC)

                def scores(n):
                    i, hq = chunk(n), n // TC
                    keys = (i + 1) * P
                    window = min(keys, 2 * P)
                    for pair in range(2):
                        for h in (2 * pair, 2 * pair + 1):
                            u, hp = 4 * n + h, 2 * hq + h // 2
                            if u >= 2:
                                pe.wait_ge(e_ready, b * 4 * NG + u - 1)
                            pe.matmul(bank[:, u % 2, keys - P:keys], ident_b[:, :], mask[:, P:2 * P], start=True, stop=False,
                                      skip_group_check=True)
                            pe.matmul(bank[:, u % 2, 0:keys], QT[:, hp, i * P:i * P + P], KZ[:, hp, h % 2, 0:keys], start=False, stop=True,
                                      skip_group_check=True).then_inc(s_ready, 1)
                        if n >= 1:
                            pe.wait_ge(et_ready, b * 4 * NG + 4 * (n - 1) + 2 * pair + 2)
                        for h in (2 * pair, 2 * pair + 1):
                            hp = 2 * hq + h // 2
                            out = bank[:, 2 + pair, 256 * (h % 2):256 * (h % 2) + window]
                            pe.matmul(out, QT[:, hp, i * P:i * P + P], KZ[:, hp, h % 2, keys - window:keys], start=True, stop=False)
                            j = pe.matmul(out, ident_b[:, :], mask[:, 2 * P - window:2 * P], start=False, stop=True)
                        j.then_inc(st_ready, 1)

                def turn_terrace(n):
                    w = 1 if chunk(n) == 0 else 2
                    for pair in range(2):
                        pe.wait_ge(et_ready, b * 4 * NG + 4 * n + 2 * pair + 2)
                        if n >= 1:
                            pe.wait_ge(EtT_ready, b * 2 * NG + 2 * (n - 1) + pair + 1)
                        for h in range(2):
                            for a in range(w):
                                i = pe.transpose(bank[:, 4 + pair, (2 * h + a) * P:(2 * h + a) * P + P],
                                                 Et[:, n % 2, 2 * pair + h, a * P:a * P + P], ident[:, :])
                        i.then_inc(ett_ready, 1)

                def weights(n):
                    i = chunk(n)
                    keys = (i + 1) * P
                    pe.wait_ge(R_ready, b * NG + n + 1)
                    if n % TC == 0 and n >= TC:
                        pe.wait_ge(wn_ready, b * HQ + n // TC)
                    for h in range(4):
                        j = pe.matmul(bank[32 * h:32 * h + 32, 7, 0:keys], R[:, n % 2, h, :], E[:, n % 2, h, 0:keys],
                                      start=(n % TC == 0), stop=(n % TC == TC - 1), skip_group_check=True)
                    j.then_inc(wacc_ready, 1)

                def terrace(n):
                    i, hq = chunk(n), n // TC
                    pe.wait_ge(EtT_ready, b * 2 * NG + 2 * n + 2)
                    if n % TC == 0 and n >= TC:
                        pe.wait_ge(yt_ready, b * HQ + hq)
                    for h in range(4):
                        col = 64 * i + 16 * h
                        v0 = 2 * D + 64 * hq + 16 * h
                        w = 1 if i == 0 else 2
                        for a in range(w):
                            j = pe.matmul(bank[:, 6, col:col + DH], EtT[:, n % 2, h, a, :], raw[:, i - (w - 1) + a, v0:v0 + DH],
                                          start=(a == 0), stop=(a == w - 1))
                    j.then_inc(av_ready, 1)

                for n in range(NG):
                    scores(n)
                    if n >= 1:
                        turn_terrace(n - 1)
                        weights(n - 1)
                        terrace(n - 1)
                turn_terrace(NG - 1)
                weights(NG - 1)
                terrace(NG - 1)

                pe.wait_ge(EtT_ready, b * 2 * NG + 2 * NG)
                for hq in range(HQ):
                    pe.wait_ge(wm_ready, b * HQ + hq + 1)
                    if hq >= 2:
                        pe.wait_ge(wT_ready, b * HQ + hq - 1)
                    for m in range(TC):
                        i = pe.transpose(bank[:, 4 + hq % 2, m * P:m * P + P], wm[:, hq, m * P:m * P + P], ident[:, :])
                    i.then_inc(wt_ready, 1)
                for hq in range(HQ):
                    pe.wait_ge(A_ready, b * TC * HQ + TC * (hq + 1))
                    for h in range(4):
                        col = 64 * hq + 16 * h
                        for m in range(TC):
                            i = pe.matmul(bank[:, 0, col:col + DH], A[:, hq % 2, m, h, :, :].rearrange("p r d -> p (r d)"),
                                          raw[:, m, 2 * D + col:2 * D + col + DH], start=(m == 0), stop=(m == TC - 1))
                    i.then_inc(kv_ready, 1)
                pe.wait_ge(BD_ready, b * 16 + 16)
                for t in range(TC):
                    if t >= 2:
                        pe.wait_ge(y_ready, b * TC + t - 1)
                    for hq in range(HQ):
                        i = pe.matmul(bank[:, 2 + t % 2, 64 * hq:64 * hq + 64], QMT[:, t, hq, :],
                                      BD[:, t, hq, :, :].rearrange("p h d -> p (h d)"), start=True, stop=True)
                    i.then_inc(lin_ready, 1)
                for t in range(TC):
                    pe.wait_ge(y_ready, b * TC + t + 1)
                    if t >= 2:
                        pe.wait_ge(yT_ready, b * TC + t - 1)
                    for kc in range(KC):
                        i = pe.transpose(bank[:, 6 + t % 2, kc * P:kc * P + P], y2[:, t % 2, kc * P:kc * P + P], ident[:, :])
                    i.then_inc(yt2_ready, 1)
                pe.wait_ge(yT_ready, b * TC + TC)
                for t in range(TC):
                    for kc in range(KC):
                        i = pe.matmul(bank[:, t, 0:D], yT[:, kc, t * P:t * P + P], w_c[:, kc, :], start=(kc == 0), stop=(kc == KC - 1))
                    i.then_inc(out_ready, 1)



def l1_cross_attention(nc, g, ctx_t, ln_gamma, ln_beta, w_q_d, w_kv_d, w_out_d, b_out, gate):
    H, DH = 16, 64
    NP = H // 2
    NS = SC // P
    NU = H * TC
    INNER = H * DH
    X, ident, bank = g.X, g.ident, g.bank
    with ExitStack() as c:
        def sb(name, shape, dt=F32):
            return c.enter_context(nc.sbuf_tensor("c1_" + name, shape, dt))

        def sem(name):
            return nc.alloc_semaphore("c1_" + name)

        w_q = sb("w_q", [P, KC, INNER])
        w_kv = sb("w_kv", [P, KC, 2 * INNER])
        w_out = sb("w_out", [P, NP, D])
        gam_bet = sb("gam_bet", [P, 2, KC])
        brow, brow_t = sb("brow", [P, D]), sb("brow_t", [P, D])
        gt, tg = sb("gt", [P, 1]), sb("tg", [P, 1])
        ctxT = sb("ctxT", [P, KC, SC])
        xn = sb("xn", [P, TC, D])
        xnT = sb("xnT", [P, KC, L])
        xb = sb("xb", [P, TC, D])
        V = sb("V", [P, NS, INNER])
        KT = sb("KT", [P, 2, 2, SC], F32R)
        QH = sb("QH", [P, 2, 2, L], F32R)
        QL = sb("QL", [P, 2, 2, L], F32R)
        nmax = sb("nmax", [P, 4])
        E = sb("E", [P, 2, SC])
        ET = sb("ET", [P, 2, NS, L])
        sums, rsum = sb("sums", [P, 2, TC]), sb("rsum", [P, 2, TC])
        minus_one = sb("minus_one", [P, TC])
        diag = sb("diag", [P, TC, P])
        rb = sb("rb", [P, 2 * P])
        oT = sb("oT", [P, NP, L])
        pre = Norm(nc, c, "c1_pre")
        ln = Norm(nc, c, "c1_ln")

        w_loaded, wo_loaded, small_loaded, ctx_loaded = sem("w_loaded"), sem("wo_loaded"), sem("small_loaded"), sem("ctx_loaded")
        ctx_free = sem("ctx_free")
        tg_ready, brow_ready, xb_ready = sem("tg_ready"), sem("brow_ready"), sem("xb_ready")
        xtp_ready, xT_ready = sem("xtp_ready"), sem("xT_ready")
        v_ready, V_ready = sem("v_ready"), sem("V_ready")
        proj_ready = sem("proj_ready")
        k_high, k_low, q_high, q_low = sem("k_high"), sem("k_low"), sem("q_high"), sem("q_low")
        s_ready, nmax_ready, e_ready = sem("s_ready"), sem("nmax_ready"), sem("e_ready")
        et_ready, et0_kept, et1_kept = sem("et_ready"), sem("et0_kept"), sem("et1_kept")
        rsum_ready, diag_ready = sem("rsum_ready"), sem("diag_ready")
        av_ready, rb_ready, oT_ready = sem("av_ready"), sem("rb_ready"), sem("oT_ready")
        out_ready, minus_one_ready = sem("out_ready"), sem("minus_one_ready")

        block = c.enter_context(nc.Block())

        @block.sync
        def _(sp):
            sp.dma_start(w_kv[:, :, :], w_kv_d.rearrange("(k p) n -> p k n", p=P)).then_inc(w_loaded, 16)
            sp.dma_start(w_q[:, :, :], w_q_d.rearrange("(k p) n -> p k n", p=P)).then_inc(w_loaded, 16)
            sp.dma_start(w_out[:, :, :], w_out_d.rearrange("(n p) d -> p n d", p=P)).then_inc(wo_loaded, 16)
            with sp.Fori(0, B) as b:
                sp.wait_ge(ctx_free, b + 1)
                sp.dma_start(ctxT[:, :, :], ctx_t[ds(b, 1), :, :].rearrange("b (k p) n -> p (b k) n", p=P)).then_inc(ctx_loaded, 16)
            sp.wait_ge(wo_loaded, 16)
            sp.wait_ge(w_loaded, 32)
            sp.wait_ge(ctx_loaded, 16 * B)

        @block.gpsimd
        def _(pool):
            pool.memset(minus_one[:, :], -1.0).then_inc(minus_one_ready, 1)
            pool.wait_ge(minus_one_ready, 1)
            pool.wait_ge(brow_ready, 1)
            with pool.Fori(0, B) as b:
                pre.rstd(g, pool, b)
                for t in range(TC):
                    pool.tensor_tensor(xb[:, t, :], pre.t[:, t, :], brow_t[:, :], ALU.add).then_inc(xb_ready, 1)

                def reciprocals(h):
                    pool.wait_ge(e_ready, b * NU + TC * h + TC)
                    pool.tensor_tensor(rsum[:, h % 2, :], sums[:, h % 2, :], minus_one[:, :], ALU.pow).then_inc(rsum_ready, 1)
                    pool.wait_ge(rsum_ready, b * H + h + 1)
                    if h >= 1:
                        pool.wait_ge(av_ready, b * H + h)
                    g.after_wait(pool)
                    for t in range(TC):
                        pool.tensor_scalar(diag[:, t, :], ident[:, :], rsum[:, h % 2, t:t + 1], 1.0, ALU.mult, ALU.mult).then_inc(diag_ready, 1)

                for h in range(H):
                    reciprocals(h)
                ln.rstd(g, pool, b)

        @block.scalar
        def _(act):
            act.dma_start(gam_bet[:, 0, :], ln_gamma).then_inc(small_loaded, 16)
            act.dma_start(gam_bet[:, 1, :], ln_beta).then_inc(small_loaded, 16)
            act.dma_start(brow[:, :], b_out.partition_broadcast(P)).then_inc(small_loaded, 16)
            act.dma_start(gt[:, :], gate.partition_broadcast(P)).then_inc(small_loaded, 16)
            act.wait_ge(small_loaded, 64)
            act.activation(tg[:, :], gt[:, :], ACT.Tanh).then_inc(tg_ready, 1)
            with act.Fori(0, B) as b:
                for kc in range(KC):
                    act.wait_ge(xtp_ready, b * KC + kc + 1)
                    act.activation(xnT[:, kc, :], bank[:, 4 + kc, :], ACT.Identity, bias=gam_bet[:, 1, kc:kc + 1],
                                   scale=gam_bet[:, 0, kc:kc + 1]).then_inc(xT_ready, 1)
                for n in range(2 * NS):
                    s, half = divmod(n, 2)
                    act.wait_ge(v_ready, b * 2 * NS + n + 1)
                    act.activation(V[:, s, half * 512:half * 512 + 512], bank[:, n % 4, :], ACT.Copy).then_inc(V_ready, 1)

                def high_k(p, half):
                    act.wait_ge(proj_ready, b * 3 * NP + 3 * p + half + 1)
                    for h in range(2):
                        act.activation(KT[0:64, p % 2, h, half * 512:half * 512 + 512], bank[64 * h:64 * h + 64, 7, :],
                                       ACT.Copy).then_inc(k_high, 1)

                def high_q(p):
                    act.wait_ge(proj_ready, b * 3 * NP + 3 * p + 3)
                    for h in range(2):
                        for r in range(2):
                            act.activation(QH[64 * r:64 * r + 64, p % 2, h, :], bank[64 * h:64 * h + 64, 7, :],
                                           ACT.Copy, scale=DH ** -0.5).then_inc(q_high, 1)

                def exps(u):
                    h = u // TC
                    act.wait_ge(nmax_ready, b * NU + u + 1)
                    if u >= 2:
                        act.wait_ge(et_ready, b * 2 * NU + 2 * (u - 1))
                    if u % TC == 0 and h >= 2:
                        act.wait_ge(rsum_ready, b * H + h - 1)
                    act.activation(E[:, u % 2, :], bank[:, 2 * (u % 2):2 * (u % 2) + 2, :].rearrange("p a n -> p (a n)"), ACT.Exp,
                                   bias=nmax[:, u % 4:u % 4 + 1], accum_out=sums[:, h % 2, u % TC:u % TC + 1]).then_inc(e_ready, 1)

                def keep(u):
                    h, t = divmod(u, TC)
                    if t == 0 and h >= 2:
                        act.wait_ge(av_ready, b * H + h - 1)
                    act.wait_ge(et_ready, b * 2 * NU + 2 * u + 1)
                    act.activation(ET[:, h % 2, 0:4, t * P:t * P + P], bank[:, 4, :].rearrange("p (k n) -> p k n", k=4),
                                   ACT.Copy).then_inc(et0_kept, 1)

                high_k(0, 0)
                high_k(0, 1)
                high_q(0)
                exps(0)
                exps(1)
                for u in range(NU):
                    keep(u)
                    if u + 2 < NU:
                        exps(u + 2)
                    p, r = divmod(u, 2 * TC)
                    if p + 1 < NP:
                        if r in (0, 3):
                            high_k(p + 1, r // 3)
                        if r == 4:
                            high_q(p + 1)

        @block.vector
        def _(dve):
            dve.wait_ge(small_loaded, 64)
            dve.wait_ge(tg_ready, 1)
            dve.tensor_scalar(brow_t[:, :], brow[:, :], tg[:, 0:1], None, ALU.mult).then_inc(brow_ready, 1)
            dve.sem_inc(ln.banks_free, TC)
            with dve.Fori(0, B) as b:
                for t in range(TC):
                    dve.tensor_copy(pre.t[:, t, :], X[:, b * TC + t, :]).then_inc(pre.sum_ready, 1)
                pre.stats(g, dve, b)
                pre.apply(dve, lambda t: xn[:, t, :], b)

                def low_k(p, half):
                    for h in range(2):
                        dve.wait_ge(k_high, b * 4 * NP + 4 * p + 2 * half + h + 1)
                        cols = slice(half * 512, half * 512 + 512)
                        dve.tensor_tensor(KT[64:P, p % 2, h, cols], bank[64 * h:64 * h + 64, 7, :],
                                          KT[0:64, p % 2, h, cols].bitcast(F32), ALU.subtract).then_inc(k_low, 1)

                def low_q(p, h):
                    dve.wait_ge(q_high, b * 4 * NP + 4 * p + 2 * h + 2)
                    for r in range(2):
                        dve.scalar_tensor_tensor(out=QL[64 * r:64 * r + 64, p % 2, h, :], in0=bank[64 * h:64 * h + 64, 7, :],
                                                 scalar=DH ** -0.5, in1=QH[64 * r:64 * r + 64, p % 2, h, :].bitcast(F32),
                                                 op0=ALU.mult, op1=ALU.subtract).then_inc(q_low, 1)

                def maxima(u):
                    dve.wait_ge(s_ready, b * NU + u + 1)
                    if u >= 4:
                        dve.wait_ge(e_ready, b * NU + u - 3)
                    dve.tensor_reduce(nmax[:, u % 4:u % 4 + 1], bank[:, 2 * (u % 2):2 * (u % 2) + 2, :], AX.XY, ALU.max,
                                      negate=True).then_inc(nmax_ready, 1)

                def keep(u):
                    h, t = divmod(u, TC)
                    if t == 0 and h >= 2:
                        dve.wait_ge(av_ready, b * H + h - 1)
                    dve.wait_ge(et_ready, b * 2 * NU + 2 * u + 2)
                    dve.tensor_copy(ET[:, h % 2, 4:8, t * P:t * P + P], bank[:, 5, :].rearrange("p (k n) -> p k n", k=4)).then_inc(et1_kept, 1)

                def normalise(h):
                    dve.wait_ge(av_ready, b * H + h + 1)
                    if h >= 1:
                        dve.wait_ge(oT_ready, b * 2 * H + 2 * h)
                    dve.tensor_copy(rb[:, :], bank[:, 6, 2 * P:4 * P]).then_inc(rb_ready, 1)
                    dve.wait_ge(rb_ready, b * H + h + 1)
                    for j in range(2):
                        dve.tensor_tensor(oT[64 * (h % 2):64 * (h % 2) + 64, h // 2, 256 * j:256 * j + 256], bank[64 * j:64 * j + 64, 6, 0:2 * P],
                                          rb[64 * j:64 * j + 64, :], ALU.mult).then_inc(oT_ready, 1)

                low_k(0, 0)
                low_k(0, 1)
                low_q(0, 0)
                low_q(0, 1)
                maxima(0)
                maxima(1)
                for u in range(NU):
                    if u + 2 < NU:
                        maxima(u + 2)
                    keep(u)
                    if u % TC == 0 and u >= 2 * TC:
                        normalise(u // TC - 2)
                    p, r = divmod(u, 2 * TC)
                    if p + 1 < NP:
                        if r in (0, 3):
                            low_k(p + 1, r // 3)
                        if r in (4, 5):
                            low_q(p + 1, r - 4)
                normalise(H - 2)
                normalise(H - 1)
                dve.wait_ge(xb_ready, b * TC + TC)
                for t in range(TC):
                    dve.wait_ge(out_ready, b * TC + t + 1)
                    dve.scalar_tensor_tensor(out=ln.t[:, t, :], in0=bank[:, t, 0:D], scalar=tg[:, 0:1], in1=xb[:, t, :],
                                             op0=ALU.mult, op1=ALU.add).then_inc(ln.sum_ready, 1)
                dve.wait_ge(ln.sum_ready, b * TC + TC)
                dve.sem_inc(ln.banks_free, TC)
                ln.stats(g, dve, b)
                ln.apply(dve, lambda t: X[:, b * TC + t, :], b)

        @block.tensor
        def _(pe):
            pe.sem_inc(ctx_free, 1)
            pe.wait_ge(w_loaded, 32)
            with pe.Fori(0, B) as b:
                pe.wait_ge(ln.banks_free, b * TC + TC)
                pe.wait_ge(pre.x_ready, b * TC + TC)
                for kc in range(KC):
                    for t in range(TC):
                        i = pe.transpose(bank[:, 4 + kc, t * P:t * P + P], xn[:, t, kc * P:kc * P + P], ident[:, :])
                    i.then_inc(xtp_ready, 1)
                pe.wait_ge(ctx_loaded, b * 16 + 16)
                for n in range(2 * NS):
                    s, half = divmod(n, 2)
                    if n >= 4:
                        pe.wait_ge(V_ready, b * 2 * NS + n - 3)
                    for kc in range(KC):
                        i = pe.matmul(bank[:, n % 4, :], ctxT[:, kc, s * P:s * P + P],
                                      w_kv[:, kc, INNER + half * 512:INNER + half * 512 + 512], start=(kc == 0), stop=(kc == KC - 1))
                    i.then_inc(v_ready, 1)
                pe.wait_ge(xT_ready, b * KC + KC)
                pe.wait_ge(V_ready, b * 2 * NS + 2 * NS)

                def bank_7_free(n):
                    if n >= 1:
                        p, j = divmod(n - 1, 3)
                        if j < 2:
                            pe.wait_ge(k_low, b * 4 * NP + 4 * p + 2 * j + 2)
                        else:
                            pe.wait_ge(q_low, b * 4 * NP + 4 * p + 4)

                def project(p, j):
                    bank_7_free(3 * p + j)
                    for kc in range(KC):
                        if j < 2:
                            i = pe.matmul(bank[:, 7, :], w_kv[:, kc, p * P:p * P + P], ctxT[:, kc, j * 512:j * 512 + 512],
                                          start=(kc == 0), stop=(kc == KC - 1))
                        else:
                            i = pe.matmul(bank[:, 7, :], w_q[:, kc, p * P:p * P + P], xnT[:, kc, :], start=(kc == 0), stop=(kc == KC - 1))
                    i.then_inc(proj_ready, 1)

                def scores(u):
                    h, t = divmod(u, TC)
                    p = h // 2
                    if u % (2 * TC) == 0:
                        pe.wait_ge(k_low, b * 4 * NP + 4 * p + 4)
                        pe.wait_ge(q_low, b * 4 * NP + 4 * p + 4)
                    if u >= 2:
                        pe.wait_ge(e_ready, b * NU + u - 1)
                    for n, q in enumerate((QL, QH)):
                        for half in range(2):
                            i = pe.matmul(bank[:, 2 * (u % 2) + half, :], q[:, p % 2, h % 2, t * P:t * P + P],
                                          KT[:, p % 2, h % 2, half * 512:half * 512 + 512], start=(n == 0), stop=(n == 1))
                    i.then_inc(s_ready, 1)

                def turn(u):
                    pe.wait_ge(e_ready, b * NU + u + 1)
                    for half in range(2):
                        if u >= 1:
                            pe.wait_ge(et1_kept if half else et0_kept, b * NU + u)
                        for k in range(4):
                            col = (4 * half + k) * P
                            i = pe.transpose(bank[:, 4 + half, k * P:k * P + P], E[:, u % 2, col:col + P], ident[:, :])
                        i.then_inc(et_ready, 1)

                def values(h, chunks):
                    if chunks.start == 0:
                        pe.wait_ge(et0_kept, b * NU + TC * h + TC)
                        pe.wait_ge(et1_kept, b * NU + TC * h + TC)
                        if h >= 1:
                            pe.wait_ge(oT_ready, b * 2 * H + 2 * h)
                    for k in chunks:
                        for j in range(2):
                            pe.matmul(bank[64 * j:64 * j + 64, 6, 0:2 * P], V[:, k, DH * h:DH * h + DH],
                                      ET[:, h % 2, k, 256 * j:256 * j + 256], start=(k == 0), stop=(k == NS - 1))
                    if chunks.stop < NS:
                        return
                    pe.wait_ge(diag_ready, b * TC * H + TC * h + TC)
                    for t in range(2):
                        for j in range(2):
                            i = pe.matmul(bank[64 * j:64 * j + 64, 6, 2 * P + t * P:3 * P + t * P], g.ones[:, :],
                                          diag[:, 2 * j + t, :], start=True, stop=True)
                    i.then_inc(av_ready, 1)

                for j in range(3):
                    project(0, j)
                scores(0)
                scores(1)
                for u in range(NU):
                    if u + 2 < NU:
                        scores(u + 2)
                    turn(u)
                    p, r = divmod(u, 2 * TC)
                    if p + 1 < NP and r in (0, 3, 4):
                        project(p + 1, (0, 3, 4).index(r))
                    if u % TC >= 1 and u >= TC:
                        values(u // TC - 1, (range(0, 3), range(3, 6), range(6, 8))[u % TC - 1])
                pe.wait_ge(q_low, b * 4 * NP + 4 * NP)
                pe.sem_inc(ctx_free, 1)
                values(H - 1, range(NS))
                pe.wait_ge(wo_loaded, 16)
                pe.wait_ge(oT_ready, b * 2 * H + 2 * H)
                for t in range(TC):
                    for p in range(NP):
                        i = pe.matmul(bank[:, t, 0:D], oT[:, p, t * P:t * P + P], w_out[:, p, :], start=(p == 0), stop=(p == NP - 1))
                    i.then_inc(out_ready, 1)





def decoder(nc, x, ctx_rows, ctx_t,
            a0_norm_w, a0_wq, a0_wkv, a0_wo, a0_q_gamma_t, a0_k_gamma_t,
            c0_x1_t, c0_w1_t, c0_b1, c0_w2_t, c0_b2, c0_w3_t, c0_b3,
            m0_router, m0_w1, m0_b1, m0_w2, m0_b2, m0_gamma, m0_beta,
            t1_w_qkv_t, t1_w_c_t, t1_mix, t1_index_decays_t, t1_mega_decays,
            c1_gamma, c1_beta, c1_wq, c1_wkv, c1_wo, c1_bo, c1_gate,
            m1_rw1, m1_rb1, m1_rw2, m1_rb2, m1_w1, m1_b1, m1_w2, m1_b2,
            out):
    g = Shared()
    with ExitStack() as ctx:
        setup(nc, g, ctx, x)
        with nc.cleanup_on_exit():
            l0_attention(nc, g, a0_norm_w, a0_wq, a0_wkv, a0_wo, a0_q_gamma_t, a0_k_gamma_t)
        with nc.cleanup_on_exit():
            l0_cross_attention(nc, g, ctx_rows, c0_x1_t, c0_w1_t, c0_b1, c0_w2_t, c0_b2, c0_w3_t, c0_b3)
        with nc.cleanup_on_exit():
            l0_ffn(nc, g, m0_router, m0_w1, m0_b1, m0_w2, m0_b2, m0_gamma, m0_beta)
        with nc.cleanup_on_exit():
            l1_attention(nc, g, t1_w_qkv_t, t1_w_c_t, t1_mix, t1_index_decays_t, t1_mega_decays)
        with nc.cleanup_on_exit():
            l1_cross_attention(nc, g, ctx_t, c1_gamma, c1_beta, c1_wq, c1_wkv, c1_wo, c1_bo, c1_gate)
        with nc.cleanup_on_exit():
            l1_ffn(nc, g, m1_rw1, m1_rb1, m1_rw2, m1_rb2, m1_w1, m1_b1, m1_w2, m1_b2)
        finish(nc, g, out)



def kernel(**inputs):
    import numpy as np
    import concourse.bacc as bacc
    from concourse.bass_utils import run_bass_kernel_spmd

    w = {name: np.asarray(a) for name, a in inputs.items()}

    def per_partition(a):
        a = a.reshape(a.shape[:-1] + (a.shape[-1] // P, P))
        return np.moveaxis(a, -1, 0)

    laid_out = [
        w["x"], w["ctx_1024"], w["ctx_1024"].transpose(0, 2, 1),
        per_partition(w["L0_attn_norm_w"]), w["L0_attn_Wq"], w["L0_attn_Wkv"], w["L0_attn_Wo"],
        w["L0_attn_q_gamma"].T, w["L0_attn_k_gamma"].T,
        w["L0_xattn_x1"].T, w["L0_xattn_W1"].T, per_partition(w["L0_xattn_b1"]), w["L0_xattn_W2"].T,
        per_partition(w["L0_xattn_b2"]), w["L0_xattn_W3"].T, w["L0_xattn_b3"],
        w["L0_ffn_router_w"], w["L0_ffn_w1"], per_partition(w["L0_ffn_b1"]), w["L0_ffn_w2"],
        w["L0_ffn_b2"], w["L0_ffn_gamma"], w["L0_ffn_beta"],
        np.concatenate([w["L1_attn_Wq"], w["L1_attn_Wk"], w["L1_attn_Wv"]]).T, w["L1_attn_Wc"].T,
        w["L1_attn_terrace_mix"].reshape(64, 1), w["L1_attn_index_decays"].T, w["L1_attn_mega_decays"],
        per_partition(w["L1_xattn_ln_gamma"]), per_partition(w["L1_xattn_ln_beta"]), w["L1_xattn_w_q"],
        w["L1_xattn_w_kv"], w["L1_xattn_w_out"], w["L1_xattn_b_out"], w["L1_xattn_gate"],
        w["L1_ffn_rW1"], per_partition(w["L1_ffn_rb1"]), w["L1_ffn_rW2"], w["L1_ffn_rb2"],
        w["L1_ffn_We1"], per_partition(w["L1_ffn_be1"]), w["L1_ffn_We2"], w["L1_ffn_be2"],
    ]
    nc = bacc.Bacc("TRN2", target_bir_lowering=False, num_devices=1)
    arrays, args = {}, []
    for n, a in enumerate(laid_out):
        a = np.ascontiguousarray(a)
        arrays[f"in_{n}_dram"] = a
        args.append(nc.dram_tensor(f"in_{n}_dram", a.shape, mybir.dt.from_np(a.dtype), kind="ExternalInput").ap())
    args.append(nc.dram_tensor("out_dram", (B, L, D), F32, kind="ExternalOutput").ap())
    decoder(nc, *args)
    r = run_bass_kernel_spmd(nc, [arrays], core_ids=[0])
    return r.results[0]["out_dram"]
```

```python
from contextlib import ExitStack

import concourse.bass as bass
from concourse import mybir

F32 = mybir.dt.float32
F32R = mybir.dt.float32r
BF16 = mybir.dt.bfloat16
ALU = mybir.AluOpType
ACT = mybir.ActivationFunctionType
AX = mybir.AxisListType

P = 128
B = 4
L = 512
D = 256
TC = L // P
KC = D // P
SC = 1024
LN_EPS = 1e-5
SLOTS = 23 * 256


ds = bass.ds


class Shared:

    def after_wait(self, engine):
        engine.sem_inc(self.passed[engine.engine], 1)


def setup(nc, g, ctx, x):
    g.X = ctx.enter_context(nc.sbuf_tensor("X", [P, B * TC, D], F32))
    g.ident = ctx.enter_context(nc.sbuf_tensor("ident", [P, P], F32))
    g.ones = ctx.enter_context(nc.sbuf_tensor("ones", [P, 64], F32))
    g.neg_half = ctx.enter_context(nc.sbuf_tensor("neg_half", [P, 16], F32))
    g.bank = ctx.enter_context(nc.psum_tensor("bank", [P, 8, 512], F32))
    g.zeros = ctx.enter_context(nc.sbuf_tensor("zeros", [P, D], F32))
    g.x_slots = nc.dram_tensor("x_slots", [SLOTS, D], F32).ap()
    g.y_slots = nc.dram_tensor("y_slots", [SLOTS, D], F32).ap()
    g.x_loaded = nc.alloc_semaphore("x_loaded")
    g.x_rest_loaded = nc.alloc_semaphore("x_rest_loaded")
    g.slots_zeroed = nc.alloc_semaphore("slots_zeroed")
    g.passed = {e.engine: nc.alloc_semaphore(f"passed_{n}")
                for n, e in (("dve", nc.vector), ("pool", nc.gpsimd), ("act", nc.scalar), ("pe", nc.tensor))}
    with ExitStack() as c:
        zeroed = nc.alloc_semaphore("ident_zeroed")
        made = nc.alloc_semaphore("constants_made")
        block = c.enter_context(nc.Block())

        @block.sync
        def _(sp):
            sp.dma_start(g.X[:, 0:TC, :], x[0].rearrange("(t p) d -> p t d", p=P)).then_inc(g.x_loaded, 16)

        @block.gpsimd
        def _(pool):
            pool.memset(g.ident[:, :], 0.0).then_inc(zeroed, 1)
            pool.memset(g.ones[:, :], 1.0).then_inc(made, 1)
            pool.memset(g.neg_half[:, :], -0.5).then_inc(made, 1)
            pool.memset(g.zeros[:, :], 0.0).then_inc(made, 1)
            pool.wait_ge(zeroed, 1)
            pool.affine_select(out=g.ident[:, :], in_=g.ident[:, :], compare_op=ALU.not_equal, fill=1.0,
                               base=0, pattern=[[-1, P]], channel_multiplier=1).then_inc(made, 1)
            pool.wait_ge(made, 4)



class Norm:

    def __init__(self, nc, c, name):
        self.t = c.enter_context(nc.sbuf_tensor(f"{name}_sum", [P, TC, D], F32))
        self.st = c.enter_context(nc.sbuf_tensor(f"{name}_stats", [P, TC, 6], F32))
        self.mv = c.enter_context(nc.sbuf_tensor(f"{name}_mean_var", [P, TC, 2], F32))
        self.ve = c.enter_context(nc.sbuf_tensor(f"{name}_var_eps", [P, TC], F32))
        self.rs = c.enter_context(nc.sbuf_tensor(f"{name}_rstd", [P, TC], F32))
        self.sum_ready = nc.alloc_semaphore(f"{name}_sum_ready")
        self.stats_ready = nc.alloc_semaphore(f"{name}_stats_ready")
        self.mv_ready = nc.alloc_semaphore(f"{name}_mv_ready")
        self.ve_ready = nc.alloc_semaphore(f"{name}_ve_ready")
        self.rs_ready = nc.alloc_semaphore(f"{name}_rs_ready")
        self.banks_free = nc.alloc_semaphore(f"{name}_banks_free")
        self.x_ready = nc.alloc_semaphore(f"{name}_x_ready")

    def stats(self, g, dve, b):
        for t in range(TC):
            dve.wait_ge(self.sum_ready, b * TC + t + 1)
            dve.bn_stats(self.st[:, t, :], self.t[:, t, :]).then_inc(self.stats_ready, 1)
        for t in range(TC):
            dve.wait_ge(self.stats_ready, b * TC + t + 1)
            g.after_wait(dve)
            dve.bn_aggr(self.mv[:, t, :], self.st[:, t, :]).then_inc(self.mv_ready, 1)

    def rstd(self, g, pool, b, eps=LN_EPS):
        pool.wait_ge(self.mv_ready, b * TC + TC)
        g.after_wait(pool)
        pool.tensor_scalar(self.ve[:, :], self.mv[:, :, 1], eps, 0.0, ALU.add, ALU.add).then_inc(self.ve_ready, 1)
        pool.wait_ge(self.ve_ready, b + 1)
        pool.tensor_tensor(self.rs[:, :], self.ve[:, :], g.neg_half[:, 0:TC], ALU.pow).then_inc(self.rs_ready, 1)

    def apply(self, dve, out, b):
        dve.wait_ge(self.rs_ready, b + 1)
        for t in range(TC):
            dve.tensor_scalar(out(t), self.t[:, t, :], self.mv[:, t, 0:1], self.rs[:, t:t + 1],
                              ALU.subtract, ALU.mult).then_inc(self.x_ready, 1)



def l0_attention(nc, g, x, norm_w, wq, wkv, wo, q_gamma_t, k_gamma_t):
    H, DH, CLAMP = 16, 64, 50.0
    NP = H // 2
    RMS_EPS = 1.1920929e-07
    X, ident, bank = g.X, g.ident, g.bank
    with ExitStack() as c:
        def sb(name, shape, dt=F32):
            return c.enter_context(nc.sbuf_tensor("a0_" + name, shape, dt))

        def sem(name):
            return nc.alloc_semaphore("a0_" + name)

        w_qkv = sb("w_qkv", [P, KC, 3, H * DH])
        w_o = sb("w_o", [P, NP, D])
        nw = sb("norm_w", [P, KC])
        gam = sb("gammas", [P, 2, H])
        gam1 = sb("gammas_plus_1", [P, 2, H])
        gq = sb("gamma_product", [P, H])
        sq_junk = sb("sq_junk", [P, D])
        ssq = sb("ssq", [P, TC])
        ms = sb("mean_square", [P, TC])
        rs = sb("rms_scale", [P, TC])
        xs = sb("xs", [P, TC, D])
        xT = sb("xT", [P, KC, L])
        raw = sb("raw", [P, 4, TC, 3 * P])
        sq = sb("sq", [P, TC, 4, DH])
        ss = sb("ss", [P, TC, 4])
        sf = sb("sf", [P, TC, 4])
        rn = sb("rn", [P, TC, 4])
        nd = sb("nd", [P, 2, TC, 4, 2, DH])
        KT = sb("KT", [P, 2, 2, L], F32R)
        QH = sb("QH", [P, 2, 2, L], F32R)
        QL = sb("QL", [P, 2, 2, L], F32R)
        E = sb("E", [P, 4, TC, L])
        es1 = sb("es1", [P, 2, L])
        es = sb("es", [P, 4, L])
        rec = sb("rec", [P, L])
        oT = sb("oT", [P, NP, L])
        ln = Norm(nc, c, "a0_ln")

        w_loaded, wo_loaded, gam_loaded = sem("w_loaded"), sem("wo_loaded"), sem("gam_loaded")
        gam_ready = sem("gam_ready")
        ssq_ready, ms_ready, rs_ready, xs_ready = sem("ssq_ready"), sem("ms_ready"), sem("rs_ready"), sem("xs_ready")
        xtp_ready, xT_ready = sem("xtp_ready"), sem("xT_ready")
        proj_ready, raw_ready = sem("proj_ready"), sem("raw_ready")
        sq_ready, ss_ready, sf_ready, rn_ready, nd_ready = sem("sq_ready"), sem("ss_ready"), sem("sf_ready"), sem("rn_ready"), sem("nd_ready")
        tr_ready, hi_ready, lo_ready = sem("tr_ready"), sem("hi_ready"), sem("lo_ready")
        s_ready, tanh_ready = sem("s_ready"), sem("tanh_ready")
        e_ready, es1_ready, es_ready = sem("e_ready"), sem("es1_ready"), sem("es_ready")
        o_ready, den_ready = sem("o_ready"), sem("den_ready")
        rec_ready, oT_ready = sem("rec_ready"), sem("oT_ready")
        wo_ready = sem("wo_ready")

        block = c.enter_context(nc.Block())

        @block.sync
        def _(sp):
            for kc in range(KC):
                rows = slice(kc * P, kc * P + P)
                sp.dma_start(w_qkv[:, kc, 0, :], wq[rows, :]).then_inc(w_loaded, 16)
                sp.dma_start(w_qkv[:, kc, 1:3, :], wkv[rows, :].rearrange("p (s n) -> p s n", s=2)).then_inc(w_loaded, 16)
            sp.dma_start(X[:, TC:B * TC, :], x[1:B].rearrange("b (t p) d -> p (b t) d", p=P)).then_inc(g.x_rest_loaded, 16)
            sp.dma_start(w_o[:, :, :], wo.rearrange("(n p) d -> p n d", p=P)).then_inc(wo_loaded, 16)
            sp.dma_start(g.x_slots.rearrange("(t p) d -> p t d", p=P),
                         g.zeros[:, None, :].to_broadcast([P, SLOTS // P, D])).then_inc(g.slots_zeroed, 16)
            sp.wait_ge(w_loaded, 16 * 4)

        @block.gpsimd
        def _(pool):
            def row_scales(b):
                pool.wait_ge(ssq_ready, b * TC + TC)
                g.after_wait(pool)
                pool.tensor_scalar(ms[:, :], ssq[:, :], 1.0 / D, RMS_EPS, ALU.mult, ALU.add).then_inc(ms_ready, 1)
                pool.wait_ge(ms_ready, b + 1)
                pool.tensor_tensor(rs[:, :], ms[:, :], g.neg_half[:, 0:TC], ALU.pow).then_inc(rs_ready, 1)

            row_scales(0)
            with pool.Fori(0, B) as b:
                def head_scales(p):
                    pool.wait_ge(ss_ready, b * NP + p + 1)
                    g.after_wait(pool)
                    pool.tensor_scalar(sf[:, :, :], ss[:, :, :], 1e-24, 0.0, ALU.max, ALU.add).then_inc(sf_ready, 1)
                    pool.wait_ge(sf_ready, b * NP + p + 1)
                    pool.tensor_tensor(rn[:, :, :], sf[:, :, :], g.neg_half[:, :].rearrange("p (t h) -> p t h", t=TC),
                                       ALU.pow).then_inc(rn_ready, 1)

                def key_sums(p, h):
                    n = 2 * p + h
                    pool.wait_ge(e_ready, b * H + n + 1)
                    if p >= 2:
                        pool.wait_ge(den_ready, b * NP + p - 1)
                    e = E[:, n % 4, :, :]
                    pool.tensor_tensor(es1[:, :, :], e[:, 0:2, :], e[:, 2:4, :], ALU.add).then_inc(es1_ready, 1)
                    pool.wait_ge(es1_ready, b * H + n + 1)
                    pool.tensor_tensor(es[:, n % 4, :], es1[:, 0, :], es1[:, 1, :], ALU.add).then_inc(es_ready, 1)
                    pool.wait_ge(es_ready, b * H + n + 1)

                head_scales(0)
                head_scales(1)
                for p in range(NP):
                    if p + 2 < NP:
                        head_scales(p + 2)
                    key_sums(p, 0)
                    key_sums(p, 1)
                row_scales(b + 1)
                ln.rstd(g, pool, b)

        @block.scalar
        def _(act):
            act.dma_start(nw[:, :], norm_w).then_inc(gam_loaded, 16)
            for n, src in ((0, q_gamma_t), (1, k_gamma_t)):
                for half in range(2):
                    act.dma_start(gam[64 * half:64 * half + 64, n, :], src).then_inc(gam_loaded, 16)
            act.wait_ge(gam_loaded, 16 * 5)
            act.wait_ge(gam_ready, 2)
            act.wait_ge(g.x_loaded, 16)

            def row_squares(b):
                for t in range(TC):
                    if t:
                        act.wait_ge(ssq_ready, b * TC + t)
                    act.activation(sq_junk[:, :], X[:, b % B * TC + t, :], ACT.Square,
                                   accum_out=ssq[:, t:t + 1]).then_inc(ssq_ready, 1)

            row_squares(0)
            with act.Fori(0, B) as b:
                for kc in range(KC):
                    act.wait_ge(xtp_ready, b * KC + kc + 1)
                    act.activation(xT[:, kc, :], bank[:, 4 + kc, :], ACT.Copy, scale=nw[:, kc:kc + 1]).then_inc(xT_ready, 1)

                def keep_raw(p, chunks):
                    for t in chunks:
                        act.wait_ge(proj_ready, b * TC * NP + TC * p + t + 1)
                        if t == 0 and p >= 4:
                            act.wait_ge(o_ready, b * NP + p - 3)
                            act.wait_ge(nd_ready, b * 4 * NP + 4 * (p - 3))
                        act.activation(raw[:, p % 4, t, :], bank[:, 2 + t % 2, 0:3 * P], ACT.Copy).then_inc(raw_ready, 1)

                def high_parts(p, parts):
                    for j in parts:
                        n = TC * p + j
                        act.wait_ge(tr_ready, b * TC * NP + n + 1)
                        src = bank[:, 4 + j % 2, :]
                        if j < 2:
                            act.activation(QH[:, p % 2, j, :], src, ACT.Copy, scale=gq[:, 2 * p + j:2 * p + j + 1]).then_inc(hi_ready, 1)
                        else:
                            act.activation(KT[:, p % 2, j - 2, :], src, ACT.Copy).then_inc(hi_ready, 1)

                def exps(p, h):
                    n = 2 * p + h
                    if n >= 4:
                        act.wait_ge(o_ready, b * NP + p - 1)
                        act.wait_ge(es_ready, b * H + n - 3)
                    for k in range(TC):
                        act.wait_ge(s_ready, b * H * TC + n * TC + k + 1)
                        act.activation(E[:, n % 4, k, :], bank[:, k % 2, :], ACT.Tanh, scale=1.0 / CLAMP).then_inc(tanh_ready, 1)
                        if h == 0 and p + 2 < NP:
                            keep_raw(p + 2, (k,))
                        if h == 1 and p + 1 < NP:
                            high_parts(p + 1, (k,))
                    act.wait_ge(tanh_ready, b * H * TC + n * TC + TC)
                    act.activation(E[:, n % 4, :, :], E[:, n % 4, :, :], ACT.Exp, scale=CLAMP * DH ** -0.5).then_inc(e_ready, 1)

                keep_raw(0, range(TC))
                keep_raw(1, range(TC))
                high_parts(0, range(4))
                for p in range(NP):
                    exps(p, 0)
                    exps(p, 1)
                act.wait_ge(ms_ready, b + 1)
                act.wait_ge(g.x_rest_loaded, 16)
                row_squares(b + 1)

        @block.vector
        def _(dve):
            dve.wait_ge(gam_loaded, 16 * 5)
            dve.tensor_scalar(gam1[:, :, :], gam[:, :, :], 1.0, DH ** 0.5, ALU.add, ALU.mult).then_inc(gam_ready, 1)
            dve.wait_ge(gam_ready, 1)
            dve.tensor_tensor(gq[:, :], gam1[:, 0, :], gam1[:, 1, :], ALU.mult).then_inc(gam_ready, 1)
            dve.wait_ge(gam_ready, 2)
            dve.sem_inc(ln.banks_free, TC)
            dve.wait_ge(g.x_loaded, 16)

            def scale_rows(b):
                dve.wait_ge(rs_ready, b + 1)
                for t in range(TC):
                    dve.tensor_scalar(xs[:, t, :], X[:, b % B * TC + t, :], rs[:, t:t + 1], None, ALU.mult).then_inc(xs_ready, 1)

            scale_rows(0)
            with dve.Fori(0, B) as b:
                def squares(p):
                    dve.wait_ge(raw_ready, b * TC * NP + TC * p + TC)
                    qk = raw[:, p % 4, :, 0:2 * P].rearrange("p t (h d) -> p t h d", d=DH)
                    dve.tensor_tensor(sq[:, :, :, :], qk, qk, ALU.mult).then_inc(sq_ready, 1)
                    dve.wait_ge(sq_ready, b * NP + p + 1)
                    dve.tensor_reduce(ss[:, :, :], sq[:, :, :, :], AX.X, ALU.add).then_inc(ss_ready, 1)

                def head_norms(p):
                    dve.wait_ge(rn_ready, b * NP + p + 1)
                    if p >= 2:
                        dve.wait_ge(tr_ready, b * TC * NP + TC * (p - 1))
                    for h in range(4):
                        src = raw[:, p % 4, :, DH * h:DH * h + DH]
                        dve.tensor_tensor(nd[:, p % 2, :, h, :, :], src[:, :, None, :].to_broadcast([P, TC, 2, DH]),
                                          rn[:, :, h:h + 1, None].to_broadcast([P, TC, 2, DH]), ALU.mult).then_inc(nd_ready, 1)

                def low_parts(p):
                    for j in range(4):
                        dve.wait_ge(hi_ready, b * TC * NP + TC * p + j + 1)
                        src = bank[:, 4 + j % 2, :]
                        if j < 2:
                            dve.scalar_tensor_tensor(out=QL[:, p % 2, j, :], in0=src, scalar=gq[:, 2 * p + j:2 * p + j + 1],
                                                     in1=QH[:, p % 2, j, :].bitcast(F32), op0=ALU.mult,
                                                     op1=ALU.subtract).then_inc(lo_ready, 1)
                        else:
                            dve.tensor_tensor(KT[DH:P, p % 2, j - 2, :], src[DH:P], KT[DH:P, p % 2, j - 2, :].bitcast(F32),
                                              ALU.subtract).then_inc(lo_ready, 1)

                def normalise(p):
                    dve.wait_ge(den_ready, b * NP + p + 1)
                    if p >= 1:
                        dve.wait_ge(oT_ready, b * NP + p)
                    dve.reciprocal(rec[:, :], bank[:, 7, :]).then_inc(rec_ready, 1)
                    dve.wait_ge(rec_ready, b * NP + p + 1)
                    dve.wait_ge(o_ready, b * NP + p + 1)
                    dve.tensor_tensor(oT[:, p, :], bank[:, 6, :], rec[:, :], ALU.mult).then_inc(oT_ready, 1)

                squares(0)
                head_norms(0)
                low_parts(0)
                squares(1)
                head_norms(1)
                for p in range(NP):
                    if p >= 2:
                        normalise(p - 2)
                    if p + 2 < NP:
                        squares(p + 2)
                    if p + 1 < NP:
                        low_parts(p + 1)
                    if p + 2 < NP:
                        head_norms(p + 2)
                normalise(NP - 2)
                normalise(NP - 1)
                for t in range(TC):
                    dve.wait_ge(wo_ready, b * TC + t + 1)
                    dve.tensor_tensor(ln.t[:, t, :], bank[:, 2 + t, 0:D], X[:, b * TC + t, :], ALU.add).then_inc(ln.sum_ready, 1)
                dve.wait_ge(ln.sum_ready, b * TC + TC)
                dve.sem_inc(ln.banks_free, TC)
                dve.wait_ge(g.x_rest_loaded, 16)
                scale_rows(b + 1)
                ln.stats(g, dve, b)
                ln.apply(dve, lambda t: X[:, b * TC + t, :], b)

        @block.tensor
        def _(pe):
            with pe.Fori(0, B) as b:
                pe.wait_ge(ln.banks_free, b * TC + TC)
                pe.wait_ge(xs_ready, b * TC + TC)
                for kc in range(KC):
                    for t in range(TC):
                        i = pe.transpose(bank[:, 4 + kc, t * P:t * P + P], xs[:, t, kc * P:kc * P + P], ident[:, :])
                    i.then_inc(xtp_ready, 1)
                pe.wait_ge(xT_ready, b * KC + KC)
                pe.wait_ge(w_loaded, 16 * 4)

                def project(p, chunks):
                    for t in chunks:
                        n = TC * p + t
                        if n >= 2:
                            pe.wait_ge(raw_ready, b * TC * NP + n - 1)
                        for kc in range(KC):
                            i = pe.matmul(bank[:, 2 + t % 2, 0:3 * P].rearrange("p (s n) -> p s n", s=3),
                                          xT[:, kc, t * P:t * P + P], w_qkv[:, kc, :, p * P:p * P + P],
                                          start=(kc == 0), stop=(kc == KC - 1))
                        i.then_inc(proj_ready, 1)

                def turn(p, parts):
                    pe.wait_ge(nd_ready, b * 4 * NP + 4 * p + 4)
                    for j in parts:
                        n = TC * p + j
                        if n >= 2:
                            pe.wait_ge(lo_ready, b * TC * NP + n - 1)
                        for t in range(TC):
                            i = pe.transpose(bank[:, 4 + j % 2, t * P:t * P + P],
                                             nd[:, p % 2, t, j, :, :].rearrange("p a d -> p (a d)"), ident[:, :])
                        i.then_inc(tr_ready, 1)

                def scores(p, h, k):
                    if h == 0 and k == 0:
                        pe.wait_ge(lo_ready, b * TC * NP + TC * p + TC)
                    n = (2 * p + h) * TC + k
                    if n >= 2:
                        pe.wait_ge(tanh_ready, b * H * TC + n - 1)
                    kt = KT[:, p % 2, h, k * P:k * P + P]
                    pe.matmul(bank[:, k % 2, :], kt, QL[:, p % 2, h, :], start=True, stop=False)
                    pe.matmul(bank[:, k % 2, :], kt, QH[:, p % 2, h, :], start=False, stop=True).then_inc(s_ready, 1)

                def values(p, chunks):
                    for k in chunks:
                        for h in range(2):
                            n = 2 * p + h
                            if k == 0:
                                pe.wait_ge(e_ready, b * H + n + 1)
                            if k == 0 and h == 0 and p >= 1:
                                pe.wait_ge(oT_ready, b * NP + p)
                            i = pe.matmul(bank[DH * h:DH * h + DH, 6, :], raw[:, p % 4, k, 2 * P + DH * h:2 * P + DH * h + DH],
                                          E[:, n % 4, k, :], start=(k == 0), stop=(k == TC - 1))
                    if k == TC - 1:
                        i.then_inc(o_ready, 1)

                def denominators(p):
                    pe.wait_ge(es_ready, b * H + 2 * p + 2)
                    if p >= 1:
                        pe.wait_ge(rec_ready, b * NP + p)
                    for h in range(2):
                        i = pe.matmul(bank[DH * h:DH * h + DH, 7, :], g.ones[:, :], es[:, (2 * p + h) % 4, :],
                                      start=True, stop=True)
                    i.then_inc(den_ready, 1)

                project(0, range(TC))
                project(1, range(TC))
                turn(0, range(4))
                for p in range(NP):
                    for k in range(TC):
                        scores(p, 0, k)
                        if p + 2 < NP:
                            project(p + 2, (k,))
                    for k in range(TC):
                        scores(p, 1, k)
                        if p >= 1:
                            values(p - 1, (k,))
                        if p + 1 < NP:
                            turn(p + 1, (k,))
                    if p >= 1:
                        denominators(p - 1)
                values(NP - 1, range(TC))
                denominators(NP - 1)
                pe.wait_ge(wo_loaded, 16)
                pe.wait_ge(oT_ready, b * NP + NP)
                for t in range(TC):
                    for p in range(NP):
                        i = pe.matmul(bank[:, 2 + t, 0:D], oT[:, p, t * P:t * P + P], w_o[:, p, :],
                                      start=(p == 0), stop=(p == NP - 1))
                    i.then_inc(wo_ready, 1)

def l0_cross_attention(nc, g, ctx_rows, x1_t, w1_t, b1, w2_t, b2, w3_t, b3):
    SCALE = 8 ** -0.5
    NS = SC // P
    X, ident, bank = g.X, g.ident, g.bank
    with ExitStack() as c:
        def sb(name, shape, dt=F32):
            return c.enter_context(nc.sbuf_tensor("c0_" + name, shape, dt))

        def sem(name):
            return nc.alloc_semaphore("c0_" + name)

        ctx = sb("ctx", [P, B * NS, D])
        x1T = sb("x1T", [P, KC, SC])
        w1, w2, w3 = sb("w1", [P, KC, D]), sb("w2", [P, KC, D]), sb("w3", [P, KC, D])
        bias = sb("bias", [P, 2, KC])
        b3row = sb("b3row", [P, D])
        v1T = sb("v1T", [P, KC, SC])
        xT = sb("xT", [P, KC, L])
        xs = sb("xs", [P, TC, D])
        xb = sb("xb", [P, TC, D])
        mx, nm = sb("mx", [P, TC]), sb("nm", [P, TC])
        sums, rsum = sb("sums", [P, TC]), sb("rsum", [P, TC])
        E = sb("E", [P, 2, SC])
        ET = sb("ET", [P, 2, NS, P])
        v5 = sb("v5", [P, 2, D])
        v5T = sb("v5T", [P, KC, L])
        v6T = sb("v6T", [P, KC, L])
        ln = Norm(nc, c, "c0_ln")

        w_loaded, ctx_loaded, small_loaded = sem("w_loaded"), sem("ctx_loaded"), sem("small_loaded")
        v1_ready, v1_kept = sem("v1_ready"), sem("v1_kept")
        xs_ready = sem("xs_ready")
        xtp_ready, xT_ready, xb_ready = sem("xtp_ready"), sem("xT_ready"), sem("xb_ready")
        s_ready, mx_ready, nm_ready, e_ready = sem("s_ready"), sem("mx_ready"), sem("nm_ready"), sem("e_ready")
        et_ready = sem("et_ready")
        et0_kept, et1_kept = sem("et0_kept"), sem("et1_kept")
        av_ready, rsum_ready, v5_ready = sem("av_ready"), sem("rsum_ready"), sem("v5_ready")
        v5t_ready, v5T_ready = sem("v5t_ready"), sem("v5T_ready")
        v6_ready, v6T_ready, v7_ready = sem("v6_ready"), sem("v6T_ready"), sem("v7_ready")

        block = c.enter_context(nc.Block())

        @block.sync
        def _(sp):
            sp.dma_start(w1[:, :, :], w1_t.rearrange("(k p) n -> p k n", p=P)).then_inc(w_loaded, 16)
            sp.dma_start(x1T[:, :, :], x1_t.rearrange("(k p) n -> p k n", p=P)).then_inc(w_loaded, 16)
            sp.dma_start(w2[:, :, :], w2_t.rearrange("(k p) n -> p k n", p=P)).then_inc(w_loaded, 16)
            sp.dma_start(w3[:, :, :], w3_t.rearrange("(k p) n -> p k n", p=P)).then_inc(w_loaded, 16)
            sp.dma_start(ctx[:, :, :], ctx_rows.rearrange("b (k p) d -> p (b k) d", p=P)).then_inc(ctx_loaded, 16)
            sp.wait_ge(w_loaded, 64)
            sp.wait_ge(ctx_loaded, 16)

        @block.gpsimd
        def _(pool):
            pool.wait_ge(small_loaded, 48)
            with pool.Fori(0, B) as b:
                for t in range(TC):
                    pool.tensor_tensor(xb[:, t, :], X[:, b * TC + t, :], b3row[:, :], ALU.add).then_inc(xb_ready, 1)
                ln.rstd(g, pool, b)

        @block.scalar
        def _(act):
            act.dma_start(bias[:, 0, :], b1).then_inc(small_loaded, 16)
            act.dma_start(bias[:, 1, :], b2).then_inc(small_loaded, 16)
            act.dma_start(b3row[:, :], b3.partition_broadcast(P)).then_inc(small_loaded, 16)
            act.wait_ge(small_loaded, 48)
            for n in range(4):
                e, s = n // 2, n % 2
                act.wait_ge(v1_ready, n + 1)
                act.activation(v1T[:, e, s * 512:s * 512 + 512], bank[:, n, :], ACT.Identity,
                               bias=bias[:, 0, e:e + 1]).then_inc(v1_kept, 1)
            with act.Fori(0, B) as b:
                for kc in range(KC):
                    act.wait_ge(xtp_ready, b * KC + kc + 1)
                    act.activation(xT[:, kc, :], bank[:, 6 + kc, :], ACT.Copy).then_inc(xT_ready, 1)

                def exps(t):
                    if t >= 2:
                        act.wait_ge(et_ready, b * 2 * TC + 2 * (t - 1))
                    act.wait_ge(nm_ready, b * TC + t + 1)
                    s = bank[:, 2 * (t % 2):2 * (t % 2) + 2, :].rearrange("p a n -> p (a n)")
                    act.activation(E[:, t % 2, :], s, ACT.Exp, bias=nm[:, t:t + 1], scale=SCALE,
                                   accum_out=sums[:, t:t + 1]).then_inc(e_ready, 1)

                def keep(t):
                    if t >= 2:
                        act.wait_ge(av_ready, b * TC + t - 1)
                    act.wait_ge(et_ready, b * 2 * TC + 2 * t + 1)
                    act.activation(ET[:, t % 2, 0:4, :].rearrange("p k n -> p (k n)"), bank[:, 4, :], ACT.Copy).then_inc(et0_kept, 1)

                def weighted(t):
                    act.wait_ge(av_ready, b * TC + t + 1)
                    act.wait_ge(rsum_ready, b * TC + t + 1)
                    if t >= 2:
                        act.wait_ge(v5t_ready, b * TC + t - 1)
                    act.activation(v5[:, t % 2, :], bank[:, 6, 0:D], ACT.Copy, scale=rsum[:, t:t + 1]).then_inc(v5_ready, 1)

                exps(0)
                exps(1)
                for t in range(TC):
                    keep(t)
                    if t + 2 < TC:
                        exps(t + 2)
                    weighted(t)
                for e in range(KC):
                    act.wait_ge(v6_ready, b * KC + e + 1)
                    act.activation(v6T[:, e, :], bank[:, e, :], ACT.Identity, bias=bias[:, 1, e:e + 1]).then_inc(v6T_ready, 1)

        @block.vector
        def _(dve):
            dve.sem_inc(ln.banks_free, TC)
            dve.tensor_copy(xs[:, :, :], X[:, 0:TC, :]).then_inc(xs_ready, 1)
            with dve.Fori(0, B) as b:
                def maxima(t):
                    dve.wait_ge(s_ready, b * TC + t + 1)
                    s = bank[:, 2 * (t % 2):2 * (t % 2) + 2, :]
                    dve.tensor_reduce(mx[:, t:t + 1], s, AX.XY, ALU.max).then_inc(mx_ready, 1)
                    dve.wait_ge(mx_ready, b * TC + t + 1)
                    dve.tensor_scalar(nm[:, t:t + 1], mx[:, t:t + 1], -SCALE, None, ALU.mult).then_inc(nm_ready, 1)

                def keep(t):
                    if t >= 2:
                        dve.wait_ge(av_ready, b * TC + t - 1)
                    dve.wait_ge(et_ready, b * 2 * TC + 2 * t + 2)
                    dve.tensor_copy(ET[:, t % 2, 4:8, :].rearrange("p k n -> p (k n)"), bank[:, 5, :]).then_inc(et1_kept, 1)
                    dve.wait_ge(e_ready, b * TC + t + 1)
                    dve.reciprocal(rsum[:, t:t + 1], sums[:, t:t + 1]).then_inc(rsum_ready, 1)

                def keep_v5T(t):
                    dve.wait_ge(v5t_ready, b * TC + t + 1)
                    dve.tensor_copy(v5T[:, :, t * P:t * P + P], bank[:, 7, 0:2 * P].rearrange("p (k n) -> p k n", k=KC)).then_inc(v5T_ready, 1)

                maxima(0)
                maxima(1)
                for t in range(TC):
                    keep(t)
                    if t >= 1:
                        keep_v5T(t - 1)
                    if t + 2 < TC:
                        maxima(t + 2)
                keep_v5T(TC - 1)
                dve.wait_ge(xb_ready, b * TC + TC)
                for t in range(TC):
                    dve.wait_ge(v7_ready, b * TC + t + 1)
                    dve.tensor_tensor(ln.t[:, t, :], bank[:, 2 + t, 0:D], xb[:, t, :], ALU.add).then_inc(ln.sum_ready, 1)
                dve.wait_ge(ln.sum_ready, b * TC + TC)
                dve.sem_inc(ln.banks_free, TC)
                dve.tensor_copy(xs[:, :, :], X[:, ds((b + 1) % B * TC, TC), :]).then_inc(xs_ready, 1)
                ln.stats(g, dve, b)
                ln.apply(dve, lambda t: X[:, b * TC + t, :], b)

        @block.tensor
        def _(pe):
            pe.wait_ge(w_loaded, 64)
            for n in range(4):
                e, s = n // 2, n % 2
                for kc in range(KC):
                    i = pe.matmul(bank[:, n, :], w1[:, kc, e * P:e * P + P], x1T[:, kc, s * 512:s * 512 + 512],
                                  start=(kc == 0), stop=(kc == KC - 1))
                i.then_inc(v1_ready, 1)
            pe.wait_ge(v1_kept, 4)
            pe.wait_ge(ctx_loaded, 16)
            with pe.Fori(0, B) as b:
                pe.wait_ge(ln.banks_free, b * TC + TC)
                pe.wait_ge(xs_ready, b + 1)
                for kc in range(KC):
                    for t in range(TC):
                        i = pe.transpose(bank[:, 6 + kc, t * P:t * P + P], xs[:, t, kc * P:kc * P + P], ident[:, :])
                    i.then_inc(xtp_ready, 1)
                pe.wait_ge(xT_ready, b * KC + KC)

                def scores(t):
                    if t >= 2:
                        pe.wait_ge(e_ready, b * TC + t - 1)
                    for s in range(2):
                        for kc in range(KC):
                            i = pe.matmul(bank[:, 2 * (t % 2) + s, :], xT[:, kc, t * P:t * P + P],
                                          v1T[:, kc, s * 512:s * 512 + 512], start=(kc == 0), stop=(kc == KC - 1))
                    i.then_inc(s_ready, 1)

                def turn(t):
                    pe.wait_ge(e_ready, b * TC + t + 1)
                    for half in range(2):
                        if t >= 1:
                            pe.wait_ge(et1_kept if half else et0_kept, b * TC + t)
                        for k in range(4):
                            s = (4 * half + k) * P
                            i = pe.transpose(bank[:, 4 + half, k * P:k * P + P], E[:, t % 2, s:s + P], ident[:, :])
                        i.then_inc(et_ready, 1)

                def values(t):
                    pe.wait_ge(et0_kept, b * TC + t + 1)
                    pe.wait_ge(et1_kept, b * TC + t + 1)
                    if t >= 1:
                        pe.wait_ge(v5_ready, b * TC + t)
                    for k in range(NS):
                        i = pe.matmul(bank[:, 6, 0:D], ET[:, t % 2, k, :], ctx[:, b * NS + k, :],
                                      start=(k == 0), stop=(k == NS - 1))
                    i.then_inc(av_ready, 1)

                def turn_v5(t):
                    pe.wait_ge(v5_ready, b * TC + t + 1)
                    if t >= 1:
                        pe.wait_ge(v5T_ready, b * TC + t)
                    for kc in range(KC):
                        i = pe.transpose(bank[:, 7, kc * P:kc * P + P], v5[:, t % 2, kc * P:kc * P + P], ident[:, :])
                    i.then_inc(v5t_ready, 1)

                scores(0)
                scores(1)
                for t in range(TC):
                    turn(t)
                    if t >= 1:
                        turn_v5(t - 1)
                    if t + 2 < TC:
                        scores(t + 2)
                    values(t)
                turn_v5(TC - 1)
                pe.wait_ge(v5T_ready, b * TC + TC)
                for e in range(KC):
                    for kc in range(KC):
                        i = pe.matmul(bank[:, e, :], w2[:, kc, e * P:e * P + P], v5T[:, kc, :],
                                      start=(kc == 0), stop=(kc == KC - 1))
                    i.then_inc(v6_ready, 1)
                pe.wait_ge(v6T_ready, b * KC + KC)
                for t in range(TC):
                    for kc in range(KC):
                        i = pe.matmul(bank[:, 2 + t, 0:D], v6T[:, kc, t * P:t * P + P], w3[:, kc, :],
                                      start=(kc == 0), stop=(kc == KC - 1))
                    i.then_inc(v7_ready, 1)



NT = B * TC
FF = 1024
FC = FF // P
BLOCK = 256
BC = BLOCK // P


def most_blocks(experts):
    return (2 * B * L + experts * (BLOCK - 1)) // BLOCK


class Routing:

    def __init__(self, nc, c, name, experts):
        self.blocks = most_blocks(experts)
        self.weight = c.enter_context(nc.sbuf_tensor(f"{name}_weight", [P, 2, NT, 1], F32))
        self.slot = c.enter_context(nc.sbuf_tensor(f"{name}_slot", [P, 2, NT], mybir.dt.uint32))
        self.block_expert = c.enter_context(nc.sbuf_tensor(f"{name}_block_expert", [P, self.blocks], mybir.dt.int32))


class TopTwo:

    def __init__(self, nc, c, name):
        self.score = c.enter_context(nc.sbuf_tensor(f"{name}_score", [P, NT, 8], F32))
        self.top = c.enter_context(nc.sbuf_tensor(f"{name}_top", [P, NT, 8], F32))
        self.index = c.enter_context(nc.sbuf_tensor(f"{name}_index", [P, NT, 8], mybir.dt.uint32))
        self.index_f = c.enter_context(nc.sbuf_tensor(f"{name}_index_f", [P, NT, 2], F32))
        self.expert = c.enter_context(nc.sbuf_tensor(f"{name}_expert", [P, 8], mybir.dt.int32))
        self.expert_f = c.enter_context(nc.sbuf_tensor(f"{name}_expert_f", [P, 8], F32))
        self.pick = c.enter_context(nc.sbuf_tensor(f"{name}_pick", [P, 2, NT, 8], F32))
        self.numbered = nc.alloc_semaphore(f"{name}_numbered")
        self.top_ready = nc.alloc_semaphore(f"{name}_top_ready")
        self.index_ready = nc.alloc_semaphore(f"{name}_index_ready")
        self.pick_ready = nc.alloc_semaphore(f"{name}_pick_ready")
        self.gated = nc.alloc_semaphore(f"{name}_gated")

    def number_experts(self, pool):
        pool.iota(self.expert[:, :], pattern=[[1, 8]], base=0, channel_multiplier=0).then_inc(self.numbered, 1)

    def find(self, dve):
        for n in range(NT):
            dve.max(self.top[:, n, :], self.score[:, n, :]).then_inc(self.top_ready, 1)
        for n in range(NT):
            dve.wait_ge(self.top_ready, n + 1)
            dve.max_index(self.index[:, n, :], self.top[:, n, :], self.score[:, n, :]).then_inc(self.index_ready, 1)
        dve.wait_ge(self.index_ready, NT)
        dve.tensor_copy(self.index_f[:, :, :], self.index[:, :, 0:2]).then_inc(self.index_ready, 1)
        dve.wait_ge(self.numbered, 1)
        dve.tensor_copy(self.expert_f[:, :], self.expert[:, :]).then_inc(self.index_ready, 1)
        dve.wait_ge(self.index_ready, NT + 2)
        for k in range(2):
            dve.tensor_tensor(self.pick[:, k, :, :], self.expert_f[:, None, :].to_broadcast([P, NT, 8]),
                              self.index_f[:, :, k:k + 1].to_broadcast([P, NT, 8]), ALU.is_equal).then_inc(self.pick_ready, 1)


class Slots:

    def __init__(self, nc, c, name, experts, routing):
        def sb(n, shape, dt=F32):
            return c.enter_context(nc.sbuf_tensor(f"{name}_{n}", shape, dt))

        self.experts, self.routing = experts, routing
        NB = routing.blocks
        self.chosen = sb("chosen", [P, NT, 8])
        self.before = sb("before", [P, P])
        self.all = sb("all", [P, P])
        self.cum = sb("cum", [P, NT + 1, 8])
        self.number = sb("number", [P, NB], mybir.dt.int32)
        self.number_f = sb("number_f", [P, NB])
        self.full = sb("full", [P, 8])
        self.started = sb("started", [P, 8, 8])
        self.blocks = sb("blocks", [P, 8])
        self.end = sb("end", [P, 8])
        self.base = sb("base", [P, 8])
        self.past = sb("past", [P, NB, 8])
        self.expert_of = sb("expert_of", [P, NB])
        self.position = sb("position", [P, NT, 8])
        self.picked = sb("picked", [P, 2, NT, 8])
        self.slot_f = sb("slot_f", [P, 2, NT])
        self.made = nc.alloc_semaphore(f"{name}_made")
        self.chosen_ready = nc.alloc_semaphore(f"{name}_chosen_ready")
        self.counted = nc.alloc_semaphore(f"{name}_counted")
        self.step = nc.alloc_semaphore(f"{name}_step")

    def constants(self, pool):
        pool.memset(self.all[:, :], 1.0).then_inc(self.made, 1)
        pool.memset(self.before[:, :], 1.0).then_inc(self.made, 1)
        pool.iota(self.number[:, :], pattern=[[1, self.routing.blocks]], base=0, channel_multiplier=0).then_inc(self.made, 1)
        pool.wait_ge(self.made, 2)
        pool.affine_select(out=self.before[:, :], in_=self.before[:, :], compare_op=ALU.is_ge, fill=0.0,
                           base=-1, pattern=[[1, P]], channel_multiplier=-1).then_inc(self.made, 1)

    def count(self, g, pe):
        pe.wait_ge(self.made, 4)
        pe.wait_ge(self.chosen_ready, 1)
        for n, ones in ((0, self.before), (1, self.all)):
            i = pe.matmul(g.bank[:, 3, P * n:P * n + P], ones[:, :], self.chosen[:, :, :].rearrange("p n e -> p (n e)"),
                          start=True, stop=True)
        i.then_inc(self.counted, 1)

    def assign(self, g, dve, top):
        NB, steps = self.routing.blocks, [0]

        def step(instruction):
            instruction.then_inc(self.step, 1)
            steps[0] += 1
            dve.wait_ge(self.step, steps[0])

        dve.wait_ge(top.pick_ready, 2)
        dve.tensor_tensor(self.chosen[:, :, :], top.pick[:, 0, :, :], top.pick[:, 1, :, :], ALU.add).then_inc(self.chosen_ready, 1)
        step(dve.memset(self.cum[:, 0, :], 0.0))
        step(dve.tensor_scalar(self.full[:, :], top.expert_f[:, :], float(BLOCK), None, ALU.mult))
        dve.wait_ge(self.made, 4)
        step(dve.tensor_copy(self.number_f[:, :], self.number[:, :]))
        dve.wait_ge(self.counted, 1)
        before = g.bank[:, 3, 0:P].rearrange("p (n e) -> p n e", e=8)
        whole = g.bank[:, 3, P:2 * P].rearrange("p (n e) -> p n e", e=8)
        for n in range(NT):
            step(dve.tensor_tensor(self.cum[:, n + 1, :], self.cum[:, n, :], whole[:, n, :], ALU.add))
        step(dve.tensor_tensor(self.started[:, :, :], self.cum[:, NT, :, None].to_broadcast([P, 8, 8]),
                               self.full[:, None, :].to_broadcast([P, 8, 8]), ALU.is_gt))
        step(dve.tensor_reduce(self.blocks[:, :], self.started[:, :, :], AX.X, ALU.add))
        step(dve.tensor_copy(self.end[:, 0:1], self.blocks[:, 0:1]))
        for e in range(1, 8):
            step(dve.tensor_tensor(self.end[:, e:e + 1], self.end[:, e - 1:e], self.blocks[:, e:e + 1], ALU.add))
        step(dve.tensor_tensor(self.base[:, :], self.end[:, :], self.blocks[:, :], ALU.subtract))
        step(dve.tensor_scalar(self.base[:, :], self.base[:, :], float(BLOCK), None, ALU.mult))
        step(dve.tensor_tensor(self.past[:, :, :], self.number_f[:, :, None].to_broadcast([P, NB, 8]),
                               self.end[:, None, :].to_broadcast([P, NB, 8]), ALU.is_ge))
        step(dve.tensor_reduce(self.expert_of[:, :], self.past[:, :, :], AX.X, ALU.add))
        step(dve.tensor_scalar(self.routing.block_expert[:, :], self.expert_of[:, :], float(self.experts - 1), None, ALU.min))
        step(dve.tensor_tensor(self.position[:, :, :], before, self.cum[:, 0:NT, :], ALU.add))
        step(dve.tensor_tensor(self.position[:, :, :], self.position[:, :, :], self.base[:, None, :].to_broadcast([P, NT, 8]), ALU.add))
        for k in range(2):
            step(dve.tensor_tensor(self.picked[:, k, :, :], top.pick[:, k, :, :], self.position[:, :, :], ALU.mult))
        step(dve.tensor_reduce(self.slot_f[:, :, :], self.picked[:, :, :, :], AX.X, ALU.add))
        step(dve.tensor_copy(self.routing.slot[:, :, :], self.slot_f[:, :, :]))


class TurnX:

    def __init__(self, nc, c, name):
        self.xs = c.enter_context(nc.sbuf_tensor(f"{name}_xs", [P, TC, D], F32))
        self.xTb = c.enter_context(nc.sbuf_tensor(f"{name}_xTb", [P, KC, L], F32))
        self.xs_ready = nc.alloc_semaphore(f"{name}_xs_ready")
        self.turned = nc.alloc_semaphore(f"{name}_turned")
        self.xTb_ready = nc.alloc_semaphore(f"{name}_xTb_ready")

    def copy(self, g, dve, b):
        dve.tensor_copy(self.xs[:, :, :], g.X[:, ds(b % B * TC, TC), :]).then_inc(self.xs_ready, 1)

    def turn(self, g, pe, b):
        pe.wait_ge(self.xs_ready, b + 1)
        for kc in range(KC):
            for t in range(TC):
                i = pe.transpose(g.bank[:, kc, t * P:t * P + P], self.xs[:, t, kc * P:kc * P + P], g.ident[:, :])
            i.then_inc(self.turned, 1)

    def take(self, g, dve, b):
        for kc in range(KC):
            dve.wait_ge(self.turned, b * KC + kc + 1)
            dve.tensor_copy(self.xTb[:, kc, :], g.bank[:, kc, :]).then_inc(self.xTb_ready, 1)


def l0_router(nc, g, routing, router_w):
    E = 8
    with ExitStack() as c:
        def sb(name, shape, dt=F32):
            return c.enter_context(nc.sbuf_tensor("r0_" + name, shape, dt))

        def sem(name):
            return nc.alloc_semaphore("r0_" + name)

        w = sb("w", [P, KC, E])
        diff, weight = sb("diff", [P, NT, 1]), routing.weight
        den = sb("den", [P, NT, 1])
        turn, top = TurnX(nc, c, "r0"), TopTwo(nc, c, "r0_top")
        slots = Slots(nc, c, "r0_slots", E, routing)
        w_loaded, logits_ready, logits_kept = sem("w_loaded"), sem("logits_ready"), sem("logits_kept")
        diff_ready, exp_ready, weight_ready = sem("diff_ready"), sem("exp_ready"), sem("weight_ready")
        block = c.enter_context(nc.Block())

        @block.sync
        def _(sp):
            sp.dma_start(w[:, :, :], router_w.rearrange("(k p) e -> p k e", p=P)).then_inc(w_loaded, 16)
            sp.wait_ge(w_loaded, 16)

        @block.gpsimd
        def _(pool):
            top.number_experts(pool)
            slots.constants(pool)

        @block.scalar
        def _(act):
            act.wait_ge(diff_ready, 1)
            act.activation(weight[:, 1, :, :], diff[:, :, :], ACT.Exp).then_inc(exp_ready, 1)

        @block.tensor
        def _(pe):
            pe.wait_ge(w_loaded, 16)
            with pe.Fori(0, B) as b:
                turn.turn(g, pe, b)
                pe.wait_ge(turn.xTb_ready, b * KC + KC)
                pe.wait_ge(logits_kept, b + 1)
                for t in range(TC):
                    for kc in range(KC):
                        i = pe.matmul(g.bank[:, 2, t * E:t * E + E], turn.xTb[:, kc, t * P:t * P + P], w[:, kc, :],
                                      start=(kc == 0), stop=(kc == KC - 1))
                i.then_inc(logits_ready, 1)
            slots.count(g, pe)

        @block.vector
        def _(dve):
            dve.sem_inc(logits_kept, 1)
            turn.copy(g, dve, 0)
            with dve.Fori(0, B) as b:
                turn.take(g, dve, b)
                turn.copy(g, dve, b + 1)
                dve.wait_ge(logits_ready, b + 1)
                dve.tensor_copy(top.score[:, ds(b * TC, TC), :],
                                g.bank[:, 2, 0:TC * E].rearrange("p (t e) -> p t e", e=E)).then_inc(logits_kept, 1)
            dve.wait_ge(logits_kept, B + 1)
            top.find(dve)
            dve.tensor_tensor(diff[:, :, :], top.top[:, :, 1:2], top.top[:, :, 0:1], ALU.subtract).then_inc(diff_ready, 1)
            dve.wait_ge(exp_ready, 1)
            dve.tensor_scalar(den[:, :, :], weight[:, 1, :, :], 1.0, None, ALU.add).then_inc(weight_ready, 1)
            dve.wait_ge(weight_ready, 1)
            dve.reciprocal(weight[:, 0, :, :], den[:, :, :]).then_inc(weight_ready, 1)
            dve.wait_ge(weight_ready, 2)
            dve.tensor_tensor(weight[:, 1, :, :], weight[:, 1, :, :], weight[:, 0, :, :], ALU.mult).then_inc(weight_ready, 1)
            dve.wait_ge(weight_ready, 3)
            slots.assign(g, dve, top)


def l1_router(nc, g, routing, rw1, rb1, rw2, rb2):
    E, RC = 4, 4
    with ExitStack() as c:
        def sb(name, shape, dt=F32):
            return c.enter_context(nc.sbuf_tensor("r1_" + name, shape, dt))

        def sem(name):
            return nc.alloc_semaphore("r1_" + name)

        w1 = sb("w1", [P, KC, RC * P])
        b1 = sb("b1", [P, RC])
        w2 = sb("w2", [P, RC, E])
        b2row = sb("b2row", [P, E])
        rh = sb("rh", [P, RC, L])
        logits = sb("logits", [P, NT, E])
        mx, sub, ex = sb("mx", [P, NT]), sb("sub", [P, NT, E]), sb("ex", [P, NT, E])
        sums, rsum = sb("sums", [P, NT]), sb("rsum", [P, NT])
        turn, top = TurnX(nc, c, "r1"), TopTwo(nc, c, "r1_top")
        slots = Slots(nc, c, "r1_slots", E, routing)
        w_loaded, h_ready, rh_ready = sem("w_loaded"), sem("h_ready"), sem("rh_ready")
        logits_ready, logits_kept, padded = sem("logits_ready"), sem("logits_kept"), sem("padded")
        step_ready, exp_ready = sem("step_ready"), sem("exp_ready")
        block = c.enter_context(nc.Block())

        @block.sync
        def _(sp):
            sp.dma_start(w1[:, :, :], rw1.rearrange("(k p) n -> p k n", p=P)).then_inc(w_loaded, 16)
            sp.dma_start(w2[:, :, :], rw2.rearrange("(k p) e -> p k e", p=P)).then_inc(w_loaded, 16)
            sp.dma_start(b1[:, :], rb1).then_inc(w_loaded, 16)
            sp.dma_start(b2row[:, :], rb2.partition_broadcast(P)).then_inc(w_loaded, 16)
            sp.wait_ge(w_loaded, 64)

        @block.gpsimd
        def _(pool):
            top.number_experts(pool)
            pool.memset(top.score[:, :, :], -1.0).then_inc(padded, 1)
            slots.constants(pool)

        @block.scalar
        def _(act):
            act.wait_ge(w_loaded, 64)
            with act.Fori(0, B) as b:
                for r in range(RC):
                    if r == 0:
                        act.wait_ge(logits_kept, b + 1)
                    act.wait_ge(h_ready, b * RC + r + 1)
                    act.activation(rh[:, r, :], g.bank[:, 4 + r, :], ACT.Gelu, bias=b1[:, r:r + 1]).then_inc(rh_ready, 1)
            act.wait_ge(step_ready, 2)
            act.activation(ex[:, :, :], sub[:, :, :], ACT.Exp).then_inc(exp_ready, 1)

        @block.tensor
        def _(pe):
            pe.wait_ge(w_loaded, 64)
            with pe.Fori(0, B) as b:
                turn.turn(g, pe, b)
                pe.wait_ge(turn.xTb_ready, b * KC + KC)
                pe.wait_ge(logits_kept, b + 1)
                for r in range(RC):
                    for kc in range(KC):
                        i = pe.matmul(g.bank[:, 4 + r, :], w1[:, kc, r * P:r * P + P], turn.xTb[:, kc, :],
                                      start=(kc == 0), stop=(kc == KC - 1))
                    i.then_inc(h_ready, 1)
                pe.wait_ge(rh_ready, b * RC + RC)
                for t in range(TC):
                    for r in range(RC):
                        i = pe.matmul(g.bank[:, 2, t * E:t * E + E], rh[:, r, t * P:t * P + P], w2[:, r, :],
                                      start=(r == 0), stop=(r == RC - 1))
                i.then_inc(logits_ready, 1)
            slots.count(g, pe)

        @block.vector
        def _(dve):
            dve.sem_inc(logits_kept, 1)
            turn.copy(g, dve, 0)
            dve.wait_ge(w_loaded, 64)
            with dve.Fori(0, B) as b:
                turn.take(g, dve, b)
                turn.copy(g, dve, b + 1)
                dve.wait_ge(logits_ready, b + 1)
                dve.tensor_tensor(logits[:, ds(b * TC, TC), :], g.bank[:, 2, 0:TC * E].rearrange("p (t e) -> p t e", e=E),
                                  b2row[:, None, :].to_broadcast([P, TC, E]), ALU.add).then_inc(logits_kept, 1)
            dve.wait_ge(logits_kept, B + 1)
            dve.tensor_reduce(mx[:, :], logits[:, :, :], AX.X, ALU.max).then_inc(step_ready, 1)
            dve.wait_ge(step_ready, 1)
            dve.tensor_tensor(sub[:, :, :], logits[:, :, :], mx[:, :, None].to_broadcast([P, NT, E]), ALU.subtract).then_inc(step_ready, 1)
            dve.wait_ge(exp_ready, 1)
            dve.tensor_reduce(sums[:, :], ex[:, :, :], AX.X, ALU.add).then_inc(step_ready, 1)
            dve.wait_ge(step_ready, 3)
            dve.reciprocal(rsum[:, :], sums[:, :]).then_inc(step_ready, 1)
            dve.wait_ge(step_ready, 4)
            dve.wait_ge(padded, 1)
            dve.tensor_tensor(top.score[:, :, 0:E], ex[:, :, :], rsum[:, :, None].to_broadcast([P, NT, E]), ALU.mult).then_inc(step_ready, 1)
            dve.wait_ge(step_ready, 5)
            top.find(dve)
            for k in range(2):
                dve.tensor_copy(routing.weight[:, k, :, :], top.top[:, :, k:k + 1]).then_inc(step_ready, 1)
            dve.wait_ge(step_ready, 7)
            slots.assign(g, dve, top)


def experts(nc, g, name, E, routing, w1, b1, w2, b2, gamma=None, beta=None, eps=None, out=None):
    X, bank = g.X, g.bank
    NB = routing.blocks
    normed = gamma is not None
    rows = 3 if normed else 1
    loads = 2 + rows
    row_slots = g.x_slots[0:NB * BLOCK, :].rearrange("(t p) d -> p t d", p=P)
    result_slots = g.y_slots[0:NB * BLOCK, :].rearrange("(t p) d -> p t d", p=P)
    with ExitStack() as c:
        def sb(n, shape, dt=F32):
            return c.enter_context(nc.sbuf_tensor(f"{name}_{n}", shape, dt))

        def sem(n):
            return nc.alloc_semaphore(f"{name}_{n}")

        w1s = sb("w1s", [P, KC, FF])
        w1h = sb("w1h", [P, 2, KC, FF], F32R)
        w1l = sb("w1l", [P, 2, KC, FF], F32R)
        w2s = sb("w2s", [P, 2, FC, D])
        b1s = sb("b1s", [P, 2, FC])
        row = sb("row", [P, 2, rows, D])
        xs = sb("xs", [P, 2, BC, D])
        xTh = sb("xTh", [P, 2, KC, BLOCK], F32R)
        xTl = sb("xTl", [P, 2, KC, BLOCK], F32R)
        hT = sb("hT", [P, FC, BLOCK])
        xb = sb("xb", [P, BC, D])
        r, z = sb("r", [P, BC, D]), sb("z", [P, BC, D])
        o = sb("o", [P, 2, BC, D])
        st, mv = sb("st", [P, BC, 6]), sb("mv", [P, BC, 2])
        ve, rstd = sb("ve", [P, BC]), sb("rstd", [P, BC])
        fetched = sb("fetched", [P, NT, 2, D])
        first = sb("first", [P, TC, D])
        wb = sb("wb", [P, 2, TC])
        ln = Norm(nc, c, name + "_ln")

        sent, out_stored = sem("sent"), sem("out_stored")
        x_loaded = [sem("x_loaded_even"), sem("x_loaded_odd")]
        loaded = [sem("loaded_even"), sem("loaded_odd")]
        free = [sem("free_even"), sem("free_odd")]
        stored = [sem("stored_even"), sem("stored_odd")]
        w1_loaded, w1h_ready, w1l_ready = sem("w1_loaded"), sem("w1h_ready"), sem("w1l_ready")
        turned, xTh_ready, xT_ready = sem("turned"), sem("xTh_ready"), sem("xT_ready")
        h_ready, hT_ready = sem("h_ready"), sem("hT_ready")
        out_ready, out_taken = sem("out_ready"), sem("out_taken")
        xb_ready, st_ready, mv_ready = sem("xb_ready"), sem("st_ready"), sem("mv_ready")
        ve_ready, rstd_ready, z_ready, o_ready = sem("ve_ready"), sem("rstd_ready"), sem("z_ready"), sem("o_ready")
        results_fetched = [sem(f"results_fetched_{b}") for b in range(B)]
        batch_fetched, wb_ready, first_ready = sem("batch_fetched"), sem("wb_ready"), sem("first_ready")
        block = c.enter_context(nc.Block())

        def h_bank(f):
            return bank[:, (0, 1, 3)[f % 3], 0:BLOCK]

        def each_block(engine, body):
            assert NB % 2 == 1
            with engine.Fori(0, NB // 2) as pair:
                body(pair, 0, False)
                body(pair, 1, False)
            body(NB // 2, 0, True)

        def at(pair, u, per_block, extra):
            return pair * (2 * per_block) + (u * per_block + extra)

        @block.sync
        def _(sp):
            def store(pair, u):
                sp.wait_ge(o_ready, at(pair, u, BC, BC))
                sp.dma_start(result_slots[:, ds(pair * (2 * BC) + u * BC, BC), :], o[:, u, :, :]).then_inc(stored[u], 16)

            def load_rows(pair, u):
                sp.dma_start(xs[:, u, :, :], row_slots[:, ds(pair * (2 * BC) + u * BC, BC), :]).then_inc(x_loaded[u], 16)

            def load_w1(pair, u):
                e = sp.value_load(routing.block_expert[0:1, ds(pair * 2 + u, 1)], min_val=0, max_val=E - 1)
                sp.dma_start(w1s[:, :, :], w1[ds(e, 1)].rearrange("o (k p) n -> p (o k) n", p=P)).then_inc(w1_loaded, 16)

            def load_weights(pair, u):
                e = sp.value_load(routing.block_expert[0:1, ds(pair * 2 + u, 1)], min_val=0, max_val=E - 1)
                sp.dma_start(b1s[:, u, :], b1[:, ds(e, 1), :].rearrange("p o f -> p (o f)")).then_inc(loaded[u], 16)
                sp.dma_start(w2s[:, u, :, :], w2[ds(e, 1)].rearrange("o (k p) n -> p (o k) n", p=P)).then_inc(loaded[u], 16)
                for n, v in enumerate((b2, gamma, beta)[0:rows]):
                    sp.dma_start(row[:, u, n, :], v[ds(e, 1)].rearrange("o d -> (o d)").partition_broadcast(P)).then_inc(loaded[u], 16)

            load_w1(0, 0)
            load_weights(0, 0)
            load_weights(0, 1)
            sp.wait_ge(w1l_ready, 1)
            load_w1(0, 1)
            sp.wait_ge(sent, 16 * 2 * NT)
            load_rows(0, 0)
            load_rows(0, 1)
            with sp.Fori(1, NB // 2) as pair:
                for u in range(2):
                    sp.wait_ge(w1l_ready, at(pair, u, 1, 0))
                    load_w1(pair, u)
                    sp.wait_ge(free[u], pair * 2 + 2)
                    load_rows(pair, u)
                    load_weights(pair, u)
                    store(pair - 1, u)
            sp.wait_ge(w1l_ready, NB - 1)
            load_w1(NB // 2, 0)
            sp.wait_ge(free[0], NB // 2 * 2 + 2)
            load_rows(NB // 2, 0)
            load_weights(NB // 2, 0)
            for u in range(2):
                store(NB // 2 - 1, u)
            store(NB // 2, 0)
            for u in range(2):
                sp.wait_ge(loaded[u], 16 * loads * (NB // 2 + 1 - u))
            if out is not None:
                for b in range(B):
                    sp.wait_ge(ln.x_ready, TC * b + TC)
                    sp.dma_start(out[b].rearrange("(t p) d -> p t d", p=P), X[:, b * TC:b * TC + TC, :]).then_inc(out_stored, 16)
                sp.wait_ge(out_stored, 16 * B)

        @block.scalar
        def _(act):
            def high_w1(pair, u):
                act.wait_ge(w1_loaded, at(pair, u, 16, 16))
                act.activation(w1h[:, u, :, :], w1s[:, :, :], ACT.Copy).then_inc(w1h_ready, 1)

            high_w1(0, 0)

            def body(pair, u, last):
                act.wait_ge(loaded[u], pair * (16 * loads) + 16 * loads)
                for f in range(FC):
                    act.wait_ge(h_ready, at(pair, u, FC, f + 1))
                    act.activation(hT[:, f, :], h_bank(f), ACT.Gelu, bias=b1s[:, u, f:f + 1]).then_inc(hT_ready, 1)
                if not last:
                    high_w1(pair + u, 1 - u)

            each_block(act, body)

        @block.tensor
        def _(pe):
            def turn(pair, u):
                pe.wait_ge(x_loaded[u], pair * 16 + 16)
                for kc in range(KC):
                    for t in range(BC):
                        i = pe.transpose(bank[:, 2, kc * BLOCK + t * P:kc * BLOCK + t * P + P],
                                         xs[:, u, t, kc * P:kc * P + P], g.ident[:, :])
                i.then_inc(turned, 1)

            turn(0, 0)

            def body(pair, u, last):
                pe.wait_ge(w1l_ready, at(pair, u, 1, 1))
                pe.wait_ge(xT_ready, at(pair, u, 1, 1))
                for f in range(FC):
                    if f >= 3:
                        pe.wait_ge(hT_ready, at(pair, u, FC, f - 2))
                    for kc in range(KC):
                        for n, (w, x) in enumerate(((w1l, xTh), (w1h, xTl), (w1h, xTh))):
                            i = pe.matmul(h_bank(f), w[:, u, kc, f * P:f * P + P], x[:, u, kc, :],
                                          start=(kc == 0 and n == 0), stop=(kc == KC - 1 and n == 2))
                    i.then_inc(h_ready, 1)
                pe.wait_ge(out_taken, at(pair, u, BC, BC))
                pe.wait_ge(loaded[u], pair * (16 * loads) + 16 * loads)
                for f in range(FC):
                    if f == FC // 2 and not last:
                        turn(pair + u, 1 - u)
                    pe.wait_ge(hT_ready, at(pair, u, FC, f + 1))
                    for t in range(BC):
                        i = pe.matmul(bank[:, 4 + 2 * u + t, 0:D], hT[:, f, t * P:t * P + P], w2s[:, u, f, :],
                                      start=(f == 0), stop=(f == FC - 1))
                        if f == FC - 1:
                            i.then_inc(out_ready, 1)
                pe.sem_inc(free[u], 1)

            each_block(pe, body)

        @block.gpsimd
        def _(pool):
            pool.wait_ge(g.slots_zeroed, 16)
            for n in range(NT):
                for k in range(2):
                    pool.indirect_dma_start(g.x_slots[0:NB * BLOCK, :], bass.IndirectOffsetOnAxis(ap=routing.slot[:, k, n:n + 1], axis=0),
                                            X[:, n, :], None).then_inc(sent, 16)
            pool.wait_ge(sent, 16 * 2 * NT)

            def body(pair, u, last):
                pool.wait_ge(loaded[u], pair * (16 * loads) + 16 * loads)
                pool.wait_ge(x_loaded[u], pair * 16 + 16)
                pool.wait_ge(out_taken, at(pair, u, BC, 2 * BC))
                for t in range(BC):
                    pool.tensor_tensor(xb[:, t, :], xs[:, u, t, :], row[:, u, 0, :], ALU.add).then_inc(xb_ready, 1)
                pool.wait_ge(mv_ready, at(pair, u, BC, BC))
                g.after_wait(pool)
                pool.tensor_scalar(ve[:, :], mv[:, :, 1], eps, 0.0, ALU.add, ALU.add).then_inc(ve_ready, 1)
                pool.wait_ge(ve_ready, at(pair, u, 1, 1))
                pool.tensor_tensor(rstd[:, :], ve[:, :], g.neg_half[:, 0:BC], ALU.pow).then_inc(rstd_ready, 1)

            if normed:
                each_block(pool, body)
            for u in range(2):
                pool.wait_ge(stored[u], 16 + 16 * (NB // 2 + 1 - u))
            for b in range(B):
                for t in range(TC):
                    for k in range(2):
                        n = b * TC + t
                        pool.indirect_dma_start(fetched[:, n, k, :], None, g.y_slots[0:NB * BLOCK, :],
                                                bass.IndirectOffsetOnAxis(ap=routing.slot[:, k, n:n + 1], axis=0)).then_inc(results_fetched[b], 16)
                if b >= 1:
                    pool.wait_ge(results_fetched[b - 1], 16 * 2 * TC)
                    pool.sem_inc(batch_fetched, 1)
                    ln.rstd(g, pool, b - 1)
            pool.wait_ge(results_fetched[B - 1], 16 * 2 * TC)
            pool.sem_inc(batch_fetched, 1)
            ln.rstd(g, pool, B - 1)

        @block.vector
        def _(dve):
            dve.sem_inc(out_taken, 2 * BC)
            for u in range(2):
                dve.sem_inc(free[u], 2)
                dve.sem_inc(stored[u], 16)

            def take_xT(pair, u):
                dve.wait_ge(turned, at(pair, u, 1, 1))
                high = xTh[:, u, :, :].rearrange("p k n -> p (k n)")
                dve.tensor_copy(high, bank[:, 2, :]).then_inc(xTh_ready, 1)
                dve.wait_ge(xTh_ready, at(pair, u, 1, 1))
                dve.tensor_tensor(xTl[:, u, :, :].rearrange("p k n -> p (k n)"), bank[:, 2, :], high.bitcast(F32),
                                  ALU.subtract).then_inc(xT_ready, 1)

            def low_w1(pair, u):
                dve.wait_ge(w1h_ready, at(pair, u, 1, 1))
                dve.tensor_tensor(w1l[:, u, :, :], w1s[:, :, :], w1h[:, u, :, :].bitcast(F32), ALU.subtract).then_inc(w1l_ready, 1)

            low_w1(0, 0)
            take_xT(0, 0)

            def body(pair, u, last):
                if not last:
                    low_w1(pair + u, 1 - u)
                    take_xT(pair + u, 1 - u)
                dve.wait_ge(loaded[u], pair * (16 * loads) + 16 * loads)
                if not normed:
                    dve.wait_ge(stored[u], pair * 16 + 16)
                for t in range(BC):
                    dve.wait_ge(out_ready, at(pair, u, BC, t + 1))
                    if normed:
                        dve.wait_ge(xb_ready, at(pair, u, BC, t + 1))
                        dve.tensor_tensor(r[:, t, :], bank[:, 4 + 2 * u + t, 0:D], xb[:, t, :], ALU.add).then_inc(out_taken, 1)
                    else:
                        dve.tensor_tensor(o[:, u, t, :], bank[:, 4 + 2 * u + t, 0:D], row[:, u, 0, :], ALU.add).then_inc(o_ready, 1)
                if not normed:
                    dve.wait_ge(o_ready, at(pair, u, BC, BC))
                    dve.sem_inc(out_taken, BC)
                else:
                    for t in range(BC):
                        dve.wait_ge(out_taken, at(pair, u, BC, 2 * BC + t + 1))
                        dve.bn_stats(st[:, t, :], r[:, t, :]).then_inc(st_ready, 1)
                    for t in range(BC):
                        dve.wait_ge(st_ready, at(pair, u, BC, t + 1))
                        g.after_wait(dve)
                        dve.bn_aggr(mv[:, t, :], st[:, t, :]).then_inc(mv_ready, 1)
                    for t in range(BC):
                        dve.wait_ge(mv_ready, at(pair, u, BC, t + 1))
                        dve.scalar_tensor_tensor(out=z[:, t, :], in0=r[:, t, :], scalar=mv[:, t, 0:1], in1=row[:, u, 1, :],
                                                 op0=ALU.subtract, op1=ALU.mult).then_inc(z_ready, 1)
                    dve.wait_ge(rstd_ready, at(pair, u, 1, 1))
                    dve.wait_ge(stored[u], pair * 16 + 16)
                    for t in range(BC):
                        dve.wait_ge(z_ready, at(pair, u, BC, t + 1))
                        dve.scalar_tensor_tensor(out=o[:, u, t, :], in0=z[:, t, :], scalar=rstd[:, t:t + 1], in1=row[:, u, 2, :],
                                                 op0=ALU.mult, op1=ALU.add).then_inc(o_ready, 1)
                    dve.wait_ge(o_ready, at(pair, u, BC, BC))
                dve.sem_inc(free[u], 1)

            each_block(dve, body)
            with dve.Fori(0, B) as b:
                dve.tensor_copy(wb[:, :, :], routing.weight[:, :, ds(b * TC, TC), 0]).then_inc(wb_ready, 1)
                dve.wait_ge(wb_ready, b + 1)
                dve.wait_ge(batch_fetched, b + 1)
                for t in range(TC):
                    dve.scalar_tensor_tensor(out=first[:, t, :], in0=fetched[:, b * TC + t, 0, :], scalar=wb[:, 0, t:t + 1],
                                             in1=X[:, b * TC + t, :], op0=ALU.mult, op1=ALU.add).then_inc(first_ready, 1)
                for t in range(TC):
                    dve.wait_ge(first_ready, b * TC + t + 1)
                    dve.scalar_tensor_tensor(out=ln.t[:, t, :], in0=fetched[:, b * TC + t, 1, :], scalar=wb[:, 1, t:t + 1],
                                             in1=first[:, t, :], op0=ALU.mult, op1=ALU.add).then_inc(ln.sum_ready, 1)
                ln.stats(g, dve, b)
                ln.apply(dve, lambda t: X[:, b * TC + t, :], b)
                dve.wait_ge(ln.x_ready, b * TC + TC)


def l0_ffn(nc, g, router_w, w1, b1, w2, b2, gamma, beta):
    with ExitStack() as c:
        routing = Routing(nc, c, "m0", 8)
        l0_router(nc, g, routing, router_w)
        experts(nc, g, "e0", 8, routing, w1, b1, w2, b2, gamma, beta, 1e-6)


def l1_ffn(nc, g, rw1, rb1, rw2, rb2, w1, b1, w2, b2, out):
    with ExitStack() as c:
        routing = Routing(nc, c, "m1", 4)
        l1_router(nc, g, routing, rw1, rb1, rw2, rb2)
        experts(nc, g, "e1", 4, routing, w1, b1, w2, b2, out=out)

def l1_attention(nc, g, w_qkv_t, w_c_t, mix2, index_decays_t2, mega_decays):
    H, DH, SEG = 16, 16, 64
    NR = L // SEG
    HQ = H // 4
    NG = HQ * TC
    NOISE_EPS = 1e-5
    MASKED = -1e30
    X, ident, bank = g.X, g.ident, g.bank
    with ExitStack() as c:
        def sb(name, shape, dt=F32):
            return c.enter_context(nc.sbuf_tensor("t1_" + name, shape, dt))

        def sem(name):
            return nc.alloc_semaphore("t1_" + name)

        w_qkv = sb("w_qkv", [P, KC, 3 * D])
        w_c = sb("w_c", [P, KC, D])
        ident_b = sb("ident_b", [P, P], BF16)
        mask = sb("mask", [P, 2 * P], BF16)
        in_half = sb("in_half", [P, 2])
        mix = sb("mix", [P, 4])
        dec, dec_e = sb("dec", [P, H]), sb("dec_e", [P, H])
        mega = sb("mega", [P, H])
        pw = sb("pw", [P, H, NR])
        RC = sb("RC", [P, TC, H, NR])
        xs = sb("xs", [P, TC, D])
        xT = sb("xT", [P, KC, L])
        raw = sb("raw", [P, TC, 3 * D + DH])
        q4 = sb("q4", [P, 2, H, 4, DH], F32R)
        k4 = sb("k4", [P, 2, H, 4, DH], F32R)
        qm = sb("qm", [P, 2, H, 2, DH])
        QT = sb("QT", [P, H // 2, L], F32R)
        KZ = sb("KZ", [P, H // 2, 2, L], F32R)
        QMT = sb("QMT", [P, TC, HQ, P])
        E = sb("E", [P, 2, 4, L])
        Et = sb("Et", [P, 2, 4, 2 * P])
        EtT = sb("EtT", [P, 2, 4, 2, P])
        nmax, nmax_t = sb("nmax", [P, 2, 4]), sb("nmax_t", [P, 2, 4])
        sums, rsum = sb("sums", [P, 2, 4]), sb("rsum", [P, 2, 4])
        sums_t, rsum_t, ct = sb("sums_t", [P, HQ, TC, 4]), sb("rsum_t", [P, TC, 4]), sb("ct", [P, TC, 4])
        R = sb("R", [P, 2, 4, 32])
        wn = sb("wn", [P, HQ, L])
        wsum, wse, rws = sb("wsum", [P, HQ]), sb("wse", [P, HQ]), sb("rws", [P, HQ])
        wm = wn
        wT = sb("wT", [P, HQ, TC, 4, NR])
        A = sb("A", [P, 2, TC, 4, NR, DH])
        BD = sb("BD", [P, TC, HQ, 4, DH])
        oq = sb("oq", [P, L])
        kvs = sb("kvs", [P, 2, TC, 32])
        y = sb("y", [P, TC, D])
        yT = sb("yT", [P, KC, L])
        ln = Norm(nc, c, "t1_ln")
        y2 = ln.t

        w_loaded, wc_loaded = sem("w_loaded"), sem("wc_loaded")
        small_loaded, zeroed = sem("small_loaded"), sem("zeroed")
        mask_step, mask_ready = sem("mask_step"), sem("mask_ready")
        half_ready, kz_zeroed = sem("half_ready"), sem("kz_zeroed")
        c_exp, c_step, c_ready = sem("c_exp"), sem("c_step"), sem("c_ready")
        xs_ready, xtp_ready, xT_ready = sem("xs_ready"), sem("xtp_ready"), sem("xT_ready")
        proj_ready, raw_ready = sem("proj_ready"), sem("raw_ready")
        hi_ready, lo_ready, qm_ready = sem("hi_ready"), sem("lo_ready"), sem("qm_ready")
        turn_ready = sem("turn_ready")
        kept_act, kept_dve = sem("kept_act"), sem("kept_dve")
        s_ready, st_ready = sem("s_ready"), sem("st_ready")
        nmax_ready, nmax_t_ready = sem("nmax_ready"), sem("nmax_t_ready")
        e_ready, et_ready = sem("e_ready"), sem("et_ready")
        rsum_ready, R_ready = sem("rsum_ready"), sem("R_ready")
        ett_ready, EtT_ready = sem("ett_ready"), sem("EtT_ready")
        wacc_ready, av_ready = sem("wacc_ready"), sem("av_ready")
        rt_ready, ct_ready, yt_ready = sem("rt_ready"), sem("ct_ready"), sem("yt_ready")
        wn_ready, wse_ready, rws_ready, wm_ready = sem("wn_ready"), sem("wse_ready"), sem("rws_ready"), sem("wm_ready")
        wt_ready, wT_ready = sem("wt_ready"), sem("wT_ready")
        A_pool, A_dve = sem("A_pool"), sem("A_dve")
        oq_ready, ot_ready, kvs_ready = sem("oq_ready"), sem("ot_ready"), sem("kvs_ready")
        kv_ready, BD_ready = sem("kv_ready"), sem("BD_ready")
        lin_ready, y_ready = sem("lin_ready"), sem("y_ready")
        yt2_ready, yT_ready, out_ready = sem("yt2_ready"), sem("yT_ready"), sem("out_ready")

        block = c.enter_context(nc.Block())

        def kept(n):
            t, j = divmod(n, 5)
            if j in (2, 3):
                return kept_dve, 4 * TC, 4 * t + 2 * (j - 1)
            return kept_act, 3 * TC, 3 * t + (j + 1 if j < 2 else 3)

        def chunk(n):
            return n % TC

        def lin_bank(t):
            return (2, 3, 6, 7)[t]

        def weigh_keys(engine, hq, m):
            k = raw[:, m, D + 64 * hq:D + 64 * hq + 64].rearrange("p (h d) -> p h d", d=DH)
            return engine.tensor_tensor(A[:, hq % 2, m, :, :, :], k[:, :, None, :].to_broadcast([P, 4, NR, DH]),
                                        wT[:, hq, m, :, :, None].to_broadcast([P, 4, NR, DH]), ALU.mult)

        @block.sync
        def _(sp):
            sp.dma_start(w_qkv[:, :, :], w_qkv_t.rearrange("(k p) n -> p k n", p=P)).then_inc(w_loaded, 16)
            sp.dma_start(w_c[:, :, :], w_c_t.rearrange("(k p) n -> p k n", p=P)).then_inc(wc_loaded, 16)
            sp.wait_ge(w_loaded, 16)

        @block.gpsimd
        def _(pool):
            pool.wait_ge(mask_step, 5)
            pool.affine_select(out=mask[:, P:2 * P], in_=mask[:, P:2 * P], compare_op=ALU.is_ge, fill=MASKED,
                               base=0, pattern=[[-1, P]], channel_multiplier=1).then_inc(mask_ready, 1)
            pool.affine_select(out=ident_b[:, :], in_=ident_b[:, :], compare_op=ALU.not_equal, fill=1.0,
                               base=0, pattern=[[-1, P]], channel_multiplier=1).then_inc(mask_ready, 1)
            pool.memset(R[:, :, :, NR:32], 0.0).then_inc(zeroed, 1)
            pool.memset(BD[:, :, :, :, :], 0.0).then_inc(zeroed, 1)
            pool.memset(RC[:, :, :, :], 0.0).then_inc(zeroed, 1)
            pool.memset(raw[:, :, 3 * D:3 * D + DH], 0.0).then_inc(zeroed, 1)
            pool.wait_ge(half_ready, 4)
            with pool.Fori(0, B) as b:
                for t in range(TC):
                    pool.wait_ge(raw_ready, b * 2 * TC + 2 * t + 1)
                    if t >= 2:
                        pool.wait_ge(turn_ready, b * 5 * TC + 5 * (t - 1))
                    g.after_wait(pool)
                    for half in range(2):
                        pool.tensor_scalar(qm[:, t % 2, :, half, :], raw[:, t, 0:D].rearrange("p (h d) -> p h d", d=DH),
                                           in_half[:, half:half + 1], 1.0, ALU.mult, ALU.mult).then_inc(qm_ready, 1)
                for hq in range(HQ):
                    pool.wait_ge(wT_ready, b * HQ + hq + 1)
                    if hq >= 2:
                        pool.wait_ge(kv_ready, b * HQ + hq - 1)
                    for m in range(2, TC):
                        weigh_keys(pool, hq, m).then_inc(A_pool, 1)
                ln.rstd(g, pool, b)

        @block.scalar
        def _(act):
            for half in range(2):
                rows = slice(64 * half, 64 * half + 64)
                act.dma_start(mix[rows, 0:1], mix2).then_inc(small_loaded, 16)
                act.dma_start(dec[rows, :], index_decays_t2).then_inc(small_loaded, 16)
            act.dma_start(mega[:, :], mega_decays.partition_broadcast(P)).then_inc(small_loaded, 16)
            act.wait_ge(small_loaded, 80)
            act.activation(mix[:, 1:2], mix[:, 0:1], ACT.Exp, scale=-1.0).then_inc(c_exp, 1)
            act.activation(dec_e[:, :], dec[:, :], ACT.Exp).then_inc(c_exp, 1)
            act.activation(pw[:, :, 1], mega[:, :], ACT.Exp, scale=float(SEG)).then_inc(c_exp, 1)
            with act.Fori(0, B) as b:
                for kc in range(KC):
                    act.wait_ge(xtp_ready, b * KC + kc + 1)
                    act.activation(xT[:, kc, :], bank[:, 6 + kc, :], ACT.Copy).then_inc(xT_ready, 1)

                def keep_raw(t):
                    act.wait_ge(proj_ready, b * TC + t + 1)
                    act.activation(raw[:, t, 0:2 * D], bank[:, 2 * (t % 2), :], ACT.Copy).then_inc(raw_ready, 1)
                    act.activation(raw[:, t, 2 * D:3 * D], bank[:, 2 * (t % 2) + 1, 0:D], ACT.Copy).then_inc(raw_ready, 1)

                def keep_turned(t):
                    for j in (0, 1, 4):
                        n = 5 * t + j
                        act.wait_ge(turn_ready, b * 5 * TC + n + 1)
                        src = bank[:, 4 + n % 4, :].rearrange("p (a n) -> p a n", a=4)
                        if j < 2:
                            act.activation(QT[:, 4 * j:4 * j + 4, t * P:t * P + P], src, ACT.Copy).then_inc(kept_act, 1)
                        else:
                            act.activation(QMT[:, t, :, :], src, ACT.Copy).then_inc(kept_act, 1)

                keep_raw(0)
                keep_raw(1)
                for t in range(TC):
                    keep_turned(t)
                    if t + 2 < TC:
                        keep_raw(t + 2)

                def keep_terrace(hq):
                    act.wait_ge(av_ready, b * NG + TC * (hq + 1))
                    if hq >= 1:
                        act.wait_ge(ot_ready, b * HQ + hq)
                    act.activation(oq[:, :], bank[:, 6, :], ACT.Copy).then_inc(oq_ready, 1)

                for n in range(NG):
                    i, hq = chunk(n), n // TC
                    keys = (i + 1) * P
                    window = min(keys, 2 * P)
                    if n % TC == 1 and hq >= 1:
                        keep_terrace(hq - 1)
                    for pair in range(2):
                        for h in (2 * pair, 2 * pair + 1):
                            u = 4 * n + h
                            if h == 0 and n >= 2:
                                act.wait_ge(wacc_ready, b * NG + n - 1)
                                act.wait_ge(R_ready, b * NG + n - 1)
                            act.wait_ge(nmax_ready, b * 4 * NG + u + 1)
                            act.activation(E[:, n % 2, h, 0:keys], bank[:, u % 2, 0:keys], ACT.Exp,
                                           bias=nmax[:, n % 2, h:h + 1], accum_out=sums[:, n % 2, h:h + 1]).then_inc(e_ready, 1)
                        for h in (2 * pair, 2 * pair + 1):
                            if h == 0 and n >= 2:
                                act.wait_ge(ett_ready, b * 2 * NG + 2 * (n - 1))
                            act.wait_ge(nmax_t_ready, b * 2 * NG + 2 * n + pair + 1)
                            act.activation(Et[:, n % 2, h, 0:window], bank[:, 2 + pair, 256 * (h % 2):256 * (h % 2) + window],
                                           ACT.Exp, bias=nmax_t[:, n % 2, h:h + 1],
                                           accum_out=sums_t[:, hq, i, h:h + 1]).then_inc(et_ready, 1)
                    if n % TC == 1 and hq >= 1:
                        act.wait_ge(wacc_ready, b * NG + TC * hq)
                        act.activation(wn[:, hq - 1, :], bank[:, 7, :], ACT.Copy, accum_out=wsum[:, hq - 1:hq]).then_inc(wn_ready, 1)
                keep_terrace(HQ - 1)
                act.wait_ge(wacc_ready, b * NG + NG)
                act.activation(wn[:, HQ - 1, :], bank[:, 7, :], ACT.Copy, accum_out=wsum[:, HQ - 1:HQ]).then_inc(wn_ready, 1)
                for hq in range(HQ):
                    act.wait_ge(wt_ready, b * HQ + hq + 1)
                    src = bank[:, 4 + hq % 2, :].rearrange("p (m h r) -> p m h r", m=TC, h=4)[:, :, :, 0:NR]
                    act.activation(wT[:, hq, :, :, :], src, ACT.Copy).then_inc(wT_ready, 1)
                for t in range(TC):
                    act.wait_ge(yt2_ready, b * TC + t + 1)
                    act.activation(yT[:, :, t * P:t * P + P], bank[:, 4 + t % 2, 0:2 * P].rearrange("p (k n) -> p k n", k=KC),
                                   ACT.Copy).then_inc(yT_ready, 1)

        @block.vector
        def _(dve):
            dve.sem_inc(ln.banks_free, TC)
            dve.tensor_copy(xs[:, :, :], X[:, 0:TC, :]).then_inc(xs_ready, 1)
            dve.memset(mask[:, P:2 * P], 0.0).then_inc(mask_step, 1)
            dve.memset(mask[:, 0:SEG], MASKED).then_inc(mask_step, 1)
            dve.memset(mask[0:SEG, SEG:P], 0.0).then_inc(mask_step, 1)
            dve.memset(mask[SEG:P, SEG:P], MASKED).then_inc(mask_step, 1)
            dve.memset(ident_b[:, :], 0.0).then_inc(mask_step, 1)
            for half in range(2):
                rows = slice(64 * half, 64 * half + 64)
                dve.memset(in_half[rows, half:half + 1], 1.0).then_inc(half_ready, 1)
                dve.memset(in_half[rows, 1 - half:2 - half], 0.0).then_inc(half_ready, 1)
                dve.memset(KZ[rows, :, 1 - half, :].bitcast(F32), 0.0).then_inc(kz_zeroed, 1)
            dve.wait_ge(c_exp, 3)
            dve.tensor_scalar(mix[:, 3:4], mix[:, 1:2], 1.0, None, ALU.add).then_inc(c_step, 1)
            dve.tensor_scalar(pw[:, :, 1], pw[:, :, 1], 0.0, 2.0, ALU.max, ALU.min).then_inc(c_step, 1)
            dve.memset(pw[:, :, 0], 1.0).then_inc(c_step, 1)
            dve.wait_ge(c_step, 3)
            dve.reciprocal(mix[:, 2:3], mix[:, 3:4]).then_inc(c_step, 1)
            dve.wait_ge(c_step, 4)
            dve.tensor_scalar(mix[:, 3:4], mix[:, 2:3], -1.0, 1.0, ALU.mult, ALU.add).then_inc(c_step, 1)
            for k in range(2, NR):
                dve.tensor_tensor(pw[:, :, k], pw[:, :, k - 1], pw[:, :, 1], ALU.mult).then_inc(c_step, 1)
                dve.wait_ge(c_step, 4 + k)
            dve.wait_ge(zeroed, 4)
            for r in range(NR - 1):
                i, half = divmod(r, 2)
                rows = slice(64 * half, 64 * half + 64)
                dve.tensor_tensor(RC[rows, i, :, r + 1:NR], pw[rows, :, 0:NR - 1 - r],
                                  dec_e[rows, :, None].to_broadcast([64, H, NR - 1 - r]), ALU.mult).then_inc(c_ready, 1)
            dve.wait_ge(c_ready, NR - 1)
            with dve.Fori(0, B) as b:
                def split(t):
                    dve.wait_ge(raw_ready, b * 2 * TC + 2 * t + 1)
                    if t >= 2:
                        dve.wait_ge(turn_ready, b * 5 * TC + 5 * (t - 1))
                    q = raw[:, t, 0:D].rearrange("p (h d) -> p h d", d=DH)
                    k = raw[:, t, D:2 * D].rearrange("p (h d) -> p h d", d=DH)
                    s = t % 2
                    for j in range(2):
                        dve.tensor_scalar(q4[:, s, :, 2 * j, :], q, 0.25, None, ALU.mult).then_inc(hi_ready, 1)
                        dve.tensor_copy(k4[:, s, :, j, :], k).then_inc(hi_ready, 1)
                    dve.wait_ge(hi_ready, b * 4 * TC + 4 * t + 4)
                    for j in range(2):
                        dve.scalar_tensor_tensor(out=q4[:, s, :, 2 * j + 1, :], in0=q, scalar=0.25,
                                                 in1=q4[:, s, :, 0, :].bitcast(F32), op0=ALU.mult, op1=ALU.subtract).then_inc(lo_ready, 1)
                        dve.tensor_tensor(k4[:, s, :, 2 + j, :], k, k4[:, s, :, 0, :].bitcast(F32), ALU.subtract).then_inc(lo_ready, 1)

                def keep_turned(t):
                    for j in (2, 3):
                        n = 5 * t + j
                        dve.wait_ge(turn_ready, b * 5 * TC + n + 1)
                        for half in range(2):
                            rows = slice(64 * half, 64 * half + 64)
                            src = bank[rows, 4 + n % 4, :].rearrange("p (a n) -> p a n", a=4)
                            dve.tensor_copy(KZ[rows, 4 * (j - 2):4 * (j - 2) + 4, half, t * P:t * P + P], src).then_inc(kept_dve, 1)

                split(0)
                for t in range(TC):
                    if t + 1 < TC:
                        split(t + 1)
                    keep_turned(t)

                def maxima(n):
                    i = chunk(n)
                    keys = (i + 1) * P
                    window = min(keys, 2 * P)
                    for pair in range(2):
                        for h in (2 * pair, 2 * pair + 1):
                            u = 4 * n + h
                            if h == 0 and n >= 2:
                                dve.wait_ge(e_ready, b * 4 * NG + 4 * (n - 1))
                                dve.wait_ge(et_ready, b * 4 * NG + 4 * (n - 1))
                            dve.wait_ge(s_ready, b * 4 * NG + u + 1)
                            dve.tensor_reduce(nmax[:, n % 2, h:h + 1], bank[:, u % 2, 0:keys], AX.X, ALU.max,
                                              negate=True).then_inc(nmax_ready, 1)
                        dve.wait_ge(st_ready, b * 2 * NG + 2 * n + pair + 1)
                        src = bank[:, 2 + pair, :].rearrange("p (h n) -> p h n", h=2)[:, :, 0:window]
                        dve.tensor_reduce(nmax_t[:, n % 2, 2 * pair:2 * pair + 2], src, AX.X, ALU.max,
                                          negate=True).then_inc(nmax_t_ready, 1)

                def scales(n):
                    i, hq = chunk(n), n // TC
                    dve.wait_ge(e_ready, b * 4 * NG + 4 * n + 4)
                    dve.reciprocal(rsum[:, n % 2, :], sums[:, n % 2, :]).then_inc(rsum_ready, 1)
                    dve.wait_ge(rsum_ready, b * NG + n + 1)
                    if n >= 2:
                        dve.wait_ge(wacc_ready, b * NG + n - 1)
                    dve.tensor_tensor(R[:, n % 2, :, 0:NR], RC[:, i, 4 * hq:4 * hq + 4, :],
                                      rsum[:, n % 2, :, None].to_broadcast([P, 4, NR]), ALU.mult).then_inc(R_ready, 1)

                def keep_EtT(n):
                    w = 1 if chunk(n) == 0 else 2
                    for pair in range(2):
                        if n >= 2 and pair == 0:
                            dve.wait_ge(av_ready, b * NG + n - 1)
                        dve.wait_ge(ett_ready, b * 2 * NG + 2 * n + pair + 1)
                        src = bank[:, 4 + pair, :].rearrange("p (h w n) -> p h w n", h=2, w=2)[:, :, 0:w, :]
                        dve.tensor_copy(EtT[:, n % 2, 2 * pair:2 * pair + 2, 0:w, :], src).then_inc(EtT_ready, 1)

                def keep_terrace(hq):
                    dve.wait_ge(et_ready, b * 4 * NG + 16 * (hq + 1))
                    if hq >= 1:
                        dve.wait_ge(yt_ready, b * HQ + hq)
                    dve.reciprocal(rsum_t[:, :, :], sums_t[:, hq, :, :]).then_inc(rt_ready, 1)
                    dve.wait_ge(rt_ready, b * HQ + hq + 1)
                    dve.tensor_scalar(ct[:, :, :], rsum_t[:, :, :], mix[:, 2:3], None, ALU.mult).then_inc(ct_ready, 1)
                    dve.wait_ge(ct_ready, b * HQ + hq + 1)
                    dve.wait_ge(ot_ready, b * HQ + hq + 1)
                    src = bank[:, 6, :].rearrange("p (i h d) -> p i h d", i=TC, h=4)[:, :, :, 0:DH]
                    dve.tensor_tensor(y[:, :, 64 * hq:64 * hq + 64].rearrange("p i (h d) -> p i h d", h=4), src,
                                      ct[:, :, :, None].to_broadcast([P, TC, 4, DH]), ALU.mult).then_inc(yt_ready, 1)

                def divide(hq):
                    dve.wait_ge(wn_ready, b * HQ + hq + 1)
                    dve.tensor_scalar(wse[:, hq:hq + 1], wsum[:, hq:hq + 1], NOISE_EPS, None, ALU.add).then_inc(wse_ready, 1)
                    dve.wait_ge(wse_ready, b * HQ + hq + 1)
                    dve.reciprocal(rws[:, hq:hq + 1], wse[:, hq:hq + 1]).then_inc(rws_ready, 1)
                    dve.wait_ge(rws_ready, b * HQ + hq + 1)
                    dve.tensor_scalar(wm[:, hq, :], wn[:, hq, :], rws[:, hq:hq + 1], None, ALU.mult).then_inc(wm_ready, 1)

                for n in range(NG):
                    maxima(n)
                    if n % TC == 1 and n >= TC:
                        keep_terrace(n // TC - 1)
                    if n >= 1:
                        scales(n - 1)
                        keep_EtT(n - 1)
                    if n % TC == 2 and n >= TC:
                        divide(n // TC - 1)
                scales(NG - 1)
                keep_EtT(NG - 1)
                divide(HQ - 1)

                def keep_kv(hq):
                    dve.wait_ge(kv_ready, b * HQ + hq + 1)
                    dve.transpose(kvs[:, hq % 2, :, :].rearrange("p t e -> p (t e)"), bank[:, hq % 2, 0:P]).then_inc(kvs_ready, 1)
                    dve.wait_ge(kvs_ready, b * HQ + hq + 1)
                    for h in range(4):
                        rows = slice(32 * h, 32 * h + 32)
                        dve.tensor_copy(BD[rows, :, hq, h, :], kvs[rows, hq % 2, :, 0:DH]).then_inc(BD_ready, 1)

                for hq in range(HQ):
                    dve.wait_ge(wT_ready, b * HQ + hq + 1)
                    if hq >= 2:
                        dve.wait_ge(kv_ready, b * HQ + hq - 1)
                    for m in range(2):
                        weigh_keys(dve, hq, m).then_inc(A_dve, 1)
                    if hq == 0:
                        keep_terrace(HQ - 1)
                    else:
                        keep_kv(hq - 1)
                keep_kv(HQ - 1)
                for t in range(TC):
                    dve.wait_ge(lin_ready, b * TC + t + 1)
                    if t == 0:
                        dve.wait_ge(yt_ready, b * HQ + HQ)
                    dve.scalar_tensor_tensor(out=y2[:, t, :], in0=bank[:, lin_bank(t), 0:D], scalar=mix[:, 3:4], in1=y[:, t, :],
                                             op0=ALU.mult, op1=ALU.add).then_inc(y_ready, 1)
                for t in range(TC):
                    dve.wait_ge(out_ready, b * TC + t + 1)
                    dve.tensor_tensor(ln.t[:, t, :], bank[:, t, 0:D], xs[:, t, :], ALU.add).then_inc(ln.sum_ready, 1)
                dve.wait_ge(ln.sum_ready, b * TC + TC)
                dve.sem_inc(ln.banks_free, TC)
                dve.tensor_copy(xs[:, :, :], X[:, ds((b + 1) % B * TC, TC), :]).then_inc(xs_ready, 1)
                ln.stats(g, dve, b)
                ln.apply(dve, lambda t: X[:, b * TC + t, :], b)

        @block.tensor
        def _(pe):
            pe.wait_ge(w_loaded, 16)
            with pe.Fori(0, B) as b:
                pe.wait_ge(ln.banks_free, b * TC + TC)
                pe.wait_ge(xs_ready, b + 1)
                for kc in range(KC):
                    for t in range(TC):
                        i = pe.transpose(bank[:, 6 + kc, t * P:t * P + P], xs[:, t, kc * P:kc * P + P], ident[:, :])
                    i.then_inc(xtp_ready, 1)
                pe.wait_ge(xT_ready, b * KC + KC)

                def project(t):
                    if t >= 2:
                        pe.wait_ge(raw_ready, b * 2 * TC + 2 * (t - 1))
                    for out, cols in ((bank[:, 2 * (t % 2), :], slice(0, 2 * D)), (bank[:, 2 * (t % 2) + 1, 0:D], slice(2 * D, 3 * D))):
                        for kc in range(KC):
                            i = pe.matmul(out, xT[:, kc, t * P:t * P + P], w_qkv[:, kc, cols], start=(kc == 0), stop=(kc == KC - 1))
                    i.then_inc(proj_ready, 1)

                def turn(t):
                    pe.wait_ge(lo_ready, b * 4 * TC + 4 * t + 4)
                    for j in range(5):
                        n = 5 * t + j
                        if n >= 4:
                            s, per, k = kept(n - 4)
                            pe.wait_ge(s, b * per + k)
                        if j == 4:
                            pe.wait_ge(qm_ready, b * 2 * TC + 2 * t + 2)
                        for a in range(4):
                            if j == 4:
                                src = qm[:, t % 2, 4 * a:4 * a + 4, :, :].rearrange("p h s d -> p (h s d)")
                            else:
                                h = 8 * (j % 2) + 2 * a
                                src = (q4 if j < 2 else k4)[:, t % 2, h:h + 2, :, :].rearrange("p h s d -> p (h s d)").bitcast(F32)
                            i = pe.transpose(bank[:, 4 + n % 4, a * P:a * P + P], src, ident[:, :])
                        i.then_inc(turn_ready, 1)

                project(0)
                project(1)
                for t in range(TC):
                    turn(t)
                    if t + 2 < TC:
                        project(t + 2)
                pe.wait_ge(mask_ready, 2)
                pe.wait_ge(zeroed, 4)
                pe.wait_ge(kz_zeroed, 2)
                pe.wait_ge(kept_act, b * 3 * TC + 3 * TC)
                pe.wait_ge(kept_dve, b * 4 * TC + 4 * TC)

                def scores(n, pair):
                    i, hq = chunk(n), n // TC
                    keys = (i + 1) * P
                    for h in (2 * pair, 2 * pair + 1):
                        u, hp = 4 * n + h, 2 * hq + h // 2
                        if u >= 2:
                            pe.wait_ge(e_ready, b * 4 * NG + u - 1)
                        pe.matmul(bank[:, u % 2, keys - P:keys], ident_b[:, :], mask[:, P:2 * P], start=True, stop=False,
                                  skip_group_check=True)
                        pe.matmul(bank[:, u % 2, 0:keys], QT[:, hp, i * P:i * P + P], KZ[:, hp, h % 2, 0:keys], start=False, stop=True,
                                  skip_group_check=True).then_inc(s_ready, 1)

                def terrace_scores(n, pair):
                    i, hq = chunk(n), n // TC
                    keys = (i + 1) * P
                    window = min(keys, 2 * P)
                    if n >= 1:
                        pe.wait_ge(et_ready, b * 4 * NG + 4 * (n - 1) + 2 * pair + 2)
                    for h in (2 * pair, 2 * pair + 1):
                        hp = 2 * hq + h // 2
                        out = bank[:, 2 + pair, 256 * (h % 2):256 * (h % 2) + window]
                        pe.matmul(out, QT[:, hp, i * P:i * P + P], KZ[:, hp, h % 2, keys - window:keys], start=True, stop=False)
                        j = pe.matmul(out, ident_b[:, :], mask[:, 2 * P - window:2 * P], start=False, stop=True)
                    j.then_inc(st_ready, 1)

                def turn_terrace(n):
                    w = 1 if chunk(n) == 0 else 2
                    for pair in range(2):
                        pe.wait_ge(et_ready, b * 4 * NG + 4 * n + 2 * pair + 2)
                        if n >= 1:
                            pe.wait_ge(EtT_ready, b * 2 * NG + 2 * (n - 1) + pair + 1)
                        for h in range(2):
                            for a in range(w):
                                i = pe.transpose(bank[:, 4 + pair, (2 * h + a) * P:(2 * h + a) * P + P],
                                                 Et[:, n % 2, 2 * pair + h, a * P:a * P + P], ident[:, :])
                        i.then_inc(ett_ready, 1)

                def weights(n):
                    i = chunk(n)
                    keys = (i + 1) * P
                    pe.wait_ge(R_ready, b * NG + n + 1)
                    if n % TC == 0 and n >= TC:
                        pe.wait_ge(wn_ready, b * HQ + n // TC)
                    for h in range(4):
                        j = pe.matmul(bank[32 * h:32 * h + 32, 7, 0:keys], R[:, n % 2, h, :], E[:, n % 2, h, 0:keys],
                                      start=(n % TC == 0), stop=(n % TC == TC - 1), skip_group_check=True)
                    j.then_inc(wacc_ready, 1)

                def terrace(n):
                    i, hq = chunk(n), n // TC
                    pe.wait_ge(EtT_ready, b * 2 * NG + 2 * n + 2)
                    if n % TC == 0 and n >= TC:
                        pe.wait_ge(yt_ready, b * HQ + hq)
                    w = 1 if i == 0 else 2
                    for a in range(w):
                        for h in range(4):
                            v0 = 2 * D + 64 * hq + 16 * h
                            j = pe.matmul(bank[32 * h:32 * h + 32, 6, i * P:i * P + P], raw[:, i - (w - 1) + a, v0:v0 + 32],
                                          EtT[:, n % 2, h, a, :], start=(a == 0), stop=(a == w - 1), skip_group_check=True)
                    j.then_inc(av_ready, 1)

                def turn_results(hq):
                    pe.wait_ge(oq_ready, b * HQ + hq + 1)
                    for i in range(TC):
                        j = pe.transpose(bank[:, 6, i * P:i * P + P], oq[:, i * P:i * P + P], ident[:, :])
                    j.then_inc(ot_ready, 1)

                scores(0, 0)
                for n in range(NG):
                    terrace_scores(n, 0)
                    scores(n, 1)
                    terrace_scores(n, 1)
                    if n % TC == 1 and n >= TC:
                        turn_results(n // TC - 1)
                    if n >= 1:
                        turn_terrace(n - 1)
                        weights(n - 1)
                    if n + 1 < NG:
                        scores(n + 1, 0)
                    if n >= 1:
                        terrace(n - 1)
                turn_terrace(NG - 1)
                weights(NG - 1)
                terrace(NG - 1)

                pe.wait_ge(EtT_ready, b * 2 * NG + 2 * NG)
                for hq in range(HQ):
                    pe.wait_ge(wm_ready, b * HQ + hq + 1)
                    if hq >= 2:
                        pe.wait_ge(wT_ready, b * HQ + hq - 1)
                    for m in range(TC):
                        i = pe.transpose(bank[:, 4 + hq % 2, m * P:m * P + P], wm[:, hq, m * P:m * P + P], ident[:, :])
                    i.then_inc(wt_ready, 1)
                    if hq == 0:
                        turn_results(HQ - 1)

                def kv(hq):
                    if hq >= 2:
                        pe.wait_ge(kvs_ready, b * HQ + hq - 1)
                    pe.wait_ge(A_dve, b * 2 * HQ + 2 * (hq + 1))
                    pe.wait_ge(A_pool, b * 2 * HQ + 2 * (hq + 1))
                    for m in range(TC):
                        for h in range(4):
                            v0 = 2 * D + 64 * hq + 16 * h
                            i = pe.matmul(bank[32 * h:32 * h + 32, hq % 2, 0:P], raw[:, m, v0:v0 + 32],
                                          A[:, hq % 2, m, h, :, :].rearrange("p r d -> p (r d)"),
                                          start=(m == 0), stop=(m == TC - 1), skip_group_check=True)
                    i.then_inc(kv_ready, 1)

                def linear(hq):
                    pe.wait_ge(BD_ready, b * 16 + 4 * hq + 4)
                    if hq == 0:
                        pe.wait_ge(wn_ready, b * HQ + HQ)
                        pe.wait_ge(yt_ready, b * HQ + HQ)
                    for t in range(TC):
                        i = pe.matmul(bank[:, lin_bank(t), 64 * hq:64 * hq + 64], QMT[:, t, hq, :],
                                      BD[:, t, hq, :, :].rearrange("p h d -> p (h d)"), start=True, stop=True)
                        if hq == HQ - 1:
                            i.then_inc(lin_ready, 1)

                for hq in range(HQ):
                    kv(hq)
                    if hq >= 1:
                        linear(hq - 1)
                linear(HQ - 1)
                for t in range(TC):
                    pe.wait_ge(y_ready, b * TC + t + 1)
                    if t >= 2:
                        pe.wait_ge(yT_ready, b * TC + t - 1)
                    for kc in range(KC):
                        i = pe.transpose(bank[:, 4 + t % 2, kc * P:kc * P + P], y2[:, t, kc * P:kc * P + P], ident[:, :])
                    i.then_inc(yt2_ready, 1)
                pe.wait_ge(wc_loaded, 16)
                pe.wait_ge(yT_ready, b * TC + TC)
                for t in range(TC):
                    for kc in range(KC):
                        i = pe.matmul(bank[:, t, 0:D], yT[:, kc, t * P:t * P + P], w_c[:, kc, :], start=(kc == 0), stop=(kc == KC - 1))
                    i.then_inc(out_ready, 1)



def l1_cross_attention(nc, g, ctx_t, ln_gamma, ln_beta, w_q_d, w_kv_d, w_out_d, b_out, gate):
    H, DH = 16, 64
    NP = H // 2
    NS = SC // P
    NU = H * TC
    INNER = H * DH
    X, ident, bank = g.X, g.ident, g.bank
    with ExitStack() as c:
        def sb(name, shape, dt=F32):
            return c.enter_context(nc.sbuf_tensor("c1_" + name, shape, dt))

        def sem(name):
            return nc.alloc_semaphore("c1_" + name)

        w_q = sb("w_q", [P, KC, INNER])
        w_kv = sb("w_kv", [P, KC, 2 * INNER])
        w_out = sb("w_out", [P, NP, D])
        gam_bet = sb("gam_bet", [P, 2, KC])
        brow, brow_t = sb("brow", [P, D]), sb("brow_t", [P, D])
        gt, tg = sb("gt", [P, 1]), sb("tg", [P, 1])
        ctxT = sb("ctxT", [P, KC, SC])
        xn = sb("xn", [P, TC, D])
        xnT = sb("xnT", [P, KC, L])
        xb = sb("xb", [P, TC, D])
        V = sb("V", [P, NS, INNER])
        KT = sb("KT", [P, 2, 2, SC], F32R)
        QH = sb("QH", [P, 2, 2, L], F32R)
        QL = sb("QL", [P, 2, 2, L], F32R)
        nmax = sb("nmax", [P, 4])
        E = sb("E", [P, 2, SC])
        ET = sb("ET", [P, 2, NS, L])
        sums, rsum = sb("sums", [P, 2, TC]), sb("rsum", [P, 2, TC])
        minus_one = sb("minus_one", [P, TC])
        diag = sb("diag", [P, TC, P])
        rb = sb("rb", [P, 2 * P])
        oT = sb("oT", [P, NP, L])
        pre = Norm(nc, c, "c1_pre")
        ln = Norm(nc, c, "c1_ln")

        w_loaded, wo_loaded, small_loaded, ctx_loaded = sem("w_loaded"), sem("wo_loaded"), sem("small_loaded"), sem("ctx_loaded")
        wv_loaded = sem("wv_loaded")
        ctx_free = sem("ctx_free")
        tg_ready, brow_ready, xb_ready = sem("tg_ready"), sem("brow_ready"), sem("xb_ready")
        xtp_ready, xT_ready = sem("xtp_ready"), sem("xT_ready")
        v_ready, V_ready = sem("v_ready"), sem("V_ready")
        proj_ready = sem("proj_ready")
        k_high, k_low, q_high, q_low = sem("k_high"), sem("k_low"), sem("q_high"), sem("q_low")
        s_ready, nmax_ready, e_ready = sem("s_ready"), sem("nmax_ready"), sem("e_ready")
        et_ready, et0_kept, et1_kept = sem("et_ready"), sem("et0_kept"), sem("et1_kept")
        rsum_ready, diag_ready = sem("rsum_ready"), sem("diag_ready")
        av_ready, rb_ready, oT_ready = sem("av_ready"), sem("rb_ready"), sem("oT_ready")
        out_ready, minus_one_ready = sem("out_ready"), sem("minus_one_ready")

        block = c.enter_context(nc.Block())

        @block.sync
        def _(sp):
            sp.dma_start(ctxT[:, :, :], ctx_t[0].rearrange("(k p) n -> p k n", p=P)).then_inc(ctx_loaded, 16)
            kv_cols = w_kv_d.rearrange("(k p) n -> p k n", p=P)
            sp.dma_start(w_kv[:, :, INNER:2 * INNER], kv_cols[:, :, INNER:2 * INNER]).then_inc(wv_loaded, 16)
            sp.dma_start(w_kv[:, :, 0:INNER], kv_cols[:, :, 0:INNER]).then_inc(w_loaded, 16)
            sp.dma_start(w_q[:, :, :], w_q_d.rearrange("(k p) n -> p k n", p=P)).then_inc(w_loaded, 16)
            sp.dma_start(w_out[:, :, :], w_out_d.rearrange("(n p) d -> p n d", p=P)).then_inc(wo_loaded, 16)
            with sp.Fori(1, B) as b:
                sp.wait_ge(ctx_free, b)
                sp.dma_start(ctxT[:, :, :], ctx_t[ds(b, 1), :, :].rearrange("b (k p) n -> p (b k) n", p=P)).then_inc(ctx_loaded, 16)
            sp.wait_ge(wo_loaded, 16)
            sp.wait_ge(w_loaded, 32)
            sp.wait_ge(ctx_loaded, 16 * B)

        @block.gpsimd
        def _(pool):
            pool.memset(minus_one[:, :], -1.0).then_inc(minus_one_ready, 1)
            pool.wait_ge(minus_one_ready, 1)
            pool.wait_ge(brow_ready, 1)
            with pool.Fori(0, B) as b:
                pre.rstd(g, pool, b)
                for t in range(TC):
                    pool.tensor_tensor(xb[:, t, :], pre.t[:, t, :], brow_t[:, :], ALU.add).then_inc(xb_ready, 1)

                def reciprocals(h):
                    pool.wait_ge(e_ready, b * NU + TC * h + TC)
                    pool.tensor_tensor(rsum[:, h % 2, :], sums[:, h % 2, :], minus_one[:, :], ALU.pow).then_inc(rsum_ready, 1)
                    pool.wait_ge(rsum_ready, b * H + h + 1)
                    if h >= 1:
                        pool.wait_ge(av_ready, b * H + h)
                    g.after_wait(pool)
                    for t in range(TC):
                        pool.tensor_scalar(diag[:, t, :], ident[:, :], rsum[:, h % 2, t:t + 1], 1.0, ALU.mult, ALU.mult).then_inc(diag_ready, 1)

                for h in range(H):
                    reciprocals(h)
                ln.rstd(g, pool, b)

        @block.scalar
        def _(act):
            act.dma_start(gam_bet[:, 0, :], ln_gamma).then_inc(small_loaded, 16)
            act.dma_start(gam_bet[:, 1, :], ln_beta).then_inc(small_loaded, 16)
            act.dma_start(brow[:, :], b_out.partition_broadcast(P)).then_inc(small_loaded, 16)
            act.dma_start(gt[:, :], gate.partition_broadcast(P)).then_inc(small_loaded, 16)
            act.wait_ge(small_loaded, 64)
            act.activation(tg[:, :], gt[:, :], ACT.Tanh).then_inc(tg_ready, 1)
            with act.Fori(0, B) as b:
                for n in range(2 * NS):
                    s, half = divmod(n, 2)
                    act.wait_ge(v_ready, b * 2 * NS + n + 1)
                    act.activation(V[:, s, half * 512:half * 512 + 512], bank[:, n % 4, :], ACT.Copy).then_inc(V_ready, 1)

                def high_k(p, half):
                    act.wait_ge(proj_ready, b * 3 * NP + 3 * p + half + 1)
                    for h in range(2):
                        act.activation(KT[0:64, p % 2, h, half * 512:half * 512 + 512], bank[64 * h:64 * h + 64, 7, :],
                                       ACT.Copy).then_inc(k_high, 1)

                def high_q(p):
                    act.wait_ge(proj_ready, b * 3 * NP + 3 * p + 3)
                    for h in range(2):
                        for r in range(2):
                            act.activation(QH[64 * r:64 * r + 64, p % 2, h, :], bank[64 * h:64 * h + 64, 7, :],
                                           ACT.Copy, scale=DH ** -0.5).then_inc(q_high, 1)

                def exps(u):
                    h = u // TC
                    act.wait_ge(nmax_ready, b * NU + u + 1)
                    if u >= 2:
                        act.wait_ge(et_ready, b * 2 * NU + 2 * (u - 1))
                    if u % TC == 0 and h >= 2:
                        act.wait_ge(rsum_ready, b * H + h - 1)
                    act.activation(E[:, u % 2, :], bank[:, 2 * (u % 2):2 * (u % 2) + 2, :].rearrange("p a n -> p (a n)"), ACT.Exp,
                                   bias=nmax[:, u % 4:u % 4 + 1], accum_out=sums[:, h % 2, u % TC:u % TC + 1]).then_inc(e_ready, 1)

                def keep(u):
                    h, t = divmod(u, TC)
                    if t == 0 and h >= 2:
                        act.wait_ge(av_ready, b * H + h - 1)
                    act.wait_ge(et_ready, b * 2 * NU + 2 * u + 1)
                    act.activation(ET[:, h % 2, 0:4, t * P:t * P + P], bank[:, 4, :].rearrange("p (k n) -> p k n", k=4),
                                   ACT.Copy).then_inc(et0_kept, 1)

                high_k(0, 0)
                high_k(0, 1)
                for kc in range(KC):
                    act.wait_ge(xtp_ready, b * KC + kc + 1)
                    act.activation(xnT[:, kc, :], bank[:, 4 + kc, :], ACT.Identity, bias=gam_bet[:, 1, kc:kc + 1],
                                   scale=gam_bet[:, 0, kc:kc + 1]).then_inc(xT_ready, 1)
                high_q(0)
                exps(0)
                exps(1)
                for u in range(NU):
                    keep(u)
                    if u + 2 < NU:
                        exps(u + 2)
                    p, r = divmod(u, 2 * TC)
                    if p + 1 < NP:
                        if r in (0, 3):
                            high_k(p + 1, r // 3)
                        if r == 4:
                            high_q(p + 1)

        @block.vector
        def _(dve):
            dve.wait_ge(small_loaded, 64)
            dve.wait_ge(tg_ready, 1)
            dve.tensor_scalar(brow_t[:, :], brow[:, :], tg[:, 0:1], None, ALU.mult).then_inc(brow_ready, 1)
            dve.sem_inc(ln.banks_free, TC)
            with dve.Fori(0, B) as b:
                for t in range(TC):
                    dve.tensor_copy(pre.t[:, t, :], X[:, b * TC + t, :]).then_inc(pre.sum_ready, 1)
                pre.stats(g, dve, b)
                pre.apply(dve, lambda t: xn[:, t, :], b)

                def low_k(p, half):
                    for h in range(2):
                        dve.wait_ge(k_high, b * 4 * NP + 4 * p + 2 * half + h + 1)
                        cols = slice(half * 512, half * 512 + 512)
                        dve.tensor_tensor(KT[64:P, p % 2, h, cols], bank[64 * h:64 * h + 64, 7, :],
                                          KT[0:64, p % 2, h, cols].bitcast(F32), ALU.subtract).then_inc(k_low, 1)

                def low_q(p, h):
                    dve.wait_ge(q_high, b * 4 * NP + 4 * p + 2 * h + 2)
                    for r in range(2):
                        dve.scalar_tensor_tensor(out=QL[64 * r:64 * r + 64, p % 2, h, :], in0=bank[64 * h:64 * h + 64, 7, :],
                                                 scalar=DH ** -0.5, in1=QH[64 * r:64 * r + 64, p % 2, h, :].bitcast(F32),
                                                 op0=ALU.mult, op1=ALU.subtract).then_inc(q_low, 1)

                def maxima(u):
                    dve.wait_ge(s_ready, b * NU + u + 1)
                    if u >= 4:
                        dve.wait_ge(e_ready, b * NU + u - 3)
                    dve.tensor_reduce(nmax[:, u % 4:u % 4 + 1], bank[:, 2 * (u % 2):2 * (u % 2) + 2, :], AX.XY, ALU.max,
                                      negate=True).then_inc(nmax_ready, 1)

                def keep(u):
                    h, t = divmod(u, TC)
                    if t == 0 and h >= 2:
                        dve.wait_ge(av_ready, b * H + h - 1)
                    dve.wait_ge(et_ready, b * 2 * NU + 2 * u + 2)
                    dve.tensor_copy(ET[:, h % 2, 4:8, t * P:t * P + P], bank[:, 5, :].rearrange("p (k n) -> p k n", k=4)).then_inc(et1_kept, 1)

                def normalise(h):
                    dve.wait_ge(av_ready, b * H + h + 1)
                    if h >= 1:
                        dve.wait_ge(oT_ready, b * 2 * H + 2 * h)
                    dve.tensor_copy(rb[:, :], bank[:, 6, 2 * P:4 * P]).then_inc(rb_ready, 1)
                    dve.wait_ge(rb_ready, b * H + h + 1)
                    for j in range(2):
                        dve.tensor_tensor(oT[64 * (h % 2):64 * (h % 2) + 64, h // 2, 256 * j:256 * j + 256], bank[64 * j:64 * j + 64, 6, 0:2 * P],
                                          rb[64 * j:64 * j + 64, :], ALU.mult).then_inc(oT_ready, 1)

                low_k(0, 0)
                low_k(0, 1)
                low_q(0, 0)
                low_q(0, 1)
                maxima(0)
                maxima(1)
                for u in range(NU):
                    if u + 2 < NU:
                        maxima(u + 2)
                    keep(u)
                    if u % TC == 0 and u >= 2 * TC:
                        normalise(u // TC - 2)
                    p, r = divmod(u, 2 * TC)
                    if p + 1 < NP:
                        if r in (0, 3):
                            low_k(p + 1, r // 3)
                        if r in (4, 5):
                            low_q(p + 1, r - 4)
                normalise(H - 2)
                normalise(H - 1)
                dve.wait_ge(xb_ready, b * TC + TC)
                for t in range(TC):
                    dve.wait_ge(out_ready, b * TC + t + 1)
                    dve.scalar_tensor_tensor(out=ln.t[:, t, :], in0=bank[:, t, 0:D], scalar=tg[:, 0:1], in1=xb[:, t, :],
                                             op0=ALU.mult, op1=ALU.add).then_inc(ln.sum_ready, 1)
                dve.wait_ge(ln.sum_ready, b * TC + TC)
                dve.sem_inc(ln.banks_free, TC)
                ln.stats(g, dve, b)
                ln.apply(dve, lambda t: X[:, b * TC + t, :], b)

        @block.tensor
        def _(pe):
            with pe.Fori(0, B) as b:
                pe.wait_ge(ln.banks_free, b * TC + TC)
                pe.wait_ge(wv_loaded, 16)
                pe.wait_ge(ctx_loaded, b * 16 + 16)
                for n in range(2 * NS):
                    s, half = divmod(n, 2)
                    if n >= 4:
                        pe.wait_ge(V_ready, b * 2 * NS + n - 3)
                    for kc in range(KC):
                        i = pe.matmul(bank[:, n % 4, :], ctxT[:, kc, s * P:s * P + P],
                                      w_kv[:, kc, INNER + half * 512:INNER + half * 512 + 512], start=(kc == 0), stop=(kc == KC - 1))
                    i.then_inc(v_ready, 1)
                pe.wait_ge(V_ready, b * 2 * NS + 2 * NS)

                def bank_7_free(n):
                    if n >= 1:
                        p, j = divmod(n - 1, 3)
                        if j < 2:
                            pe.wait_ge(k_low, b * 4 * NP + 4 * p + 2 * j + 2)
                        else:
                            pe.wait_ge(q_low, b * 4 * NP + 4 * p + 4)

                def project(p, j):
                    bank_7_free(3 * p + j)
                    for kc in range(KC):
                        if j < 2:
                            i = pe.matmul(bank[:, 7, :], w_kv[:, kc, p * P:p * P + P], ctxT[:, kc, j * 512:j * 512 + 512],
                                          start=(kc == 0), stop=(kc == KC - 1))
                        else:
                            i = pe.matmul(bank[:, 7, :], w_q[:, kc, p * P:p * P + P], xnT[:, kc, :], start=(kc == 0), stop=(kc == KC - 1))
                    i.then_inc(proj_ready, 1)

                def scores(u):
                    h, t = divmod(u, TC)
                    p = h // 2
                    if u % (2 * TC) == 0:
                        pe.wait_ge(k_low, b * 4 * NP + 4 * p + 4)
                        pe.wait_ge(q_low, b * 4 * NP + 4 * p + 4)
                    if u >= 2:
                        pe.wait_ge(e_ready, b * NU + u - 1)
                    for n, q in enumerate((QL, QH)):
                        for half in range(2):
                            i = pe.matmul(bank[:, 2 * (u % 2) + half, :], q[:, p % 2, h % 2, t * P:t * P + P],
                                          KT[:, p % 2, h % 2, half * 512:half * 512 + 512], start=(n == 0), stop=(n == 1))
                    i.then_inc(s_ready, 1)

                def turn(u):
                    pe.wait_ge(e_ready, b * NU + u + 1)
                    for half in range(2):
                        if u >= 1:
                            pe.wait_ge(et1_kept if half else et0_kept, b * NU + u)
                        for k in range(4):
                            col = (4 * half + k) * P
                            i = pe.transpose(bank[:, 4 + half, k * P:k * P + P], E[:, u % 2, col:col + P], ident[:, :])
                        i.then_inc(et_ready, 1)

                def values(h, chunks):
                    if chunks.start == 0:
                        pe.wait_ge(et0_kept, b * NU + TC * h + TC)
                        pe.wait_ge(et1_kept, b * NU + TC * h + TC)
                        if h >= 1:
                            pe.wait_ge(oT_ready, b * 2 * H + 2 * h)
                    for k in chunks:
                        for j in range(2):
                            pe.matmul(bank[64 * j:64 * j + 64, 6, 0:2 * P], V[:, k, DH * h:DH * h + DH],
                                      ET[:, h % 2, k, 256 * j:256 * j + 256], start=(k == 0), stop=(k == NS - 1))
                    if chunks.stop < NS:
                        return
                    pe.wait_ge(diag_ready, b * TC * H + TC * h + TC)
                    for t in range(2):
                        for j in range(2):
                            i = pe.matmul(bank[64 * j:64 * j + 64, 6, 2 * P + t * P:3 * P + t * P], g.ones[:, :],
                                          diag[:, 2 * j + t, :], start=True, stop=True)
                    i.then_inc(av_ready, 1)

                pe.wait_ge(w_loaded, 32)
                project(0, 0)
                project(0, 1)
                pe.wait_ge(pre.x_ready, b * TC + TC)
                for kc in range(KC):
                    for t in range(TC):
                        i = pe.transpose(bank[:, 4 + kc, t * P:t * P + P], xn[:, t, kc * P:kc * P + P], ident[:, :])
                    i.then_inc(xtp_ready, 1)
                pe.wait_ge(xT_ready, b * KC + KC)
                project(0, 2)
                scores(0)
                scores(1)
                for u in range(NU):
                    if u + 2 < NU:
                        scores(u + 2)
                    turn(u)
                    p, r = divmod(u, 2 * TC)
                    if p + 1 < NP and r in (0, 3, 4):
                        project(p + 1, (0, 3, 4).index(r))
                    if u % TC >= 1 and u >= TC:
                        values(u // TC - 1, (range(0, 3), range(3, 6), range(6, 8))[u % TC - 1])
                pe.wait_ge(q_low, b * 4 * NP + 4 * NP)
                pe.sem_inc(ctx_free, 1)
                values(H - 1, range(NS))
                pe.wait_ge(wo_loaded, 16)
                pe.wait_ge(oT_ready, b * 2 * H + 2 * H)
                for t in range(TC):
                    for p in range(NP):
                        i = pe.matmul(bank[:, t, 0:D], oT[:, p, t * P:t * P + P], w_out[:, p, :], start=(p == 0), stop=(p == NP - 1))
                    i.then_inc(out_ready, 1)





def decoder(nc, x, ctx_rows, ctx_t,
            a0_norm_w, a0_wq, a0_wkv, a0_wo, a0_q_gamma_t, a0_k_gamma_t,
            c0_x1_t, c0_w1_t, c0_b1, c0_w2_t, c0_b2, c0_w3_t, c0_b3,
            m0_router, m0_w1, m0_b1, m0_w2, m0_b2, m0_gamma, m0_beta,
            t1_w_qkv_t, t1_w_c_t, t1_mix, t1_index_decays_t, t1_mega_decays,
            c1_gamma, c1_beta, c1_wq, c1_wkv, c1_wo, c1_bo, c1_gate,
            m1_rw1, m1_rb1, m1_rw2, m1_rb2, m1_w1, m1_b1, m1_w2, m1_b2,
            out):
    g = Shared()
    with ExitStack() as ctx:
        setup(nc, g, ctx, x)
        with nc.cleanup_on_exit():
            l0_attention(nc, g, x, a0_norm_w, a0_wq, a0_wkv, a0_wo, a0_q_gamma_t, a0_k_gamma_t)
        with nc.cleanup_on_exit():
            l0_cross_attention(nc, g, ctx_rows, c0_x1_t, c0_w1_t, c0_b1, c0_w2_t, c0_b2, c0_w3_t, c0_b3)
        with nc.cleanup_on_exit():
            l0_ffn(nc, g, m0_router, m0_w1, m0_b1, m0_w2, m0_b2, m0_gamma, m0_beta)
        with nc.cleanup_on_exit():
            l1_attention(nc, g, t1_w_qkv_t, t1_w_c_t, t1_mix, t1_index_decays_t, t1_mega_decays)
        with nc.cleanup_on_exit():
            l1_cross_attention(nc, g, ctx_t, c1_gamma, c1_beta, c1_wq, c1_wkv, c1_wo, c1_bo, c1_gate)
        with nc.cleanup_on_exit():
            l1_ffn(nc, g, m1_rw1, m1_rb1, m1_rw2, m1_rb2, m1_w1, m1_b1, m1_w2, m1_b2, out)



def kernel(**inputs):
    import numpy as np
    import concourse.bacc as bacc
    from concourse.bass_utils import run_bass_kernel_spmd

    w = {name: np.asarray(a) for name, a in inputs.items()}

    def per_partition(a):
        a = a.reshape(a.shape[:-1] + (a.shape[-1] // P, P))
        return np.moveaxis(a, -1, 0)

    laid_out = [
        w["x"], w["ctx_1024"], w["ctx_1024"].transpose(0, 2, 1),
        per_partition(w["L0_attn_norm_w"]), w["L0_attn_Wq"], w["L0_attn_Wkv"], w["L0_attn_Wo"],
        w["L0_attn_q_gamma"].T, w["L0_attn_k_gamma"].T,
        w["L0_xattn_x1"].T, w["L0_xattn_W1"].T, per_partition(w["L0_xattn_b1"]), w["L0_xattn_W2"].T,
        per_partition(w["L0_xattn_b2"]), w["L0_xattn_W3"].T, w["L0_xattn_b3"],
        w["L0_ffn_router_w"], w["L0_ffn_w1"], per_partition(w["L0_ffn_b1"]), w["L0_ffn_w2"],
        w["L0_ffn_b2"], w["L0_ffn_gamma"], w["L0_ffn_beta"],
        np.concatenate([w["L1_attn_Wq"], w["L1_attn_Wk"], w["L1_attn_Wv"]]).T, w["L1_attn_Wc"].T,
        w["L1_attn_terrace_mix"].reshape(64, 1), w["L1_attn_index_decays"].T, w["L1_attn_mega_decays"],
        per_partition(w["L1_xattn_ln_gamma"]), per_partition(w["L1_xattn_ln_beta"]), w["L1_xattn_w_q"],
        w["L1_xattn_w_kv"], w["L1_xattn_w_out"], w["L1_xattn_b_out"], w["L1_xattn_gate"],
        w["L1_ffn_rW1"], per_partition(w["L1_ffn_rb1"]), w["L1_ffn_rW2"], w["L1_ffn_rb2"],
        w["L1_ffn_We1"], per_partition(w["L1_ffn_be1"]), w["L1_ffn_We2"], w["L1_ffn_be2"],
    ]
    nc = bacc.Bacc("TRN2", target_bir_lowering=False, num_devices=1)
    arrays, args = {}, []
    for n, a in enumerate(laid_out):
        a = np.ascontiguousarray(a)
        arrays[f"in_{n}_dram"] = a
        args.append(nc.dram_tensor(f"in_{n}_dram", a.shape, mybir.dt.from_np(a.dtype), kind="ExternalInput").ap())
    args.append(nc.dram_tensor("out_dram", (B, L, D), F32, kind="ExternalOutput").ap())
    decoder(nc, *args)
    r = run_bass_kernel_spmd(nc, [arrays], core_ids=[0])
    return r.results[0]["out_dram"]
```
